# Optimizing a Trainium2 kernel written in Bass

```python
import numpy as np
import jax
import jax.numpy as jnp

def _softmax(x, axis=-1):
    return jax.nn.softmax(x, axis=axis)

def _gelu(x):
    return jax.nn.gelu(x, approximate=True)

def _silu(x):
    return jax.nn.silu(x)

def _sigmoid(x):
    return jax.nn.sigmoid(x)

def _layernorm(x, axis=-1, eps=1e-05):
    m = jnp.mean(x, axis=axis, keepdims=True)
    v = jnp.var(x, axis=axis, keepdims=True)
    return (x - m) / jnp.sqrt(v + eps)

def _scatter_add(tgt, idx, src, axis=0):
    return tgt.at[idx].add(src)

def _segment_sum(src, seg, n):
    return jax.ops.segment_sum(src, seg, n)
kernel_name = 'mk_decoder_preln_d2_seqx_r4_bdb4b0'

def setup_inputs(seed: int=0):
    np.random.seed(seed)
    _w = jnp.asarray

    def _rec_inputs():
        import jax
        import jax.numpy as jnp
        _rk = jax.random.key(seed)
        x = -0.0002928 + 1 * jax.random.normal(jax.random.fold_in(_rk, 1), (32, 128, 256), jnp.float32)
        _lenS = 128 - jax.random.randint(jax.random.fold_in(_rk, 7), (32,), 0, max(1, 128 // 4) + 1, jnp.int32)
        _lenS2 = 128 - jax.random.randint(jax.random.fold_in(_rk, 8), (32,), 0, max(1, 128 // 4) + 1, jnp.int32)
        _ctx_1024P = jax.random.normal(jax.random.fold_in(_rk, 11), (32, 16, 256), jnp.float32)
        _ctx_1024c = jax.random.dirichlet(jax.random.fold_in(_rk, 511), 0.3 * jnp.ones((16,), jnp.float32), (32, 128))
        _ctx_1024t = jnp.einsum('bsk,bkd->bsd', _ctx_1024c, _ctx_1024P)
        _ctx_1024t = _ctx_1024t * jax.lax.rsqrt(jnp.mean(jnp.square(_ctx_1024t)) + 1e-12) * 0.953939
        ctx_1024 = -1.39393e-06 + 0.999914 * (_ctx_1024t + 0.3 * jax.random.normal(jax.random.fold_in(_rk, 611), (32, 128, 256), jnp.float32))
        return (x, ctx_1024)
    x, ctx_1024 = _rec_inputs()

    def _L0_attn_setup():
        import jax, jax.numpy as jnp
        import numpy as np
        import math
        D_MODEL = 256
        key = jax.random.key(seed)
        ks = jax.random.split(key, 7)
        B, S, D = (4, 1024, D_MODEL)
        s = 0.02
        return {'hidden_states': jax.random.normal(ks[0], (B, S, D), jnp.float32), 'Wq': jax.random.normal(ks[1], (D, D), jnp.float32) * s, 'bq': jnp.zeros((D,), jnp.float32), 'Wk': jax.random.normal(ks[2], (D, D), jnp.float32) * s, 'bk': jnp.zeros((D,), jnp.float32), 'Wv': jax.random.normal(ks[3], (D, D), jnp.float32) * s, 'bv': jnp.zeros((D,), jnp.float32)}
    _L0_attn_all = _L0_attn_setup()
    _L0_attn_in = {k: v for k, v in _L0_attn_all.items() if k in ('Wq', 'bq', 'Wk', 'bk', 'Wv', 'bv')}
    del _L0_attn_all

    def _L0_xattn_setup():
        import jax, jax.numpy as jnp
        import numpy as np
        SCALE_BASE = 512.0
        GN_EPS = 1e-05

        def _xpos(x, downscale):
            L, D = (x.shape[-2], x.shape[-1])
            half = D // 2
            base = (jnp.arange(0, D, 2, dtype=jnp.float32) + 0.4 * D) / (1.4 * D)
            min_pos = -(L // 2)
            power = (jnp.arange(min_pos, min_pos + L, dtype=jnp.float32) / SCALE_BASE)[:, None]
            scale = base[None, :] ** power
            inv_freq = 1.0 / 10000.0 ** (jnp.arange(half, dtype=jnp.float32) / half)
            ang = jnp.arange(L, dtype=jnp.float32)[:, None] * inv_freq[None, :]
            sin, cos = (jnp.sin(ang), jnp.cos(ang))
            if downscale:
                scale = 1.0 / scale
            sin_s = jnp.repeat(sin * scale, 2, axis=-1)
            cos_s = jnp.repeat(cos * scale, 2, axis=-1)
            x1, x2 = (x[..., ::2], x[..., 1::2])
            rot = jnp.stack((-x2, x1), axis=-1).reshape(x.shape)
            return x * cos_s + rot * sin_s

        def _decay_mask(L, H):
            gammas = 1.0 - jnp.exp(jnp.linspace(np.log(1.0 / 32.0), np.log(1.0 / 512.0), H)).astype(jnp.float32)
            idx = jnp.arange(L)
            dist = idx[:, None] - idx[None, :]
            causal = dist >= 0
            d = jnp.maximum(dist, 0).astype(jnp.float32)
            return jnp.where(causal[None], gammas[:, None, None] ** d[None], 0.0)
        key = jax.random.key(seed)
        ks = jax.random.split(key, 9)
        B, L, D, H = (2, 512, 256, 16)
        hd = D // H
        return {'query': jax.random.normal(ks[0], (B, L, D), jnp.float32), 'key': jax.random.normal(ks[1], (B, L, D), jnp.float32), 'value': jax.random.normal(ks[2], (B, L, D), jnp.float32), 'W_Q': jax.random.normal(ks[3], (H, D, hd), jnp.float32) / D, 'W_K': jax.random.normal(ks[4], (H, D, hd), jnp.float32) / D, 'W_V': jax.random.normal(ks[5], (H, D, hd), jnp.float32) / D, 'g_w': jax.random.normal(ks[6], (D, D), jnp.float32) * (2.0 / (D + D)) ** 0.5, 'g_b': jnp.zeros((D,), jnp.float32), 'out_w': jax.random.normal(ks[7], (D, D), jnp.float32) * (2.0 / (D + D)) ** 0.5, 'out_b': jnp.zeros((D,), jnp.float32)}
    _L0_xattn_all = _L0_xattn_setup()
    _L0_xattn_in = {k: v for k, v in _L0_xattn_all.items() if k in ('W_Q', 'W_K', 'W_V', 'g_w', 'g_b', 'out_w', 'out_b')}
    del _L0_xattn_all

    def _L0_ffn_setup():
        import jax, jax.numpy as jnp
        import numpy as np
        E = 8
        TOP_K = 2
        D = 256
        H = 2 * D
        key = jax.random.key(seed)
        k0, k1, k2, k3, k4 = jax.random.split(key, 5)
        scale = 0.02
        x = jax.random.normal(k0, (4, 512, D), dtype=jnp.float32)
        Wg = jax.random.normal(k1, (D, E), dtype=jnp.float32) * scale
        W1 = jax.random.normal(k2, (E, D, H), dtype=jnp.float32) * scale
        W2 = jax.random.normal(k3, (E, D, H), dtype=jnp.float32) * scale
        W3 = jax.random.normal(k4, (E, H, D), dtype=jnp.float32) * scale
        return {'x': x, 'Wg': Wg, 'W1': W1, 'W2': W2, 'W3': W3}
    _L0_ffn_all = _L0_ffn_setup()
    _L0_ffn_in = {k: v for k, v in _L0_ffn_all.items() if k in ('Wg', 'W1', 'W2', 'W3')}
    del _L0_ffn_all

    def _L1_attn_setup():
        import jax, jax.numpy as jnp
        import numpy as np
        D_MODEL = 256
        OMEGA_DIM = 64
        VQ_CODES = 64
        VQ_DIM = 64
        N_PARAMS = OMEGA_DIM * (OMEGA_DIM - 1) // 2
        TRIU_R, TRIU_C = np.triu_indices(OMEGA_DIM, k=1)
        RMS_EPS = 1e-06
        NORM_EPS = 1e-12

        def _normalize(v):
            n = jnp.linalg.norm(v, axis=-1, keepdims=True)
            return v / jnp.maximum(n, NORM_EPS)

        def _rmsnorm(x, w):
            ms = jnp.mean(x * x, axis=-1, keepdims=True)
            return x * jax.lax.rsqrt(ms + RMS_EPS) * w
        key = jax.random.key(seed)
        ks = jax.random.split(key, 12)
        B, L = (16, 1024)
        s = 0.02
        return {'x': jax.random.normal(ks[0], (B, L, D_MODEL), jnp.float32), 'omega_proj_w': jax.random.normal(ks[1], (N_PARAMS, D_MODEL), jnp.float32) * s, 'omega_proj_b': jnp.zeros((N_PARAMS,), jnp.float32), 'omega_out_w': jax.random.normal(ks[2], (D_MODEL, OMEGA_DIM), jnp.float32) * s, 'omega_out_b': jnp.zeros((D_MODEL,), jnp.float32), 'vq_proj_in_w': jax.random.normal(ks[3], (VQ_DIM, D_MODEL), jnp.float32) * s, 'vq_proj_in_b': jnp.zeros((VQ_DIM,), jnp.float32), 'vq_proj_out_w': jax.random.normal(ks[4], (D_MODEL, VQ_DIM), jnp.float32) * s, 'vq_proj_out_b': jnp.zeros((D_MODEL,), jnp.float32), 'codebook': jax.random.normal(ks[5], (VQ_CODES, VQ_DIM), jnp.float32), 'omega_mix': jnp.float32(0.1), 'vq_mix': jnp.float32(0.05), 'norm_w': jnp.ones((D_MODEL,), jnp.float32)}
    _L1_attn_all = _L1_attn_setup()
    _L1_attn_in = {k: v for k, v in _L1_attn_all.items() if k in ('omega_proj_w', 'omega_proj_b', 'omega_out_w', 'omega_out_b', 'vq_proj_in_w', 'vq_proj_in_b', 'vq_proj_out_w', 'vq_proj_out_b', 'codebook', 'omega_mix', 'vq_mix', 'norm_w')}
    del _L1_attn_all

    def _L1_xattn_setup():
        import jax, jax.numpy as jnp
        import numpy as np
        import math
        NUM_HEADS = 16
        key = jax.random.key(seed)
        ks = jax.random.split(key, 9)
        B, S, D = (2, 512, 256)
        hd = D // NUM_HEADS
        s_in = 1.0 / math.sqrt(D)
        return {'q': jax.random.normal(ks[0], (B, S, D), jnp.float32), 'k': jax.random.normal(ks[1], (B, S, D), jnp.float32), 'v': jax.random.normal(ks[2], (B, S, D), jnp.float32), 'Wq': jax.random.normal(ks[3], (D, D), jnp.float32) * s_in, 'bq': jnp.zeros((D,), jnp.float32), 'Wk': jax.random.normal(ks[4], (D, hd), jnp.float32) * s_in, 'bk': jnp.zeros((hd,), jnp.float32), 'Wv': jax.random.normal(ks[5], (D, hd), jnp.float32) * s_in, 'bv': jnp.zeros((hd,), jnp.float32)}
    _L1_xattn_all = _L1_xattn_setup()
    _L1_xattn_in = {k: v for k, v in _L1_xattn_all.items() if k in ('Wq', 'bq', 'Wk', 'bk', 'Wv', 'bv')}
    del _L1_xattn_all

    def _L1_ffn_setup():
        import jax, jax.numpy as jnp
        import numpy as np
        E = 8
        K = 2
        key = jax.random.key(seed)
        ks = jax.random.split(key, 8)
        B, T, d = (4, 512, 256)
        h = 4 * d // E
        s = 0.02
        X = jax.random.normal(ks[0], (B, T, d), jnp.float32)
        routing_W = jax.random.normal(ks[1], (E, d), jnp.float32) * s
        expert_bias = jnp.zeros((E,), jnp.float32)
        sW1 = jax.random.normal(ks[2], (d, h), jnp.float32) * s
        sb1 = jnp.zeros((h,), jnp.float32)
        sW2 = jax.random.normal(ks[3], (h, d), jnp.float32) * s
        sb2 = jnp.zeros((d,), jnp.float32)
        rW1 = jax.random.normal(ks[4], (E, d, h), jnp.float32) * s
        rb1 = jnp.zeros((E, h), jnp.float32)
        rW2 = jax.random.normal(ks[5], (E, h, d), jnp.float32) * s
        rb2 = jnp.zeros((E, d), jnp.float32)
        return dict(X=X, routing_W=routing_W, expert_bias=expert_bias, sW1=sW1, sb1=sb1, sW2=sW2, sb2=sb2, rW1=rW1, rb1=rb1, rW2=rW2, rb2=rb2)
    _L1_ffn_all = _L1_ffn_setup()
    _L1_ffn_in = {k: v for k, v in _L1_ffn_all.items() if k in ('routing_W', 'expert_bias', 'sW1', 'sb1', 'sW2', 'sb2', 'rW1', 'rb1', 'rW2', 'rb2')}
    del _L1_ffn_all
    return {'x': x, 'ctx_1024': ctx_1024, 'L0_attn_Wq': _L0_attn_in['Wq'], 'L0_attn_bq': _L0_attn_in['bq'], 'L0_attn_Wk': _L0_attn_in['Wk'], 'L0_attn_bk': _L0_attn_in['bk'], 'L0_attn_Wv': _L0_attn_in['Wv'], 'L0_attn_bv': _L0_attn_in['bv'], 'L0_xattn_W_Q': _L0_xattn_in['W_Q'], 'L0_xattn_W_K': _L0_xattn_in['W_K'], 'L0_xattn_W_V': _L0_xattn_in['W_V'], 'L0_xattn_g_w': _L0_xattn_in['g_w'], 'L0_xattn_g_b': _L0_xattn_in['g_b'], 'L0_xattn_out_w': _L0_xattn_in['out_w'], 'L0_xattn_out_b': _L0_xattn_in['out_b'], 'L0_ffn_Wg': _L0_ffn_in['Wg'], 'L0_ffn_W1': _L0_ffn_in['W1'], 'L0_ffn_W2': _L0_ffn_in['W2'], 'L0_ffn_W3': _L0_ffn_in['W3'], 'L1_attn_omega_proj_w': _L1_attn_in['omega_proj_w'], 'L1_attn_omega_proj_b': _L1_attn_in['omega_proj_b'], 'L1_attn_omega_out_w': _L1_attn_in['omega_out_w'], 'L1_attn_omega_out_b': _L1_attn_in['omega_out_b'], 'L1_attn_vq_proj_in_w': _L1_attn_in['vq_proj_in_w'], 'L1_attn_vq_proj_in_b': _L1_attn_in['vq_proj_in_b'], 'L1_attn_vq_proj_out_w': _L1_attn_in['vq_proj_out_w'], 'L1_attn_vq_proj_out_b': _L1_attn_in['vq_proj_out_b'], 'L1_attn_codebook': _L1_attn_in['codebook'], 'L1_attn_omega_mix': _L1_attn_in['omega_mix'], 'L1_attn_vq_mix': _L1_attn_in['vq_mix'], 'L1_attn_norm_w': _L1_attn_in['norm_w'], 'L1_xattn_Wq': _L1_xattn_in['Wq'], 'L1_xattn_bq': _L1_xattn_in['bq'], 'L1_xattn_Wk': _L1_xattn_in['Wk'], 'L1_xattn_bk': _L1_xattn_in['bk'], 'L1_xattn_Wv': _L1_xattn_in['Wv'], 'L1_xattn_bv': _L1_xattn_in['bv'], 'L1_ffn_routing_W': _L1_ffn_in['routing_W'], 'L1_ffn_expert_bias': _L1_ffn_in['expert_bias'], 'L1_ffn_sW1': _L1_ffn_in['sW1'], 'L1_ffn_sb1': _L1_ffn_in['sb1'], 'L1_ffn_sW2': _L1_ffn_in['sW2'], 'L1_ffn_sb2': _L1_ffn_in['sb2'], 'L1_ffn_rW1': _L1_ffn_in['rW1'], 'L1_ffn_rb1': _L1_ffn_in['rb1'], 'L1_ffn_rW2': _L1_ffn_in['rW2'], 'L1_ffn_rb2': _L1_ffn_in['rb2']}

def reference(x, ctx_1024, L0_attn_Wq, L0_attn_bq, L0_attn_Wk, L0_attn_bk, L0_attn_Wv, L0_attn_bv, L0_xattn_W_Q, L0_xattn_W_K, L0_xattn_W_V, L0_xattn_g_w, L0_xattn_g_b, L0_xattn_out_w, L0_xattn_out_b, L0_ffn_Wg, L0_ffn_W1, L0_ffn_W2, L0_ffn_W3, L1_attn_omega_proj_w, L1_attn_omega_proj_b, L1_attn_omega_out_w, L1_attn_omega_out_b, L1_attn_vq_proj_in_w, L1_attn_vq_proj_in_b, L1_attn_vq_proj_out_w, L1_attn_vq_proj_out_b, L1_attn_codebook, L1_attn_omega_mix, L1_attn_vq_mix, L1_attn_norm_w, L1_xattn_Wq, L1_xattn_bq, L1_xattn_Wk, L1_xattn_bk, L1_xattn_Wv, L1_xattn_bv, L1_ffn_routing_W, L1_ffn_expert_bias, L1_ffn_sW1, L1_ffn_sb1, L1_ffn_sW2, L1_ffn_sb2, L1_ffn_rW1, L1_ffn_rb1, L1_ffn_rW2, L1_ffn_rb2):
    import jax
    import jax.numpy as jnp

    def _L0_attn_ref(hidden_states, Wq, bq, Wk, bk, Wv, bv):
        import jax, jax.numpy as jnp
        import numpy as np
        import math
        D_MODEL = 256
        D = hidden_states.shape[-1]
        scale = 1.0 / math.sqrt(D)
        q = hidden_states @ Wq.T + bq
        k = hidden_states @ Wk.T + bk
        v = hidden_states @ Wv.T + bv
        q = jax.nn.softmax(q, axis=-1)
        k = jax.nn.softmax(k, axis=-2) * scale
        v = jax.nn.softmax(v, axis=-2)
        attn = jnp.einsum('bqd,bkd->bqk', q, k)
        out = jnp.einsum('bqk,bkd->bqd', attn, v)
        return out

    def _L0_xattn_ref(query, key, value, W_Q, W_K, W_V, g_w, g_b, out_w, out_b):
        import jax, jax.numpy as jnp
        import numpy as np
        SCALE_BASE = 512.0
        GN_EPS = 1e-05

        def _xpos(x, downscale):
            L, D = (x.shape[-2], x.shape[-1])
            half = D // 2
            base = (jnp.arange(0, D, 2, dtype=jnp.float32) + 0.4 * D) / (1.4 * D)
            min_pos = -(L // 2)
            power = (jnp.arange(min_pos, min_pos + L, dtype=jnp.float32) / SCALE_BASE)[:, None]
            scale = base[None, :] ** power
            inv_freq = 1.0 / 10000.0 ** (jnp.arange(half, dtype=jnp.float32) / half)
            ang = jnp.arange(L, dtype=jnp.float32)[:, None] * inv_freq[None, :]
            sin, cos = (jnp.sin(ang), jnp.cos(ang))
            if downscale:
                scale = 1.0 / scale
            sin_s = jnp.repeat(sin * scale, 2, axis=-1)
            cos_s = jnp.repeat(cos * scale, 2, axis=-1)
            x1, x2 = (x[..., ::2], x[..., 1::2])
            rot = jnp.stack((-x2, x1), axis=-1).reshape(x.shape)
            return x * cos_s + rot * sin_s

        def _decay_mask(L, H):
            gammas = 1.0 - jnp.exp(jnp.linspace(np.log(1.0 / 32.0), np.log(1.0 / 512.0), H)).astype(jnp.float32)
            idx = jnp.arange(L)
            dist = idx[:, None] - idx[None, :]
            causal = dist >= 0
            d = jnp.maximum(dist, 0).astype(jnp.float32)
            return jnp.where(causal[None], gammas[:, None, None] ** d[None], 0.0)
        B, L, D = query.shape
        H = W_Q.shape[0]
        q = jnp.einsum('bld,hde->bhle', query, W_Q)
        k = jnp.einsum('bld,hde->bhle', key, W_K)
        v = jnp.einsum('bld,hde->bhle', value, W_V)
        q = _xpos(q, downscale=False)
        k = _xpos(k, downscale=True)
        sim = jnp.einsum('bhnd,bhsd->bhns', q, k) * _decay_mask(L, H)[None]
        ret = jnp.einsum('bhns,bhsd->bhnd', sim, v)
        mu = ret.mean(axis=-1, keepdims=True)
        var = ret.var(axis=-1, keepdims=True)
        ret = (ret - mu) / jnp.sqrt(var + GN_EPS)
        ret = ret.transpose(0, 2, 1, 3).reshape(B, L, D)
        gate = jax.nn.silu(query @ g_w.T + g_b)
        return ret * gate @ out_w.T + out_b

    def _L0_ffn_ref(x, Wg, W1, W2, W3):
        import jax, jax.numpy as jnp
        import numpy as np
        E = 8
        TOP_K = 2
        D = 256
        H = 2 * D
        logits = jnp.einsum('bsd,de->bse', x, Wg)
        top_vals, top_idx = jax.lax.top_k(logits, TOP_K)
        probs = jax.nn.softmax(top_vals, axis=-1)
        onehot = jax.nn.one_hot(top_idx, E, dtype=x.dtype)
        weights = jnp.einsum('bsk,bske->bse', probs, onehot)
        out = jnp.zeros_like(x)
        for e in range(E):
            u = jnp.einsum('bsd,dh->bsh', x, W1[e])
            v = jnp.einsum('bsd,dh->bsh', x, W2[e])
            h = u * jax.nn.sigmoid(u) * v
            y = jnp.einsum('bsh,hd->bsd', h, W3[e])
            out = out + y * weights[..., e][..., None]
        return out

    def _L1_attn_ref(x, omega_proj_w, omega_proj_b, omega_out_w, omega_out_b, vq_proj_in_w, vq_proj_in_b, vq_proj_out_w, vq_proj_out_b, codebook, omega_mix, vq_mix, norm_w):
        import jax, jax.numpy as jnp
        import numpy as np
        D_MODEL = 256
        OMEGA_DIM = 64
        VQ_CODES = 64
        VQ_DIM = 64
        N_PARAMS = OMEGA_DIM * (OMEGA_DIM - 1) // 2
        TRIU_R, TRIU_C = np.triu_indices(OMEGA_DIM, k=1)
        RMS_EPS = 1e-06
        NORM_EPS = 1e-12

        def _normalize(v):
            n = jnp.linalg.norm(v, axis=-1, keepdims=True)
            return v / jnp.maximum(n, NORM_EPS)

        def _rmsnorm(x, w):
            ms = jnp.mean(x * x, axis=-1, keepdims=True)
            return x * jax.lax.rsqrt(ms + RMS_EPS) * w
        B = x.shape[0]
        residual = x
        h_mean = jnp.mean(x, axis=1)
        params = h_mean @ omega_proj_w.T + omega_proj_b
        omega = jnp.zeros((B, OMEGA_DIM, OMEGA_DIM), x.dtype).at[:, TRIU_R, TRIU_C].set(params)
        omega = omega - jnp.swapaxes(omega, -1, -2)
        I = jnp.eye(OMEGA_DIM, dtype=x.dtype)
        omega2 = jnp.einsum('bij,bjk->bik', omega, omega)
        omega3 = jnp.einsum('bij,bjk->bik', omega2, omega)
        G = I + omega + 0.5 * omega2 + 1.0 / 6.0 * omega3
        x_head = x[:, :, :OMEGA_DIM]
        x_rotated = jnp.einsum('bld,bde->ble', x_head, G)
        lie_out = x_rotated @ omega_out_w.T + omega_out_b
        vq_input = h_mean @ vq_proj_in_w.T + vq_proj_in_b
        scores = _normalize(vq_input) @ _normalize(codebook).T
        vq_idx = jnp.argmax(scores, axis=-1)
        vq_code = codebook[vq_idx]
        vq_out = vq_input + jax.lax.stop_gradient(vq_code - vq_input)
        vq_contribution = (vq_out @ vq_proj_out_w.T + vq_proj_out_b)[:, None, :]
        out = residual + omega_mix * lie_out + vq_mix * vq_contribution
        return _rmsnorm(out, norm_w)

    def _L1_xattn_ref(q, k, v, Wq, bq, Wk, bk, Wv, bv):
        import jax, jax.numpy as jnp
        import numpy as np
        import math
        NUM_HEADS = 16
        B, S, D = q.shape
        H = NUM_HEADS
        hd = D // H
        qp = (q @ Wq + bq).reshape(B, H, S, hd)
        kp = k @ Wk + bk
        vp = v @ Wv + bv
        scale = 1.0 / math.sqrt(D)
        att = jnp.einsum('bhsd,btd->bhst', qp, kp) * scale
        att = jax.nn.softmax(att, axis=-1)
        out = jnp.einsum('bhst,btd->bhsd', att, vp)
        out = out.transpose(0, 2, 1, 3).reshape(B, S, D)
        return out

    def _L1_ffn_ref(X, routing_W, expert_bias, sW1, sb1, sW2, sb2, rW1, rb1, rW2, rb2):
        import jax, jax.numpy as jnp
        import numpy as np
        E = 8
        K = 2
        B, T, d = X.shape
        shared = jax.nn.silu(X @ sW1 + sb1) @ sW2 + sb2
        logits = jnp.einsum('btd,ed->bte', X, routing_W) + expert_bias
        activation = jnp.sqrt(jax.nn.softplus(logits))
        top_vals, top_idx = jax.lax.top_k(activation, K)
        combine = jnp.sum(jax.nn.one_hot(top_idx, E, dtype=X.dtype) * top_vals[..., None], axis=-2)
        Xf = X.reshape(-1, d)
        cf = combine.reshape(-1, E)
        hdn = jax.nn.silu(jnp.einsum('nd,edh->enh', Xf, rW1) + rb1[:, None, :])
        y = jnp.einsum('enh,ehd->end', hdn, rW2) + rb2[:, None, :]
        routed = jnp.einsum('ne,end->nd', cf, y).reshape(B, T, d)
        return shared + routed
    x = x + _L0_attn_ref(_layernorm(x, axis=-1), L0_attn_Wq, L0_attn_bq, L0_attn_Wk, L0_attn_bk, L0_attn_Wv, L0_attn_bv)
    x = x + _L0_xattn_ref(_layernorm(x, axis=-1), ctx_1024, ctx_1024, L0_xattn_W_Q, L0_xattn_W_K, L0_xattn_W_V, L0_xattn_g_w, L0_xattn_g_b, L0_xattn_out_w, L0_xattn_out_b)
    x = x + _L0_ffn_ref(_layernorm(x, axis=-1), L0_ffn_Wg, L0_ffn_W1, L0_ffn_W2, L0_ffn_W3)
    x = x + _L1_attn_ref(_layernorm(x, axis=-1), L1_attn_omega_proj_w, L1_attn_omega_proj_b, L1_attn_omega_out_w, L1_attn_omega_out_b, L1_attn_vq_proj_in_w, L1_attn_vq_proj_in_b, L1_attn_vq_proj_out_w, L1_attn_vq_proj_out_b, L1_attn_codebook, L1_attn_omega_mix, L1_attn_vq_mix, L1_attn_norm_w)
    x = x + _L1_xattn_ref(_layernorm(x, axis=-1), ctx_1024, ctx_1024, L1_xattn_Wq, L1_xattn_bq, L1_xattn_Wk, L1_xattn_bk, L1_xattn_Wv, L1_xattn_bv)
    x = x + _L1_ffn_ref(_layernorm(x, axis=-1), L1_ffn_routing_W, L1_ffn_expert_bias, L1_ffn_sW1, L1_ffn_sb1, L1_ffn_sW2, L1_ffn_sb2, L1_ffn_rW1, L1_ffn_rb1, L1_ffn_rW2, L1_ffn_rb2)
    return x

_drawn_inputs = setup_inputs


def setup_inputs(seed=0):
    import zlib

    import numpy as np

    out = dict(_drawn_inputs(seed))
    spreads = {'L0_attn_bq': (0.0, 2.0),
     'L0_attn_bk': (0.0, 2.0),
     'L0_attn_bv': (0.0, 2.0),
     'L0_xattn_g_b': (0.0, 0.1),
     'L0_xattn_out_b': (0.0, 0.1),
     'L1_attn_omega_proj_b': (0.0, 0.8),
     'L1_attn_omega_out_b': (0.0, 2.0),
     'L1_attn_vq_proj_in_b': (0.0, 0.8),
     'L1_attn_vq_proj_out_b': (0.0, 2.0),
     'L1_attn_norm_w': (1.0, 0.2),
     'L1_xattn_bq': (0.0, 2.0),
     'L1_xattn_bk': (0.0, 2.0),
     'L1_xattn_bv': (0.0, 0.1),
     'L1_ffn_expert_bias': (0.0, 0.1),
     'L1_ffn_sb1': (0.0, 0.8),
     'L1_ffn_sb2': (0.0, 0.1),
     'L1_ffn_rb1': (0.0, 0.8),
     'L1_ffn_rb2': (0.0, 0.1)}
    factors = {'L0_attn_Wq': 41.348,
     'L0_attn_Wk': 62.462,
     'L0_attn_Wv': 64.0,
     'L0_ffn_Wg': 4.024,
     'L0_ffn_W1': 3.594,
     'L0_ffn_W2': 3.579,
     'L0_ffn_W3': 3.519,
     'L1_attn_omega_proj_w': 8.0,
     'L1_attn_omega_out_w': 6.754,
     'L1_attn_vq_proj_in_w': 8.0,
     'L1_attn_vq_proj_out_w': 8.0,
     'L1_attn_codebook': 8.0,
     'L1_ffn_sW1': 3.426,
     'L1_ffn_sW2': 3.222}
    for name, (base, spread) in spreads.items():
        noise = np.random.default_rng([zlib.crc32(name.encode()), seed]).standard_normal(out[name].shape)
        drawn = base * np.exp(spread * noise) if base else spread * noise
        out[name] = jnp.asarray(drawn.astype(out[name].dtype))
    for name, factor in factors.items():
        out[name] = (out[name] * factor).astype(out[name].dtype)
    return out
```

```python
import concourse.bass as bass
from concourse import mybir
from contextlib import ExitStack

f32 = mybir.dt.float32
f16 = mybir.dt.float16
bf16 = mybir.dt.bfloat16
i32 = mybir.dt.int32
ALU = mybir.AluOpType
ACT = mybir.ActivationFunctionType
AX = mybir.AxisListType.X

B, S, D = 32, 128, 256
P = 128
DC = D // P
GB = 4
GT = GB * S
NG = B // GB
LN_EPS = 1e-5
E = 8
ONES = 32
TERMS = ((0, 0), (0, 1), (1, 0))


class Core:

    def __init__(self, nc, scope, sems, prefix):
        self.nc, self.scope, self.sems, self.prefix = nc, scope, sems, prefix

    def sb(self, name, shape, dt=f32):
        return self.scope.enter_context(self.nc.sbuf_tensor(self.prefix + name, shape, dt))

    def ps(self, name, shape, dt=f32):
        return self.scope.enter_context(self.nc.psum_tensor(self.prefix + name, shape, dt))

    def sem(self, name):
        self.sems.append(self.nc.alloc_semaphore(name=self.prefix + name))
        return self.sems[-1]


def give_back(nc, sems):
    with nc.Block() as block:
        @block.gpsimd
        def _(pool):
            nc.clear_and_free_semaphores(sems)


def spread(ap, n):
    return ap.unsqueeze(2).broadcast_to((ap.shape[0], ap.shape[1], n))


def repeat(ap, n):
    return ap.unsqueeze(1).broadcast_to((ap.shape[0], n, ap.shape[1]))


class RowStats:

    def __init__(self, c):
        self.stat = c.sb("rs_stat", [P, GB, 6])
        self.apart, self.apart2, self.both, self.dev, self.devs, self.mean, self.ve = (
            c.sb("rs_" + n, [P, GB]) for n in "apart apart2 both dev devs mean ve".split())
        self.stat_done, self.summed, self.scaled, self.ve_done = (
            c.sem("rs_" + n) for n in "stat_done summed scaled ve_done".split())

    def run(self, dve, X, g):
        mean_e, dev_e, mean_o, dev_o = (self.stat[:, :, n] for n in (1, 2, 4, 5))
        for b in range(GB):
            dve.bn_stats(self.stat[:, b, :], X[:, g * GB + b, :]).then_inc(self.stat_done, 1)
        dve.wait_ge(self.stat_done, g * GB + GB)
        dve.tensor_tensor(self.apart[:, :], mean_e, mean_o, ALU.subtract).then_inc(self.summed, 1)
        dve.tensor_tensor(self.both[:, :], mean_e, mean_o, ALU.add).then_inc(self.summed, 1)
        dve.tensor_tensor(self.dev[:, :], dev_e, dev_o, ALU.add).then_inc(self.summed, 1)
        dve.wait_ge(self.summed, g * 3 + 3)
        dve.tensor_tensor(self.apart2[:, :], self.apart[:, :], self.apart[:, :], ALU.mult).then_inc(self.scaled, 1)
        dve.tensor_scalar(self.mean[:, :], self.both[:, :], 0.5, None, ALU.mult).then_inc(self.scaled, 1)
        dve.tensor_scalar(self.devs[:, :], self.dev[:, :], 1.0 / D, LN_EPS, ALU.mult, ALU.add).then_inc(self.scaled, 1)
        dve.wait_ge(self.scaled, g * 3 + 3)
        dve.scalar_tensor_tensor(self.ve[:, :], self.apart2[:, :], 0.25, self.devs[:, :], ALU.mult, ALU.add)\
           .then_inc(self.ve_done, 1)


class Front:

    def __init__(self, c, X, ident, power, turn, used):
        self.X, self.ident, self.power, self.turn, self.used = X, ident, power, turn, used
        self.rs = RowStats(c)
        self.rstd = c.sb("ln_rstd", [P, GB])
        self.xn = c.sb("ln_xn", [P, GB, D])
        self.xh = c.sb("xh", [P, DC, GT], f16)
        self.xl = c.sb("xl", [P, DC, GT], f16)
        self.rstd_done = c.sem("ln_rstd_done")
        self.xn_done = c.sem("ln_xn_done")
        self.turned = c.sem("ln_turned")
        self.xh_done = c.sem("xh_done")
        self.xl_done = c.sem("xl_done")

    def stats(self, dve, g):
        self.rs.run(dve, self.X, g)

    def power_of_var(self, pool, g):
        pool.wait_ge(self.rs.ve_done, g + 1)
        pool.tensor_tensor(self.rstd[:, :], self.rs.ve[:, :], self.power[:, 0:GB], ALU.pow).then_inc(self.rstd_done, 1)

    def norm(self, dve, g, first=False):
        dve.wait_ge(self.rstd_done, g + 1)
        if not first:
            dve.wait_ge(self.turned, g)
        for b in range(GB):
            dve.tensor_scalar(self.xn[:, b, :], self.X[:, g * GB + b, :], self.rs.mean[:, b:b + 1],
                              self.rstd[:, b:b + 1], ALU.subtract, ALU.mult).then_inc(self.xn_done, 1)

    def transpose(self, pe, g):
        pe.wait_ge(self.xn_done, g * GB + GB)
        for dc in range(DC):
            for b in range(GB):
                last = pe.transpose(self.turn[:, dc, b * S:(b + 1) * S], self.xn[:, b, dc * P:(dc + 1) * P],
                                    self.ident[:, :])
        last.then_inc(self.turned, 1)

    def high(self, act, g, first=False):
        act.wait_ge(self.turned, g + 1)
        if not first:
            sem, per = self.used
            act.wait_ge(sem, g * per)
        act.activation(self.xh[:, :, :], self.turn[:, :, :], ACT.Copy).then_inc(self.xh_done, 1)

    def low(self, dve, g):
        dve.wait_ge(self.xh_done, g + 1)
        dve.tensor_tensor(self.xl[:, :, :], self.turn[:, :, :], self.xh[:, :, :], ALU.subtract)\
           .then_inc(self.xl_done, 1)


def split_weights(nc, sems, jobs, name):
    WIDE = 2048
    pieces = []
    for src, hi, lo, factor in jobs:
        n = src.shape[1]
        for a in range(0, n, WIDE):
            z = min(n, a + WIDE)
            pieces.append((src[:, a:z], hi[:, a:z], lo[:, a:z], factor))
    with ExitStack() as scope:
        c = Core(nc, scope, sems, name)
        stage = c.sb("stage", [P, 3, WIDE])
        loaded = [c.sem(f"loaded{i}") for i in range(3)]
        high_done, low_done = c.sem("high_done"), c.sem("low_done")
        with nc.Block() as block:
            @block.sync
            def _(sp):
                for n, (src, hi, lo, factor) in enumerate(pieces):
                    if n >= 3:
                        sp.wait_ge(low_done, n - 2)
                    sp.dma_start(stage[0:src.shape[0], n % 3, 0:src.shape[1]], src).then_inc(loaded[n % 3], 16)

            @block.scalar
            def _(act):
                for n, (src, hi, lo, factor) in enumerate(pieces):
                    act.wait_ge(loaded[n % 3], 16 * (n // 3 + 1))
                    act.activation(hi, stage[0:src.shape[0], n % 3, 0:src.shape[1]], ACT.Copy, scale=factor)\
                       .then_inc(high_done, 1)

            @block.vector
            def _(dve):
                for n, (src, hi, lo, factor) in enumerate(pieces):
                    dve.wait_ge(high_done, n + 1)
                    dve.scalar_tensor_tensor(lo, stage[0:src.shape[0], n % 3, 0:src.shape[1]], factor, hi,
                                             ALU.mult, ALU.subtract).then_inc(low_done, 1)


def project_features(pe, out, weight, cols, moving, done=None):
    steps = [(dc, a, b) for dc in range(DC) for a, b in TERMS]
    for n, (dc, a, b) in enumerate(steps):
        last = pe.matmul(out, weight[a][:, dc, cols], moving[b][:, dc, :], start=(n == 0), stop=(n == len(steps) - 1))
    return last


def project_tokens(pe, out, weight, cols, still, tokens):
    steps = [(dc, a, b) for dc in range(DC) for a, b in TERMS]
    for n, (dc, a, b) in enumerate(steps):
        last = pe.matmul(out, still[a][:, dc, tokens], weight[b][:, dc, cols], start=(n == 0),
                         stop=(n == len(steps) - 1))
    return last


def softmax_attention(nc, sems, X, ident, power, A):
    SCALE = 16.0
    with ExitStack() as scope:
        c = Core(nc, scope, sems, "a_")
        W = {n: [c.sb(f"w{n}{t}", [P, DC, D], f16) for t in range(2)] for n in "qkv"}
        split_weights(nc, sems, [(A[f"L0_attn_W{n}"].rearrange("p a b -> p (a b)"),
                                  W[n][0][:, :, :].rearrange("p a b -> p (a b)"),
                                  W[n][1][:, :, :].rearrange("p a b -> p (a b)"), SCALE) for n in "qkv"], "aw_")
        pA, pB, pC, pD = (c.ps(n, [P, 2, 512]) for n in ("pA", "pB", "pC", "pD"))
        projected = {n: c.sem(f"{n}_projected") for n in "qkv"}
        fr = Front(c, X, ident, power, pA, (projected["v"], 1))
        bq = c.sb("bq", [P, D])
        bkv = c.sb("bkv", [P, 2, DC])
        bias_in = c.sem("bias_in")
        bkvs = c.sb("bkvs", [P, 2, DC])
        bias_done = c.sem("bias_done")
        q = c.sb("q", [P, GB, D])
        nqmax = c.sb("nqmax", [P, GB])
        qe = c.sb("qe", [P, GB, D])
        qsum = c.sb("qsum", [P, GB])
        qs16 = c.sb("qs16", [P, GB])
        rq = c.sb("rq", [P, GB])
        mx = {n: c.sb(f"{n}max", [P, 2 * GB]) for n in "kv"}
        mb = {n: c.sb(f"{n}maxb", [P, 2 * GB]) for n in "kv"}
        dif = {n: c.sb(f"{n}dif", [P, DC, GT]) for n in "kv"}
        ex = {n: c.sb(f"{n}exp", [P, DC, GT]) for n in "kv"}
        sm = {n: c.sb(f"{n}sum", [P, 2 * GB]) for n in "kv"}
        rs = {n: c.sb(f"{n}rec", [P, 2 * GB]) for n in "kv"}
        vn = c.sb("vn", [P, DC, GT])
        qT = c.sb("qT", [P, DC, GT])
        vt = c.sb("vt", [P, GB, D])
        aT = c.sb("aT", [P, GB, S])
        names = ("q_biased nqmax_done qexp_done q16_done rq_done qe_turned qT_done vn_done vn_turned vt_done "
                 "attended aT_done weighed x_done").split()
        s = {n: c.sem(n) for n in names}
        kv = {(n, w): c.sem(f"{n}_{w}") for n in "kv" for w in ("max", "maxb", "dif", "exp", "sum", "rec")}
        pC8 = pC[:, :, :].rearrange("p a (b t) -> p (a b) t", t=S)
        pD8 = pD[:, :, :].rearrange("p a (b t) -> p (a b) t", t=S)
        pA8 = pA[:, :, :].rearrange("p a (b t) -> p (a b) t", t=S)
        pB4 = pB[:, :, :].rearrange("p a (b t) -> p (a b) t", t=D)
        pD4 = pD[:, :, :].rearrange("p a (b t) -> p (a b) t", t=D)
        pC4 = pC[:, :, :].rearrange("p a (b t) -> p (a b) t", t=D)

        def eight(t):
            return t[:, :, :].rearrange("p a (b t) -> p (a b) t", t=S)

        with nc.Block() as block:
            @block.sync
            def _(sp):
                sp.dma_start(bq[:, :], A["L0_attn_bq"].partition_broadcast(P)).then_inc(bias_in, 16)
                sp.dma_start(bkv[:, 0, :], A["L0_attn_bk"]).then_inc(bias_in, 16)
                sp.dma_start(bkv[:, 1, :], A["L0_attn_bv"]).then_inc(bias_in, 16)

            @block.tensor
            def _(pe):
                def main(g, first, nxt):
                    pe.wait_ge(fr.xl_done, g + 1)
                    if not first:
                        pe.wait_ge(s["aT_done"], g)
                    for b in range(GB):
                        last = project_tokens(pe, pB4[:, b, :], [w[:, :, :] for w in W["q"]], slice(0, D),
                                              (fr.xh, fr.xl), slice(b * S, (b + 1) * S))
                    last.then_inc(projected["q"], 1)
                    if not first:
                        pe.wait_ge(s["vt_done"], g)
                    for m in range(DC):
                        last = project_features(pe, pC[:, m, :], W["k"], slice(m * P, (m + 1) * P), (fr.xh, fr.xl))
                    last.then_inc(projected["k"], 1)
                    if not first:
                        pe.wait_ge(s["x_done"], g * GB)
                    for m in range(DC):
                        last = project_features(pe, pD[:, m, :], W["v"], slice(m * P, (m + 1) * P), (fr.xh, fr.xl))
                    last.then_inc(projected["v"], 1)
                    pe.wait_ge(s["qexp_done"], g * GB + GB)
                    for dc in range(DC):
                        for b in range(GB):
                            last = pe.transpose(pA[:, dc, b * S:(b + 1) * S], qe[:, b, dc * P:(dc + 1) * P], ident[:, :])
                    last.then_inc(s["qe_turned"], 1)
                    pe.wait_ge(kv["k", "dif"], g * 2 + 2)
                    pe.wait_ge(s["vn_done"], g + 1)
                    for b in range(GB):
                        for dc in range(DC):
                            last = pe.transpose(pC4[:, b, dc * P:(dc + 1) * P], vn[:, dc, b * S:(b + 1) * S], ident[:, :])
                    last.then_inc(s["vn_turned"], 1)
                    pe.wait_ge(s["qT_done"], g + 1)
                    pe.wait_ge(kv["k", "exp"], g + 1)
                    for b in range(GB):
                        t = slice(b * S, (b + 1) * S)
                        for dc in range(DC):
                            last = pe.matmul(pB[:, 0, t], ex["k"][:, dc, t], qT[:, dc, t], start=(dc == 0), stop=(dc == DC - 1))
                    last.then_inc(s["attended"], 1)
                    if nxt is not None:
                        fr.transpose(pe, nxt)
                    pe.wait_ge(s["aT_done"], g + 1)
                    pe.wait_ge(s["vt_done"], g + 1)
                    pe.wait_ge(kv["v", "dif"], g * 2 + 2)
                    for b in range(GB):
                        last = pe.matmul(pD4[:, b, :], aT[:, b, :], vt[:, b, :], start=True, stop=True)
                    last.then_inc(s["weighed"], 1)

                fr.transpose(pe, 0)
                main(0, True, 1)
                with pe.Fori(1, NG - 1) as g:
                    main(g, False, g + 1)
                main(NG - 1, False, None)

            @block.vector
            def _(dve):
                def difference(n, g, psum8):
                    at = 0 if n == "k" else 1
                    dve.wait_ge(projected[n], g + 1)
                    dve.tensor_reduce(mx[n][:, :], psum8, AX, ALU.max).then_inc(kv[n, "max"], 1)
                    dve.wait_ge(kv[n, "max"], g + 1)
                    dve.tensor_tensor(mb[n][:, :].rearrange("p (a b) -> p a b", a=DC),
                                      mx[n][:, :].rearrange("p (a b) -> p a b", a=DC),
                                      spread(bkvs[:, at, :], GB), ALU.add).then_inc(kv[n, "maxb"], 1)
                    dve.wait_ge(kv[n, "maxb"], g + 1)
                    for m in range(DC):
                        dve.scalar_tensor_tensor(eight(dif[n])[:, m * GB:(m + 1) * GB, :], psum8[:, m * GB:(m + 1) * GB, :],
                                                 bkvs[:, at, m:m + 1], spread(mb[n][:, m * GB:(m + 1) * GB], S),
                                                 ALU.add, ALU.subtract).then_inc(kv[n, "dif"], 1)

                def main(g, first, nxt):
                    dve.wait_ge(projected["q"], g + 1)
                    dve.scalar_tensor_tensor(q[:, :, :], pB4, 1.0 / SCALE, repeat(bq[:, :], GB), ALU.mult, ALU.add)\
                       .then_inc(s["q_biased"], 1)
                    dve.wait_ge(s["q_biased"], g + 1)
                    dve.tensor_reduce(nqmax[:, :], q[:, :, :], AX, ALU.max, negate=True).then_inc(s["nqmax_done"], 1)
                    difference("k", g, pC8)
                    difference("v", g, pD8)
                    if nxt is not None:
                        fr.stats(dve, nxt)
                    dve.wait_ge(kv["k", "exp"], g + 1)
                    dve.tensor_reduce(sm["k"][:, :], eight(ex["k"]), AX, ALU.add).then_inc(kv["k", "sum"], 1)
                    dve.wait_ge(kv["k", "sum"], g + 1)
                    dve.reciprocal(rs["k"][:, :], sm["k"][:, :]).then_inc(kv["k", "rec"], 1)
                    dve.wait_ge(kv["k", "rec"], g + 1)
                    dve.wait_ge(s["qe_turned"], g + 1)
                    dve.tensor_tensor(eight(qT), pA8, spread(rs["k"][:, :], S), ALU.mult).then_inc(s["qT_done"], 1)
                    dve.wait_ge(kv["v", "exp"], g + 1)
                    dve.tensor_reduce(sm["v"][:, :], eight(ex["v"]), AX, ALU.add).then_inc(kv["v", "sum"], 1)
                    dve.wait_ge(kv["v", "sum"], g + 1)
                    dve.reciprocal(rs["v"][:, :], sm["v"][:, :]).then_inc(kv["v", "rec"], 1)
                    if nxt is not None:
                        fr.norm(dve, nxt)
                    dve.wait_ge(s["qexp_done"], g * GB + GB)
                    dve.tensor_scalar(qs16[:, :], qsum[:, :], float(D) ** 0.5, None, ALU.mult).then_inc(s["q16_done"], 1)
                    dve.wait_ge(s["q16_done"], g + 1)
                    dve.reciprocal(rq[:, :], qs16[:, :]).then_inc(s["rq_done"], 1)
                    if nxt is not None:
                        fr.low(dve, nxt)
                    dve.wait_ge(s["rq_done"], g + 1)
                    dve.wait_ge(s["weighed"], g + 1)
                    for b in range(GB):
                        dve.scalar_tensor_tensor(X[:, g * GB + b, :], pD4[:, b, :], rq[:, b:b + 1], X[:, g * GB + b, :],
                                                 ALU.mult, ALU.add).then_inc(s["x_done"], 1)

                dve.wait_ge(bias_in, 48)
                dve.tensor_scalar(bkvs[:, :, :], bkv[:, :, :], SCALE, None, ALU.mult).then_inc(bias_done, 1)
                dve.wait_ge(bias_done, 1)
                fr.stats(dve, 0)
                fr.norm(dve, 0, first=True)
                fr.low(dve, 0)
                main(0, True, 1)
                with dve.Fori(1, NG - 1) as g:
                    main(g, False, g + 1)
                main(NG - 1, False, None)

            @block.scalar
            def _(act):
                def main(g, first, nxt):
                    act.wait_ge(s["nqmax_done"], g + 1)
                    for b in range(GB):
                        act.activation(qe[:, b, :], q[:, b, :], ACT.Exp, bias=nqmax[:, b:b + 1],
                                       accum_out=qsum[:, b:b + 1]).then_inc(s["qexp_done"], 1)
                    for n in "kv":
                        act.wait_ge(kv[n, "dif"], g * 2 + 2)
                        act.activation(ex[n][:, :, :], dif[n][:, :, :], ACT.Exp, scale=1.0 / SCALE)\
                           .then_inc(kv[n, "exp"], 1)
                    act.wait_ge(s["vn_turned"], g + 1)
                    act.activation(vt[:, :, :], pC4, ACT.Copy).then_inc(s["vt_done"], 1)
                    act.wait_ge(s["attended"], g + 1)
                    act.activation(aT[:, :, :].rearrange("p a b -> p (a b)"), pB[:, 0, :], ACT.Copy).then_inc(s["aT_done"], 1)
                    if nxt is not None:
                        fr.high(act, nxt)

                nc.scalar.preload_act_table(ACT.Exp)
                fr.high(act, 0, first=True)
                main(0, True, 1)
                with act.Fori(1, NG - 1) as g:
                    main(g, False, g + 1)
                main(NG - 1, False, None)

            @block.gpsimd
            def _(pool):
                def main(g, first, nxt):
                    if nxt is not None:
                        fr.power_of_var(pool, nxt)
                    pool.wait_ge(kv["v", "rec"], g + 1)
                    pool.tensor_tensor(eight(vn), eight(ex["v"]), spread(rs["v"][:, :], S), ALU.mult)\
                        .then_inc(s["vn_done"], 1)

                fr.power_of_var(pool, 0)
                main(0, True, 1)
                with pool.Fori(1, NG - 1) as g:
                    main(g, False, g + 1)
                main(NG - 1, False, None)


class Router:

    def __init__(self, c, X, ident, power, XH, XL, Wg):
        self.turn = [c.ps(f"turn{i}", [P, DC, GT]) for i in range(1)]
        self.logits = c.ps("logits", [P, B, E])
        self.fr = Front(c, X, ident, power, self.turn[0], None)
        self.XH, self.XL, self.Wg = XH, XL, Wg
        self.logits_done = c.sem("logits_done")

    def high(self, act, g):
        fr = self.fr
        act.wait_ge(fr.turned, g + 1)
        act.activation(self.XH[:, :, bass.ds(g * GT, GT)], fr.turn[:, :, :], ACT.Copy).then_inc(fr.xh_done, 1)

    def low(self, dve, g):
        fr = self.fr
        dve.wait_ge(fr.xh_done, g + 1)
        dve.tensor_tensor(self.XL[:, :, bass.ds(g * GT, GT)], fr.turn[:, :, :], self.XH[:, :, bass.ds(g * GT, GT)],
                          ALU.subtract).then_inc(fr.xl_done, 1)

    def engines(self, block):
        fr = self.fr

        @block.tensor
        def _(pe):
            fr.transpose(pe, 0)

            def rest(g):
                pe.wait_ge(fr.xl_done, g)
                fr.transpose(pe, g)
            with pe.Fori(1, NG) as g:
                rest(g)
            pe.wait_ge(fr.xl_done, NG)
            steps = [(dc, a, b) for dc in range(DC) for a, b in TERMS]
            for t in range(B):
                for n, (dc, a, b) in enumerate(steps):
                    last = pe.matmul(self.logits[:, t, :], (self.XH, self.XL)[a][:, dc, t * S:(t + 1) * S],
                                     self.Wg[b][:, dc, :], start=(n == 0), stop=(n == len(steps) - 1))
            last.then_inc(self.logits_done, 1)

        @block.scalar
        def _(act):
            self.high(act, 0)
            with act.Fori(1, NG) as g:
                self.high(act, g)

        @block.gpsimd
        def _(pool):
            with pool.Fori(0, NG) as g:
                fr.power_of_var(pool, g)

        @block.vector
        def _(dve):
            fr.stats(dve, 0)
            fr.norm(dve, 0, first=True)
            with dve.Fori(0, NG - 1) as g:
                fr.stats(dve, g + 1)
                fr.norm(dve, g + 1)
                self.low(dve, g)
            self.low(dve, NG - 1)


def choose_two(c, dve, score, lower, s, wait):
    gt = c.sb("gt", [P, B, E, E])
    eq = c.sb("eq", [P, B, E, E])
    rank = c.sb("rank", [P, B, E])
    chosen = c.sb("chosen", [P, B, E])
    mine = score[:, :, :].unsqueeze(3).broadcast_to((P, B, E, E))
    other = score[:, :, :].unsqueeze(2).broadcast_to((P, B, E, E))
    dve.tensor_tensor(gt[:, :, :, :], other, mine, ALU.is_gt).then_inc(s, 1)
    dve.tensor_tensor(eq[:, :, :, :], other, mine, ALU.is_equal).then_inc(s, 1)
    wait(2)
    dve.tensor_tensor(eq[:, :, :, :].rearrange("p b e f -> p b (e f)"), eq[:, :, :, :].rearrange("p b e f -> p b (e f)"),
                      repeat(lower[:, :], B), ALU.mult).then_inc(s, 1)
    wait(1)
    dve.tensor_tensor(gt[:, :, :, :], gt[:, :, :, :], eq[:, :, :, :], ALU.add).then_inc(s, 1)
    wait(1)
    dve.tensor_reduce(rank[:, :, :].rearrange("p b e -> p (b e)"), gt[:, :, :, :].rearrange("p b e f -> p (b e) f"),
                      AX, ALU.add).then_inc(s, 1)
    wait(1)
    dve.tensor_scalar(chosen[:, :, :], rank[:, :, :], 1.5, None, ALU.is_lt).then_inc(s, 1)
    wait(1)
    return chosen


def starts(value, n):
    return isinstance(value, int) and value == n


def own_steps(dve, s):
    count = [0]

    def wait(n):
        count[0] += n
        dve.wait_ge(s, count[0])
    return wait


class Shares:

    def __init__(self, c, cfT, ident16):
        self.c, self.cfT, self.ident16 = c, cfT, ident16
        self.parts = c.sb("parts", [P, B, 3, E], f16)
        self.left1 = c.sb("left1", [P, B, E])
        self.left2 = c.sb("left2", [P, B, E])
        self.turned = c.ps("shares_turned", [P, B * S], f16)
        self.parts_done = c.sem("parts_done")
        self.shares_turned = c.sem("shares_turned_done")
        self.cfT_done = c.sem("cfT_done")

    def cut(self, dve, share, s, wait):
        dve.tensor_copy(self.parts[:, :, 0, :], share[:, :, :]).then_inc(s, 1)
        wait(1)
        dve.tensor_tensor(self.left1[:, :, :], share[:, :, :], self.parts[:, :, 0, :], ALU.subtract).then_inc(s, 1)
        wait(1)
        dve.tensor_copy(self.parts[:, :, 1, :], self.left1[:, :, :]).then_inc(s, 1)
        wait(1)
        dve.tensor_tensor(self.left2[:, :, :], self.left1[:, :, :], self.parts[:, :, 1, :], ALU.subtract).then_inc(s, 1)
        wait(1)
        dve.tensor_copy(self.parts[:, :, 2, :], self.left2[:, :, :]).then_inc(self.parts_done, 1)

    def turn(self, pe):
        pe.wait_ge(self.parts_done, 1)
        for b in range(B):
            last = pe.transpose(self.turned[0:3 * E, b * S:(b + 1) * S],
                                self.parts[:, b, :, :].rearrange("p a e -> p (a e)"), self.ident16[:, :])
        last.then_inc(self.shares_turned, 1)

    def keep(self, dve):
        dve.wait_ge(self.shares_turned, 1)
        dve.tensor_copy(self.cfT[0:3 * E, :], self.turned[0:3 * E, :]).then_inc(self.cfT_done, 1)


def constants(nc, sems, ident, ident16, lower, select, cfT, prefix):
    with ExitStack() as scope:
        c = Core(nc, scope, sems, prefix)
        zeroed, made, copied = c.sem("zeroed"), c.sem("made"), c.sem("copied")
        with nc.Block() as block:
            @block.gpsimd
            def _(pool):
                pool.memset(lower[:, :], 1.0).then_inc(zeroed, 1)
                pool.memset(select[:, :, :], 0.0).then_inc(zeroed, 1)
                pool.wait_ge(zeroed, 2)
                pool.affine_select(out=lower[:, :].rearrange("p (e f) -> p e f", e=E),
                                   in_=lower[:, :].rearrange("p (e f) -> p e f", e=E), compare_op=ALU.is_gt, fill=0.0,
                                   base=0, pattern=[[1, E], [-1, E]], channel_multiplier=0).then_inc(made, 1)
                for part in range(3):
                    pool.affine_select(out=select[:, :, :], in_=select[:, :, :], compare_op=ALU.not_equal, fill=1.0,
                                       base=-E * part, pattern=[[-1, E], [0, P]], channel_multiplier=1)\
                        .then_inc(made, 1)
                    pool.wait_ge(made, part + 2)

            @block.vector
            def _(dve):
                dve.tensor_copy(ident16[:, :], ident[:, :]).then_inc(copied, 1)
                dve.memset(cfT[:, :], 0.0).then_inc(copied, 1)
                dve.wait_ge(copied, 2)
                dve.memset(cfT[ONES:ONES + 1, :], 1.0).then_inc(copied, 1)


def moe_swiglu(nc, sems, X, ident, power, A):
    SCALE = 256.0
    HC = 4
    HID = HC * P
    with ExitStack() as scope:
        c = Core(nc, scope, sems, "m_")
        XH, XL = c.sb("XH", [P, DC, B * S], f16), c.sb("XL", [P, DC, B * S], f16)
        cfT = c.sb("cfT", [P, B * S], f16)
        ident16 = c.sb("ident16", [P, P], f16)
        lower = c.sb("lower", [P, E * E])
        select = c.sb("select", [P, E, P], f16)
        constants(nc, sems, ident, ident16, lower, select, cfT, "const1_")
        W1, W2 = ([c.sb(f"w{n}{t}", [P, E, DC, HID], f16) for t in range(2)] for n in (1, 2))
        W3 = [c.sb(f"w3{t}", [P, E, HC, D], f16) for t in range(2)]
        Wg = [c.sb(f"wg{t}", [P, DC, E], f16) for t in range(2)]

        def flat(t):
            return t.rearrange("p a b c -> p (a b c)") if len(t.shape) == 4 else t.rearrange("p a b -> p (a b)")

        split_weights(nc, sems, [(flat(A[f"L0_ffn_{n}"]), flat(w[0][:]), flat(w[1][:]), SCALE)
                                 for n, w in (("Wg", Wg), ("W1", W1), ("W2", W2), ("W3", W3))], "mw_")
        with ExitStack() as inner:
            r = Core(nc, inner, sems, "mr_")
            route = Router(r, X, ident, power, XH, XL, Wg)
            shares = Shares(r, cfT, ident16)
            lg, top, low, ex, kept, tot, rec, share = (
                r.sb(n, [P, B, E]) if n in ("lg", "low", "ex", "kept", "share") else r.sb(n, [P, B])
                for n in ("lg", "top", "low", "ex", "kept", "tot", "rec", "share"))
            s, exp_done, low_done = r.sem("routing"), r.sem("exp_done"), r.sem("low_done")
            with nc.Block() as block:
                route.engines(block)
            with nc.Block() as block:
                @block.vector
                def _(dve):
                    wait = own_steps(dve, s)
                    dve.tensor_scalar(lg[:, :, :], route.logits[:, :, :], 1.0 / SCALE, None, ALU.mult).then_inc(s, 1)
                    wait(1)
                    dve.tensor_reduce(top[:, :], lg[:, :, :], AX, ALU.max).then_inc(s, 1)
                    wait(1)
                    dve.tensor_tensor(low[:, :, :], lg[:, :, :], spread(top[:, :], E), ALU.subtract)\
                       .then_inc(low_done, 1)
                    chosen = choose_two(r, dve, lg, lower, s, wait)
                    dve.wait_ge(exp_done, 1)
                    dve.tensor_tensor(kept[:, :, :], ex[:, :, :], chosen[:, :, :], ALU.mult).then_inc(s, 1)
                    wait(1)
                    dve.tensor_reduce(tot[:, :], kept[:, :, :], AX, ALU.add).then_inc(s, 1)
                    wait(1)
                    dve.reciprocal(rec[:, :], tot[:, :]).then_inc(s, 1)
                    wait(1)
                    dve.tensor_tensor(share[:, :, :], kept[:, :, :], spread(rec[:, :], E), ALU.mult).then_inc(s, 1)
                    wait(1)
                    shares.cut(dve, share, s, wait)
                    shares.keep(dve)

                @block.scalar
                def _(act):
                    act.wait_ge(low_done, 1)
                    act.activation(ex[:, :, :], low[:, :, :], ACT.Exp).then_inc(exp_done, 1)

                @block.tensor
                def _(pe):
                    shares.turn(pe)
        pU = [c.ps(f"pU{i}", [P, GT]) for i in range(2)]
        pV = [c.ps(f"pV{i}", [P, GT]) for i in range(2)]
        pC = c.ps("pC", [P, GT])
        pY = c.ps("pY", [P, GB, D])
        sg, t_, h, hc = ([c.sb(f"{n}{i}", [P, GT]) for i in range(2)] for n in ("sg", "t", "h", "hc"))
        hh, hl = ([c.sb(f"{n}{i}", [P, GT], f16) for i in range(HC)] for n in ("hh", "hl"))
        cfB = c.sb("cfB", [P, GT])
        (u_done, v_done, sg_done, t_done, h_done, hc_done, hh_done, hl_done, down_done, share_spread, cfB_done,
         y_added) = (c.sem(n) for n in "u_done v_done sg_done t_done h_done hc_done hh_done hl_done down_done "
                                       "share_spread cfB_done y_added".split())
        PER = E * HC

        def run(eng, step, tail):
            step(0, 0, None)
            step(0, 1, (0, 0))
            with eng.Fori(2, E) as e:
                step(0, e, (0, e - 1))
            with eng.Fori(1, NG) as g:
                step(g, 0, (g - 1, E - 1))
                with eng.Fori(1, E) as e:
                    step(g, e, (g, e - 1))
            tail((NG - 1, E - 1))

        with nc.Block() as block:
            @block.tensor
            def _(pe):
                def down(g, e, j, first):
                    pe.wait_ge(hl_done, g * PER + e * HC + j + 1)
                    for b in range(GB):
                        for n, (x, y) in enumerate(TERMS):
                            last = pe.matmul(pY[:, b, :], (hh, hl)[x][j][:, b * S:(b + 1) * S], W3[y][:, e, j, :],
                                             start=first and n == 0 and b % 2 == 0, stop=False, skip_group_check=True)
                    last.then_inc(down_done, 1)

                def step(g, e, prev):
                    i0 = g * PER + e * HC
                    for j in range(HC):
                        if prev is not None or j >= 2:
                            pe.wait_ge(h_done, i0 + j - 1)
                        if j == 0:
                            if prev is not None:
                                pe.wait_ge(cfB_done, g * E + e)
                            pe.matmul(pC[:, :], select[:, e, :], cfT[:, bass.ds(g * GT, GT)], start=True, stop=True)\
                              .then_inc(share_spread, 1)
                        for ps, W, sem in ((pU, W1, u_done), (pV, W2, v_done)):
                            steps = [(dc, x, y) for dc in range(DC) for x, y in TERMS]
                            for n, (dc, x, y) in enumerate(steps):
                                last = pe.matmul(ps[j % 2][:, :], W[x][:, e, dc, j * P:(j + 1) * P],
                                                 (XH, XL)[y][:, dc, bass.ds(g * GT, GT)], start=(n == 0),
                                                 stop=(n == len(steps) - 1))
                            last.then_inc(sem, 1)
                        if j >= 2:
                            if j == 2 and starts(e, 0) and prev is not None:
                                pe.wait_ge(y_added, g)
                            down(g, e, j - 2, starts(e, 0) and j == 2)
                        elif prev is not None:
                            down(prev[0], prev[1], j + 2, False)

                def tail(prev):
                    down(prev[0], prev[1], HC - 2, False)
                    down(prev[0], prev[1], HC - 1, False)
                run(pe, step, tail)

            @block.scalar
            def _(act):
                def high(g, e, j, early):
                    k = g * PER + e * HC + j
                    act.wait_ge(hc_done, k + 1)
                    if not early:
                        act.wait_ge(down_done, k - HC + 1)
                    act.activation(hh[j][:, :], hc[j % 2][:, :], ACT.Copy).then_inc(hh_done, 1)

                def step(g, e, prev):
                    i0 = g * PER + e * HC
                    for j in range(HC):
                        act.wait_ge(u_done, i0 + j + 1)
                        if prev is not None or j >= 2:
                            act.wait_ge(t_done, i0 + j - 1)
                        act.activation(sg[j % 2][:, :], pU[j % 2][:, :], ACT.Sigmoid, scale=1.0 / SCALE)\
                           .then_inc(sg_done, 1)
                        if j > 0:
                            high(g, e, j - 1, prev is None)
                        elif prev is not None:
                            high(prev[0], prev[1], HC - 1, starts(e, 1) and starts(g, 0))
                        if j == 0:
                            if prev is not None:
                                act.wait_ge(hc_done, i0)
                            act.wait_ge(share_spread, g * E + e + 1)
                            act.activation(cfB[:, :], pC[:, :], ACT.Copy).then_inc(cfB_done, 1)

                def tail(prev):
                    high(prev[0], prev[1], HC - 1, False)
                nc.scalar.preload_act_table(ACT.Sigmoid)
                run(act, step, tail)

            @block.gpsimd
            def _(pool):
                def step(g, e, prev):
                    i0 = g * PER + e * HC
                    pool.wait_ge(cfB_done, g * E + e + 1)
                    for j in range(HC):
                        pool.wait_ge(h_done, i0 + j + 1)
                        if prev is not None or j >= 2:
                            pool.wait_ge(hl_done, i0 + j - 1)
                        pool.tensor_tensor(hc[j % 2][:, :], h[j % 2][:, :], cfB[:, :], ALU.mult).then_inc(hc_done, 1)
                run(pool, step, lambda prev: None)

            @block.vector
            def _(dve):
                def low(g, e, j):
                    k = g * PER + e * HC + j
                    dve.wait_ge(hh_done, k + 1)
                    dve.tensor_tensor(hl[j][:, :], hc[j % 2][:, :], hh[j][:, :], ALU.subtract).then_inc(hl_done, 1)

                def take(g):
                    dve.wait_ge(down_done, g * PER + PER)
                    dve.scalar_tensor_tensor(X[:, bass.ds(g * GB, GB), :], pY[:, :, :], 1.0 / SCALE,
                                             X[:, bass.ds(g * GB, GB), :], ALU.mult, ALU.add).then_inc(y_added, 1)

                def step(g, e, prev):
                    i0 = g * PER + e * HC
                    for j in range(HC):
                        dve.wait_ge(sg_done, i0 + j + 1)
                        if prev is not None or j >= 2:
                            dve.wait_ge(h_done, i0 + j - 1)
                        dve.tensor_tensor(t_[j % 2][:, :], pU[j % 2][:, :], sg[j % 2][:, :], ALU.mult).then_inc(t_done, 1)
                        dve.wait_ge(t_done, i0 + j + 1)
                        dve.wait_ge(v_done, i0 + j + 1)
                        if prev is not None or j >= 2:
                            dve.wait_ge(hc_done, i0 + j - 1)
                        dve.scalar_tensor_tensor(h[j % 2][:, :], t_[j % 2][:, :], 1.0 / SCALE / SCALE, pV[j % 2][:, :],
                                                 ALU.mult, ALU.mult).then_inc(h_done, 1)
                        if j > 0:
                            low(g, e, j - 1)
                        elif prev is not None:
                            low(prev[0], prev[1], HC - 1)
                        if j == 1 and starts(e, 0) and prev is not None:
                            take(g - 1)

                def tail(prev):
                    low(prev[0], prev[1], HC - 1)
                    take(NG - 1)
                run(dve, step, tail)


NH, HD = 16, 16


def retention(nc, sems, X, ident, power, A):
    SCALE = 256.0
    QK = 16.0
    with ExitStack() as scope:
        c = Core(nc, scope, sems, "r_")
        W = {n: [c.sb(f"w{n}{t}", [P, DC, D], f16) for t in range(2)] for n in ("Q", "Qs", "K", "Ks", "V", "g", "o")}
        split_weights(nc, sems, [(A[f"L0_xattn_W{n}"].rearrange("p a b -> p (a b)"),
                                  W[n][0][:, :, :].rearrange("p a b -> p (a b)"),
                                  W[n][1][:, :, :].rearrange("p a b -> p (a b)"), SCALE) for n in W], "rw_")
        pA, pB = (c.ps(n, [P, 2, 512]) for n in ("pA", "pB"))
        pS = c.ps("pS", [P, 4, 2, 2, S])
        names = ("q_projected qs_projected k_projected ks_projected v_projected gate_projected q1 q2 qr qm k1 k2 kT "
                 "vh vl gz gate scored masked simh siml retained mu_sum mu centred squared var_sum var sd rstd "
                 "normed gated gated_turned gh gl out_projected bias_added x_done ctx_in ctx_h ctx_l tables_in").split()
        s = {n: c.sem(n + "_done") for n in names}
        fr = Front(c, X, ident, power, pB, (s["gate_projected"], 1))
        cf = c.sb("ctx", [P, DC, GT])
        ch, cl = (c.sb(n, [P, DC, GT], f16) for n in ("ch", "cl"))
        tab = {n: c.sb(n, [P, S]) for n in ("cos_q", "sin_q", "cos_k", "sin_k")}
        odd = c.sb("odd", [P, 2])
        decay = c.sb("decay", [P, 4, 2, 2, S])
        gb, ob = c.sb("gb", [P, D]), c.sb("ob", [P, D])
        a1, a2 = (c.sb(n, [P, DC, GT]) for n in ("a1", "a2"))
        qr, kT = (c.sb(n, [P, DC, GT]) for n in ("qr", "kT"))
        qm = c.sb("qm", [P, 2, DC, GT])
        vh, vl = (c.sb(n, [P, GB, D], f16) for n in ("vh", "vl"))
        gz, gate = (c.sb(n, [P, GB, D]) for n in ("gz", "gate"))
        sim = c.sb("sim", [P, 4, 2, 2, S])
        simh, siml = (c.sb(n, [P, 4, 2, 2, S], f16) for n in ("simh", "siml"))
        rc = c.sb("rc", [P, GB * NH, HD])
        sq = c.sb("sq", [P, GB * NH, HD])
        musum, mu, varsum, var, sd, rstd = (c.sb(n, [P, GB * NH]) for n in ("musum", "mu", "varsum", "var", "sd", "rstd"))
        gh, gl = (c.sb(n, [P, DC, GT], f16) for n in ("gh", "gl"))
        pAr = pA[:, :, :].rearrange("p a (b t) -> p (a b) t", t=HD)
        pA4 = pA[:, :, :].rearrange("p a (b t) -> p (a b) t", t=D)
        pB4 = pB[:, :, :].rearrange("p a (b t) -> p (a b) t", t=D)
        pA8 = pA[:, :, :].rearrange("p a (b t) -> p (a b) t", t=S)
        pB8 = pB[:, :, :].rearrange("p a (b t) -> p (a b) t", t=S)

        def eight(t):
            return t[:, :, :].rearrange("p a (b t) -> p (a b) t", t=S)

        def wide(t):
            return t[:, :, :, :, :].rearrange("p r c v t -> p (r c v t)")

        def loop(eng, main):
            main(0, True, 1)
            with eng.Fori(1, NG - 1) as g:
                main(g, False, g + 1)
            main(NG - 1, False, None)

        with nc.Block() as block:
            @block.sync
            def _(sp):
                sp.dma_start(cf[:, :, :], A["ctxT"][:, :, 0:GT]).then_inc(s["ctx_in"], 16)
                for t, n in [(tab[n][:, :], n) for n in tab] + [(odd[:, :], "odd"), (wide(decay), "decay")]:
                    sp.dma_start(t, A[n]).then_inc(s["tables_in"], 16)
                for t, n in ((gb, "L0_xattn_g_b"), (ob, "L0_xattn_out_b")):
                    sp.dma_start(t[:, :], A[n].partition_broadcast(P)).then_inc(s["tables_in"], 16)
                with sp.Fori(1, NG) as g:
                    sp.wait_ge(s["ctx_l"], g)
                    sp.dma_start(cf[:, :, :], A["ctxT"][:, :, bass.ds(g * GT, GT)]).then_inc(s["ctx_in"], 16)

            @block.tensor
            def _(pe):
                def scores(g, b, first):
                    if b > 0 or not first:
                        pe.wait_ge(s["masked"], g * GB + b)
                    t = slice(b * S, (b + 1) * S)
                    for dc in range(DC):
                        for r in range(4):
                            rows = slice(32 * r, 32 * r + 32)
                            last = pe.matmul(pS[:, r, dc, :, :], kT[rows, dc, t], qm[rows, :, dc, t], start=True, stop=True)
                    last.then_inc(s["scored"], 1)

                def retain(g, b):
                    pe.wait_ge(s["siml"], g * GB + b + 1)
                    for h in range(NH):
                        dc, r, v = h // 8, h % 8 // 2, h % 2
                        for n, (x, y) in enumerate(TERMS):
                            last = pe.matmul(pA4[:, b, h * HD:(h + 1) * HD], (simh, siml)[x][:, r, dc, v, :],
                                             (vh, vl)[y][:, b, h * HD:(h + 1) * HD], start=(n == 0), stop=(n == 2))
                    last.then_inc(s["retained"], 1)

                def main(g, first, nxt):
                    pe.wait_ge(fr.xl_done, g + 1)
                    pe.wait_ge(s["ctx_l"], g + 1)
                    x, ctx = (fr.xh, fr.xl), (ch, cl)
                    for n, ps, m, done, free in (("Q", pA, x, "q_projected", ("x_done", 0, 0)),
                                                 ("Qs", pB, x, "qs_projected", None),
                                                 ("K", pA, ctx, "k_projected", ("q1", 1, 1)),
                                                 ("Ks", pB, ctx, "ks_projected", ("q2", 1, 1))):
                        if free is not None and (free[2] or not first):
                            pe.wait_ge(s[free[0]], g + free[2])
                        for a in range(DC):
                            last = project_features(pe, ps[:, a, :], W[n], slice(a * P, (a + 1) * P), m)
                        last.then_inc(s[done], 1)
                    pe.wait_ge(s["k1"], g + 1)
                    for b in range(GB):
                        last = project_tokens(pe, pA4[:, b, :], W["V"], slice(0, D), ctx, slice(b * S, (b + 1) * S))
                    last.then_inc(s["v_projected"], 1)
                    pe.wait_ge(s["k2"], g + 1)
                    for b in range(GB):
                        last = project_tokens(pe, pB4[:, b, :], W["g"], slice(0, D), x, slice(b * S, (b + 1) * S))
                    last.then_inc(s["gate_projected"], 1)
                    pe.wait_ge(s["kT"], g + 1)
                    pe.wait_ge(s["qm"], 2 * g + 2)
                    scores(g, 0, first)
                    pe.wait_ge(s["vl"], g + 1)
                    for b in range(1, GB):
                        scores(g, b, first)
                        retain(g, b - 1)
                    if nxt is not None:
                        pe.wait_ge(s["gz"], g + 1)
                        fr.transpose(pe, nxt)
                    retain(g, GB - 1)
                    pe.wait_ge(s["gated"], g + 1)
                    if nxt is not None:
                        pe.wait_ge(fr.xl_done, nxt + 1)
                    for dc in range(DC):
                        for b in range(GB):
                            last = pe.transpose(pB[:, dc, b * S:(b + 1) * S], gate[:, b, dc * P:(dc + 1) * P], ident[:, :])
                    last.then_inc(s["gated_turned"], 1)
                    pe.wait_ge(s["gl"], g + 1)
                    pe.wait_ge(s["centred"], g + 1)
                    for b in range(GB):
                        last = project_tokens(pe, pA4[:, b, :], W["o"], slice(0, D), (gh, gl), slice(b * S, (b + 1) * S))
                    last.then_inc(s["out_projected"], 1)

                fr.transpose(pe, 0)
                loop(pe, main)

            @block.vector
            def _(dve):
                def mask(g, b):
                    dve.wait_ge(s["scored"], g * GB + b + 1)
                    if not (b == 0 and starts(g, 0)):
                        dve.wait_ge(s["siml"], g * GB + b)
                    dve.tensor_tensor(wide(sim), wide(pS), wide(decay), ALU.mult).then_inc(s["masked"], 1)

                def context_low(g):
                    dve.wait_ge(s["ctx_h"], g + 1)
                    dve.tensor_tensor(cl[:, :, :], cf[:, :, :], ch[:, :, :], ALU.subtract).then_inc(s["ctx_l"], 1)

                def main(g, first, nxt):
                    dve.wait_ge(s["q_projected"], g + 1)
                    if not first:
                        dve.wait_ge(s["kT"], g)
                    dve.tensor_tensor(eight(a1), pA8, repeat(tab["cos_q"][:, :], 8), ALU.mult).then_inc(s["q1"], 1)
                    dve.wait_ge(s["qs_projected"], g + 1)
                    dve.tensor_tensor(eight(a2), pB8, repeat(tab["sin_q"][:, :], 8), ALU.mult).then_inc(s["q2"], 1)
                    dve.wait_ge(s["q1"], g + 1)
                    dve.wait_ge(s["q2"], g + 1)
                    if not first:
                        dve.wait_ge(s["qm"], 2 * g)
                    dve.tensor_tensor(qr[:, :, :], a1[:, :, :], a2[:, :, :], ALU.add).then_inc(s["qr"], 1)
                    dve.wait_ge(s["qr"], g + 1)
                    dve.wait_ge(s["k_projected"], g + 1)
                    dve.tensor_tensor(eight(a1), pA8, repeat(tab["cos_k"][:, :], 8), ALU.mult).then_inc(s["k1"], 1)
                    dve.wait_ge(s["ks_projected"], g + 1)
                    dve.tensor_tensor(eight(a2), pB8, repeat(tab["sin_k"][:, :], 8), ALU.mult).then_inc(s["k2"], 1)
                    dve.wait_ge(s["vh"], g + 1)
                    dve.tensor_tensor(vl[:, :, :], pA4, vh[:, :, :], ALU.subtract).then_inc(s["vl"], 1)
                    dve.wait_ge(s["gate_projected"], g + 1)
                    dve.scalar_tensor_tensor(gz[:, :, :], pB4, 1.0 / SCALE, repeat(gb[:, :], GB), ALU.mult, ALU.add)\
                       .then_inc(s["gz"], 1)
                    mask(g, 0)
                    if nxt is not None:
                        fr.stats(dve, nxt)
                        context_low(nxt)
                    mask(g, 1)
                    if nxt is not None:
                        fr.norm(dve, nxt)
                    mask(g, 2)
                    mask(g, 3)
                    if nxt is not None:
                        fr.low(dve, nxt)
                    dve.wait_ge(s["retained"], g * GB + GB)
                    dve.tensor_reduce(musum[:, :], pAr, AX, ALU.add).then_inc(s["mu_sum"], 1)
                    dve.wait_ge(s["mu_sum"], g + 1)
                    dve.tensor_scalar(mu[:, :], musum[:, :], 1.0 / HD, None, ALU.mult).then_inc(s["mu"], 1)
                    dve.wait_ge(s["mu"], g + 1)
                    dve.tensor_tensor(rc[:, :, :], pAr, spread(mu[:, :], HD), ALU.subtract).then_inc(s["centred"], 1)
                    dve.wait_ge(s["squared"], g + 1)
                    dve.tensor_reduce(varsum[:, :], sq[:, :, :], AX, ALU.add).then_inc(s["var_sum"], 1)
                    dve.wait_ge(s["var_sum"], g + 1)
                    RET = QK * QK * SCALE
                    dve.tensor_scalar(var[:, :], varsum[:, :], 1.0 / HD, LN_EPS * RET * RET, ALU.mult, ALU.add)\
                       .then_inc(s["var"], 1)
                    dve.wait_ge(s["sd"], g + 1)
                    dve.reciprocal(rstd[:, :], sd[:, :]).then_inc(s["rstd"], 1)
                    dve.wait_ge(s["normed"], g + 1)
                    dve.wait_ge(s["gate"], g + 1)
                    dve.tensor_tensor(gate[:, :, :].rearrange("p b d -> p (b d)"), sq[:, :, :].rearrange("p b d -> p (b d)"),
                                      gate[:, :, :].rearrange("p b d -> p (b d)"), ALU.mult).then_inc(s["gated"], 1)
                    dve.wait_ge(s["gh"], g + 1)
                    dve.tensor_tensor(gl[:, :, :], pB[:, :, :], gh[:, :, :], ALU.subtract).then_inc(s["gl"], 1)
                    dve.wait_ge(s["out_projected"], g + 1)
                    dve.wait_ge(s["bias_added"], g + 1)
                    rows = X[:, bass.ds(g * GB, GB), :]
                    dve.scalar_tensor_tensor(rows, pA4, 1.0 / SCALE, rows, ALU.mult, ALU.add).then_inc(s["x_done"], 1)

                dve.wait_ge(s["tables_in"], 16 * 8)
                fr.stats(dve, 0)
                fr.norm(dve, 0, first=True)
                context_low(0)
                fr.low(dve, 0)
                loop(dve, main)

            @block.scalar
            def _(act):
                def context_high(g):
                    act.wait_ge(s["ctx_in"], g * 16 + 16)
                    if not starts(g, 0):
                        act.wait_ge(s["v_projected"], g)
                    act.activation(ch[:, :, :], cf[:, :, :], ACT.Copy).then_inc(s["ctx_h"], 1)

                def sim_high(g, b):
                    act.wait_ge(s["masked"], g * GB + b + 1)
                    if not (b == 0 and starts(g, 0)):
                        act.wait_ge(s["retained"], g * GB + b)
                    act.activation(wide(simh), wide(sim), ACT.Copy).then_inc(s["simh"], 1)

                def main(g, first, nxt):
                    act.wait_ge(s["qr"], g + 1)
                    if not first:
                        act.wait_ge(s["scored"], g * GB)
                    for v in range(2):
                        act.activation(qm[:, v, :, :], qr[:, :, :], ACT.Copy, scale=odd[:, v:v + 1]).then_inc(s["qm"], 1)
                    act.wait_ge(s["v_projected"], g + 1)
                    act.activation(vh[:, :, :], pA4, ACT.Copy).then_inc(s["vh"], 1)
                    act.wait_ge(s["gz"], g + 1)
                    if not first:
                        act.wait_ge(s["gated_turned"], g)
                    act.activation(gate[:, :, :], gz[:, :, :], ACT.Silu).then_inc(s["gate"], 1)
                    sim_high(g, 0)
                    if nxt is not None:
                        context_high(nxt)
                    for b in range(1, GB):
                        sim_high(g, b)
                    if nxt is not None:
                        fr.high(act, nxt)
                    act.wait_ge(s["centred"], g + 1)
                    act.activation(sq[:, :, :], rc[:, :, :], ACT.Square).then_inc(s["squared"], 1)
                    act.wait_ge(s["var"], g + 1)
                    act.activation(sd[:, :], var[:, :], ACT.Sqrt).then_inc(s["sd"], 1)
                    act.wait_ge(s["gated_turned"], g + 1)
                    act.activation(gh[:, :, :], pB[:, :, :], ACT.Copy).then_inc(s["gh"], 1)

                act.wait_ge(s["tables_in"], 16 * 8)
                context_high(0)
                fr.high(act, 0, first=True)
                loop(act, main)

            @block.gpsimd
            def _(pool):
                def main(g, first, nxt):
                    pool.wait_ge(s["k1"], g + 1)
                    pool.wait_ge(s["k2"], g + 1)
                    if not first:
                        pool.wait_ge(s["scored"], g * GB)
                    pool.tensor_tensor(kT[:, :, :], a1[:, :, :], a2[:, :, :], ALU.add).then_inc(s["kT"], 1)
                    pool.wait_ge(fr.xn_done, g * GB + GB)
                    rows = X[:, bass.ds(g * GB, GB), :]
                    pool.tensor_tensor(rows, rows, repeat(ob[:, :], GB), ALU.add).then_inc(s["bias_added"], 1)
                    if nxt is not None:
                        fr.power_of_var(pool, nxt)
                    for b in range(GB):
                        pool.wait_ge(s["simh"], g * GB + b + 1)
                        pool.tensor_tensor(wide(siml), wide(sim), wide(simh), ALU.subtract).then_inc(s["siml"], 1)
                    pool.wait_ge(s["rstd"], g + 1)
                    RET = QK * QK * SCALE
                    pool.tensor_tensor(sq[:, :, :], rc[:, :, :], spread(rstd[:, :], HD), ALU.mult).then_inc(s["normed"], 1)

                pool.wait_ge(s["tables_in"], 16 * 8)
                fr.power_of_var(pool, 0)
                loop(pool, main)


def shape_tables():
    import numpy as np
    f = np.float32
    half = HD // 2
    base = (np.arange(0, HD, 2, dtype=f) + f(0.4 * HD)) / f(1.4 * HD)
    powers = (np.arange(-(S // 2), S - S // 2, dtype=f) / f(512.0))[:, None]
    scale = base[None, :] ** powers
    inv = (1.0 / 10000.0 ** (np.arange(half, dtype=f) / half)).astype(f)
    ang = np.arange(S, dtype=f)[:, None] * inv[None, :]
    sin, cos = np.sin(ang), np.cos(ang)
    sign = np.where(np.arange(HD) % 2 == 0, -1.0, 1.0).astype(f)[:, None]

    def feature_rows(t, factor):
        return np.tile(np.repeat(t, 2, axis=1).T * f(factor), (8, 1)).astype(f)

    down = 16.0 / 256.0
    d = {"cos_q": feature_rows(cos * scale, down), "sin_q": feature_rows(sin * scale, down) * np.tile(sign, (8, 1)),
         "cos_k": feature_rows(cos / scale, down), "sin_k": feature_rows(sin / scale, down) * np.tile(sign, (8, 1))}
    gammas = 1.0 - np.exp(np.linspace(np.log(1.0 / 32.0), np.log(1.0 / 512.0), NH)).astype(f)
    dist = np.arange(S)[None, :] - np.arange(S)[:, None]
    m = np.where(dist[None] >= 0, gammas[:, None, None].astype(f) ** np.maximum(dist, 0)[None].astype(f), 0.0).astype(f)
    d["decay"] = np.ascontiguousarray(m.reshape(2, 4, 2, S, S).transpose(3, 1, 0, 2, 4)).reshape(P, -1)
    rows = (np.arange(P) // HD) % 2
    d["odd"] = np.stack([rows == 0, rows == 1], axis=1).astype(f)
    return {n: np.ascontiguousarray(v) for n, v in d.items()}


LD, CODES = 64, 64


def lie_rotation(nc, sems, X, ident, power, A):
    SCALE = 16.0
    with ExitStack() as scope:
        c = Core(nc, scope, sems, "l_")
        XN = c.sb("XN", [P, B, D])
        hT = [c.sb(f"hT{t}", [P, B * S], f16) for t in range(2)]
        pb = [c.sb(f"pb{t}", [P, B, D], f16) for t in range(2)]
        nw = c.sb("nw", [P, D])
        hm = c.sb("hm", [P, DC, B])
        mix = c.sb("mix", [P, 2])
        ones = c.sb("ones", [P, 1])
        consts_in = c.sem("consts_in")

        with ExitStack() as inner:
            r = Core(nc, inner, sems, "lf_")
            rs, rstd = RowStats(r), r.sb("rstd", [P, GB])
            xn = r.sb("xn", [P, 2, GB, D])
            pT = r.ps("pT", [P, 2, GB * S])
            pM = r.ps("pM", [P, DC, B])
            names = "rstd xn xn_kept meant turned high low ones".split()
            s = {n: r.sem(n + "_done") for n in names}
            with nc.Block() as block:
                @block.sync
                def _(sp):
                    sp.dma_start(nw[:, :], A["L1_attn_norm_w"].partition_broadcast(P)).then_inc(consts_in, 16)
                    sp.dma_start(mix[:, 0:1], A["L1_attn_omega_mix"].partition_broadcast(P)).then_inc(consts_in, 16)
                    sp.dma_start(mix[:, 1:2], A["L1_attn_vq_mix"].partition_broadcast(P)).then_inc(consts_in, 16)
                    sp.wait_ge(consts_in, 48)

                @block.vector
                def _(dve):
                    dve.memset(ones[:, :], 1.0 / S).then_inc(s["ones"], 1)
                    dve.memset(hT[0][LD:LD + 1, :], 1.0).then_inc(s["ones"], 1)
                    dve.memset(hT[1][LD:LD + 1, :], 0.0).then_inc(s["ones"], 1)

                    def group(g, u, early):
                        rs.run(dve, X, g)
                        dve.wait_ge(s["rstd"], g + 1)
                        if not early:
                            dve.wait_ge(s["turned"], g - 1)
                            dve.wait_ge(s["xn_kept"], g - 1)
                        for b in range(GB):
                            dve.tensor_scalar(xn[:, u, b, :], X[:, g * GB + b, :], rs.mean[:, b:b + 1], rstd[:, b:b + 1],
                                              ALU.subtract, ALU.mult).then_inc(s["xn"], 1)
                        dve.wait_ge(s["high"], g + 1)
                        dve.tensor_tensor(hT[1][0:LD, bass.ds(g * GT, GT)], pT[0:LD, u, :],
                                          hT[0][0:LD, bass.ds(g * GT, GT)], ALU.subtract).then_inc(s["low"], 1)
                    group(0, 0, True)
                    group(1, 1, True)
                    with dve.Fori(2, NG - 1, 2) as g:
                        group(g, 0, False)
                        group(g + 1, 1, False)

                @block.gpsimd
                def _(pool):
                    with pool.Fori(0, NG) as g:
                        pool.wait_ge(rs.ve_done, g + 1)
                        pool.tensor_tensor(rstd[:, :], rs.ve[:, :], power[:, 0:GB], ALU.pow).then_inc(s["rstd"], 1)

                @block.tensor
                def _(pe):
                    pe.wait_ge(s["ones"], 3)

                    def group(g, u, early):
                        pe.wait_ge(s["xn"], g * GB + GB)
                        if not early:
                            pe.wait_ge(s["low"], g - 1)
                        for b in range(GB):
                            for dc in range(DC):
                                pe.matmul(pM[:, dc, bass.ds(g * GB + b, 1)], xn[:, u, b, dc * P:(dc + 1) * P],
                                          ones[:, :], start=True, stop=True)
                        for b in range(GB):
                            last = pe.transpose(pT[0:LD, u, b * S:(b + 1) * S], xn[:, u, b, 0:LD], ident[:, :])
                        last.then_inc(s["turned"], 1)
                    group(0, 0, True)
                    group(1, 1, True)
                    with pe.Fori(2, NG - 1, 2) as g:
                        group(g, 0, False)
                        group(g + 1, 1, False)

                @block.scalar
                def _(act):
                    def group(g, u):
                        act.wait_ge(s["turned"], g + 1)
                        act.activation(hT[0][0:LD, bass.ds(g * GT, GT)], pT[0:LD, u, :], ACT.Copy).then_inc(s["high"], 1)
                        act.activation(XN[:, bass.ds(g * GB, GB), :], xn[:, u, :, :], ACT.Copy).then_inc(s["xn_kept"], 1)
                    with act.Fori(0, NG - 1, 2) as g:
                        group(g, 0)
                        group(g + 1, 1)
                    act.wait_ge(s["turned"], NG)
                    act.activation(hm[:, :, :], pM[:, :, :], ACT.Copy).then_inc(s["meant"], 1)

        with ExitStack() as inner:
            r = Core(nc, inner, sems, "lo_")
            Wp = r.sb("Wp", [P, DC, LD, LD])
            bp, sign = r.sb("bp", [LD, LD]), r.sb("sign", [LD, LD])
            Wvi, Wvo, Woo = r.sb("Wvi", [P, DC, LD]), r.sb("Wvo", [LD, D]), r.sb("Woo", [LD, D])
            bvi, bvo, boo = r.sb("bvi", [B, LD]), r.sb("bvo", [B, D]), r.sb("boo", [B, D])
            code, behind = r.sb("code", [CODES, LD]), r.sb("behind", [B, CODES])
            om0, om, m2, GT_ = (r.sb(n, [LD, B, LD]) for n in ("om0", "om", "m2", "GT"))
            g1, g2 = om0, m2
            pf = Wp[:, :, :, :].rearrange("p a i j -> p (a i j)").rearrange("p (b d) -> p b d", d=D)
            shift = r.sb("shift", [B, D])
            p1, p2 = r.ps("p1", [P, 2048]), r.ps("p2", [P, 2048])
            w_in = r.sem("w_in")
            shift_in, split_high, split_low = r.sem("shift_in"), r.sem("split_high"), r.sem("split_low")
            d_, t_, a_ = r.sem("vector_step"), r.sem("tensor_step"), r.sem("pool_step")
            half = r.sb("half", [P, 1])
            sm = {n: r.sb(n, sh) for n, sh in (("vq", [B, LD]), ("vsq", [B, LD]), ("vss", [B, 1]), ("vn0", [B, 1]),
                                              ("vn1", [B, 1]), ("vn2", [B, 1]), ("vnorm", [B, LD]),
                                              ("csq", [CODES, LD]), ("css", [CODES, 1]), ("cn0", [CODES, 1]),
                                              ("cn1", [CODES, 1]), ("cn2", [CODES, 1]), ("cnorm", [CODES, LD]),
                                              ("vT", [LD, B]), ("cT", [LD, CODES]), ("sc", [B, CODES]), ("top", [B, 1]),
                                              ("eq", [B, CODES]), ("val", [B, CODES]), ("best", [B, 1]),
                                              ("hot", [B, CODES]), ("hotT", [CODES, B]), ("dif", [B, LD]),
                                              ("vqo", [B, LD]), ("vqoT", [LD, B]), ("sh1", [B, D]), ("sh2", [B, D]),
                                              ("bo2", [B, D]))}
            with nc.Block() as block:
                loads = ((bp, "L1_attn_omega_b"), (sign, "sign"), (Wvi, "L1_attn_Wvi"), (Wvo, "L1_attn_Wvo"),
                         (Woo, "L1_attn_Woo"), (code, "L1_attn_codebook"), (behind, "behind"))

                @block.sync
                def _(sp):
                    for t, n in loads:
                        sp.dma_start(t[:], A[n]).then_inc(w_in, 16)
                    for t, n in ((bvi, "L1_attn_vq_proj_in_b"), (bvo, "L1_attn_vq_proj_out_b"),
                                 (boo, "L1_attn_omega_out_b")):
                        sp.dma_start(t[:, :], A[n].partition_broadcast(B)).then_inc(w_in, 16)
                    sp.dma_start(Wp[:, :, :, :], A["L1_attn_Wp"]).then_inc(w_in, 16)
                    sp.wait_ge(d_, 26)
                    sp.dma_start(pf[LD:LD + 1, :, :], shift[:, :]).then_inc(shift_in, 16)

                @block.tensor
                def _(pe):
                    pe.wait_ge(w_in, 16 * 11)
                    for dc in range(DC):
                        last = pe.matmul(p2[0:B, 0:LD], hm[:, dc, :], Wvi[:, dc, :], start=(dc == 0), stop=(dc == 1))
                    last.then_inc(t_, 1)
                    for j in range(LD):
                        for dc in range(DC):
                            last = pe.matmul(p1[0:LD, j * B:(j + 1) * B], Wp[:, dc, :, j], hm[:, dc, :],
                                             start=(dc == 0), stop=(dc == 1))
                    last.then_inc(t_, 1)
                    pe.wait_ge(d_, 11)
                    pe.transpose(p2[0:LD, 512:512 + B], sm["vnorm"][:, :], ident[0:B, 0:B]).then_inc(t_, 1)
                    pe.transpose(p2[0:LD, 1024:1024 + CODES], sm["cnorm"][:, :], ident[0:CODES, 0:CODES]).then_inc(t_, 1)
                    pe.wait_ge(d_, 13)
                    pe.matmul(p2[0:B, 1536:1536 + CODES], sm["vT"][:, :], sm["cT"][:, :], start=True, stop=True)\
                      .then_inc(t_, 1)
                    pe.wait_ge(d_, 19)
                    pe.transpose(p2[0:CODES, 512:512 + B], sm["hot"][:, :], ident[0:B, 0:B]).then_inc(t_, 1)
                    pe.wait_ge(d_, 20)
                    pe.matmul(p2[0:B, 1024:1024 + LD], sm["hotT"][:, :], code[:, :], start=True, stop=True).then_inc(t_, 1)
                    pe.wait_ge(d_, 22)
                    pe.transpose(p2[0:LD, 512:512 + B], sm["vqo"][:, :], ident[0:B, 0:B]).then_inc(t_, 1)
                    pe.wait_ge(d_, 23)
                    pe.matmul(p2[0:B, 0:D], sm["vqoT"][:, :], Wvo[:, :], start=True, stop=True).then_inc(t_, 1)
                    pe.wait_ge(d_, 28)
                    for b in range(B):
                        last = pe.matmul(p1[0:LD, b * LD:(b + 1) * LD], om[:, b, :], om[:, b, :], start=True, stop=True)
                    last.then_inc(t_, 1)
                    pe.wait_ge(d_, 29)
                    for b in range(B):
                        last = pe.matmul(p2[0:LD, b * LD:(b + 1) * LD], m2[:, b, :], om[:, b, :], start=True, stop=True)
                    last.then_inc(t_, 1)
                    pe.wait_ge(d_, 32)
                    for q in range(B // 8):
                        ps = (p1, p2)[q % 2]
                        if q >= 2:
                            pe.wait_ge(d_, 32 + q - 1)
                        for b in range(8):
                            last = pe.matmul(ps[0:LD, b * D:(b + 1) * D], GT_[:, q * 8 + b, :], Woo[:, :], start=True,
                                             stop=True)
                        last.then_inc(t_, 1)

                @block.gpsimd
                def _(pool):
                    pool.memset(half[:, :], 0.5).then_inc(a_, 1)
                    pool.wait_ge(a_, 1)
                    pool.wait_ge(d_, 5)
                    pool.tensor_tensor(sm["vn0"][:, :], sm["vss"][:, :], half[0:B, :], ALU.pow).then_inc(a_, 1)
                    pool.tensor_tensor(sm["cn0"][:, :], sm["css"][:, :], half[0:CODES, :], ALU.pow).then_inc(a_, 1)

                @block.vector
                def _(dve):
                    n = [0]

                    def step(ins, settle=True):
                        ins.then_inc(d_, 1)
                        n[0] += 1
                        if settle:
                            dve.wait_ge(d_, n[0])

                    def bc(t, m):
                        return t.broadcast_to((t.shape[0], m))
                    v = sm
                    dve.wait_ge(w_in, 16 * 11)
                    dve.wait_ge(t_, 1)
                    step(dve.tensor_tensor(v["vq"][:, :], p2[0:B, 0:LD], bvi[:, :], ALU.add))
                    step(dve.tensor_tensor(v["vsq"][:, :], v["vq"][:, :], v["vq"][:, :], ALU.mult))
                    step(dve.tensor_reduce(v["vss"][:, :], v["vsq"][:, :], AX, ALU.add))
                    step(dve.tensor_tensor(v["csq"][:, :], code[:, :], code[:, :], ALU.mult))
                    step(dve.tensor_reduce(v["css"][:, :], v["csq"][:, :], AX, ALU.add))
                    dve.wait_ge(a_, 3)
                    step(dve.tensor_scalar(v["vn1"][:, :], v["vn0"][:, :], 1e-12, None, ALU.max))
                    step(dve.reciprocal(v["vn2"][:, :], v["vn1"][:, :]))
                    step(dve.tensor_scalar(v["cn1"][:, :], v["cn0"][:, :], 1e-12, None, ALU.max))
                    step(dve.reciprocal(v["cn2"][:, :], v["cn1"][:, :]))
                    step(dve.tensor_scalar(v["vnorm"][:, :], v["vq"][:, :], v["vn2"][:, 0:1], None, ALU.mult))
                    step(dve.tensor_scalar(v["cnorm"][:, :], code[:, :], v["cn2"][:, 0:1], None, ALU.mult))
                    dve.wait_ge(t_, 4)
                    step(dve.tensor_copy(v["vT"][:, :], p2[0:LD, 512:512 + B]))
                    step(dve.tensor_copy(v["cT"][:, :], p2[0:LD, 1024:1024 + CODES]))
                    dve.wait_ge(t_, 5)
                    step(dve.tensor_copy(v["sc"][:, :], p2[0:B, 1536:1536 + CODES]))
                    step(dve.tensor_reduce(v["top"][:, :], v["sc"][:, :], AX, ALU.max))
                    step(dve.tensor_tensor(v["eq"][:, :], v["sc"][:, :], bc(v["top"][:, :], CODES), ALU.is_equal))
                    step(dve.tensor_tensor(v["val"][:, :], v["eq"][:, :], behind[:, :], ALU.mult))
                    step(dve.tensor_reduce(v["best"][:, :], v["val"][:, :], AX, ALU.max))
                    step(dve.tensor_tensor(v["hot"][:, :], v["val"][:, :], bc(v["best"][:, :], CODES), ALU.is_equal))
                    dve.wait_ge(t_, 6)
                    step(dve.tensor_copy(v["hotT"][:, :], p2[0:CODES, 512:512 + B]))
                    dve.wait_ge(t_, 7)
                    step(dve.tensor_tensor(v["dif"][:, :], p2[0:B, 1024:1024 + LD], v["vq"][:, :], ALU.subtract))
                    step(dve.tensor_tensor(v["vqo"][:, :], v["vq"][:, :], v["dif"][:, :], ALU.add))
                    dve.wait_ge(t_, 8)
                    step(dve.tensor_copy(v["vqoT"][:, :], p2[0:LD, 512:512 + B]))
                    dve.wait_ge(t_, 9)
                    step(dve.tensor_tensor(v["sh1"][:, :], p2[0:B, 0:D], bvo[:, :], ALU.add))
                    step(dve.tensor_scalar(v["bo2"][:, :], boo[:, :], mix[0:B, 0:1], None, ALU.mult))
                    step(dve.scalar_tensor_tensor(shift[:, :], v["sh1"][:, :], mix[0:B, 1:2], v["bo2"][:, :],
                                                  ALU.mult, ALU.add))
                    step(dve.tensor_tensor(om0[:, :, :].rearrange("p b j -> p j b"),
                                           p1[0:LD, :].rearrange("p (j b) -> p j b", b=B), spread(bp[:, :], B), ALU.add))
                    step(dve.tensor_tensor(om[:, :, :], om0[:, :, :], repeat(sign[:, :], B), ALU.mult))
                    dve.wait_ge(t_, 10)
                    step(dve.tensor_copy(m2[:, :, :].rearrange("p b j -> p (b j)"), p1[0:LD, :]))
                    step(dve.scalar_tensor_tensor(g1[:, :, :], m2[:, :, :], -0.5, om[:, :, :], ALU.mult, ALU.subtract))
                    dve.wait_ge(t_, 11)
                    step(dve.scalar_tensor_tensor(g2[:, :, :].rearrange("p b j -> p (b j)"), p2[0:LD, :], 1.0 / 6.0,
                                                  g1[:, :, :].rearrange("p b j -> p (b j)"), ALU.mult, ALU.add))
                    step(dve.tensor_tensor(GT_[:, :, :], g2[:, :, :], repeat(ident[0:LD, 0:LD], B), ALU.add))
                    for q in range(B // 8):
                        dve.wait_ge(t_, 12 + q)
                        ps = (p1, p2)[q % 2]
                        step(dve.tensor_scalar(pf[0:LD, q * 8:(q + 1) * 8, :].rearrange("p b d -> p (b d)"), ps[0:LD, :],
                                               mix[0:LD, 0:1], None, ALU.mult))
                    dve.wait_ge(split_high, 1)
                    dve.scalar_tensor_tensor(pb[1][0:LD + 1, :, :], pf[0:LD + 1, :, :], SCALE, pb[0][0:LD + 1, :, :],
                                             ALU.mult, ALU.subtract).then_inc(split_low, 1)

                @block.scalar
                def _(act):
                    act.wait_ge(shift_in, 16)
                    act.wait_ge(d_, 36)
                    act.activation(pb[0][0:LD + 1, :, :], pf[0:LD + 1, :, :], ACT.Copy, scale=SCALE).then_inc(split_high, 1)

        with ExitStack() as inner:
            r = Core(nc, inner, sems, "ly_")
            pY = [r.ps(f"pY{i}", [P, GB, D]) for i in range(2)]
            y, sq, z = (r.sb(n, [P, 2, GB, D]) for n in ("y", "sq", "z"))
            ss, me, rr = (r.sb(n, [P, 2, GB]) for n in ("ss", "me", "rr"))
            eps, nw16 = r.sb("eps", [P, GB]), r.sb("nw16", [P, D])
            eps_made, nw_made = r.sem("eps_made"), r.sem("nw_made")
            names = "rotated y squared ss me rr z x".split()
            s = {n: r.sem(n + "_done") for n in names}
            with nc.Block() as block:
                def twos(eng, group):
                    group(0, 0, True)
                    group(1, 1, True)
                    with eng.Fori(2, NG - 1, 2) as g:
                        group(g, 0, False)
                        group(g + 1, 1, False)

                @block.tensor
                def _(pe):
                    def group(g, u, early):
                        if not early:
                            pe.wait_ge(s["y"], g - 1)
                        for b in range(GB):
                            for n, (x, w) in enumerate(TERMS):
                                last = pe.matmul(pY[u][:, b, :], hT[x][0:LD + 1, bass.ds((g * GB + b) * S, S)],
                                                 pb[w][0:LD + 1, g * GB + b, :], start=(n == 0), stop=(n == 2))
                        last.then_inc(s["rotated"], 1)
                    twos(pe, group)

                @block.vector
                def _(dve):
                    def take(g, u, early):
                        dve.wait_ge(s["rotated"], g + 1)
                        if not early:
                            dve.wait_ge(s["z"], (g - 1) * GB)
                            dve.wait_ge(s["squared"], (g - 1) * GB)
                        dve.scalar_tensor_tensor(y[:, u, :, :], pY[u][:, :, :], 1.0 / SCALE, XN[:, bass.ds(g * GB, GB), :],
                                                 ALU.mult, ALU.add).then_inc(s["y"], 1)

                    def finish(g, u, early):
                        dve.wait_ge(s["rr"], g + 1)
                        if not early:
                            dve.wait_ge(s["x"], g - 1)
                        for b in range(GB):
                            dve.scalar_tensor_tensor(z[:, u, b, :], y[:, u, b, :], rr[:, u, b:b + 1], nw16[:, :], ALU.mult,
                                                     ALU.mult).then_inc(s["z"], 1)

                    dve.tensor_scalar(nw16[:, :], nw[:, :], float(D) ** 0.5, None, ALU.mult).then_inc(nw_made, 1)
                    dve.wait_ge(nw_made, 1)
                    take(0, 0, True)
                    take(1, 1, True)
                    finish(0, 0, True)
                    take(2, 0, False)
                    finish(1, 1, True)
                    with dve.Fori(2, NG - 2, 2) as g:
                        take(g + 1, 1, False)
                        finish(g, 0, False)
                        take(g + 2, 0, False)
                        finish(g + 1, 1, False)
                    take(NG - 1, 1, False)
                    finish(NG - 2, 0, False)
                    finish(NG - 1, 1, False)

                @block.scalar
                def _(act):
                    def group(g, u, early):
                        act.wait_ge(s["y"], g + 1)
                        if not early:
                            act.wait_ge(s["me"], g - 1)
                        for b in range(GB):
                            act.activation(sq[:, u, b, :], y[:, u, b, :], ACT.Square, accum_out=ss[:, u, b:b + 1])\
                               .then_inc(s["squared"], 1)
                    twos(act, group)

                @block.gpsimd
                def _(pool):
                    pool.memset(eps[:, :], D * 1e-6).then_inc(eps_made, 1)
                    pool.wait_ge(eps_made, 1)

                    def group(g, u, early):
                        pool.wait_ge(s["squared"], g * GB + GB)
                        pool.tensor_tensor(me[:, u, :], ss[:, u, :], eps[:, :], ALU.add).then_inc(s["me"], 1)
                        pool.wait_ge(s["me"], g + 1)
                        if not early:
                            pool.wait_ge(s["z"], (g - 1) * GB)
                        pool.tensor_tensor(rr[:, u, :], me[:, u, :], power[:, 0:GB], ALU.pow).then_inc(s["rr"], 1)
                        pool.wait_ge(s["z"], g * GB + GB)
                        rows = X[:, bass.ds(g * GB, GB), :]
                        pool.tensor_tensor(rows, rows, z[:, u, :, :], ALU.add).then_inc(s["x"], 1)
                    twos(pool, group)


def one_key_attention(nc, sems, X, ident, power, A):
    SCALE = 256.0
    SL = P // HD
    with ExitStack() as scope:
        c = Core(nc, scope, sems, "q_")
        Wq = [c.sb(f"wq{t}", [P, DC, D], f16) for t in range(2)]
        Wk = [c.sb(f"wk{t}", [P, DC, P], f16) for t in range(2)]
        Wv = [c.sb(f"wv{t}", [P, DC, HD], f16) for t in range(2)]

        def flat(t):
            return t.rearrange("p a b -> p (a b)")
        split_weights(nc, sems, [(flat(A[f"L1_xattn_{n}"]), flat(w[0][:]), flat(w[1][:]), SCALE)
                                 for n, w in (("Wq", Wq), ("Wk", Wk), ("Wv", Wv))], "qw_")
        pA = c.ps("pA", [P, 2, 512])
        pS = [c.ps(f"pS{i}", [P, SL, S]) for i in range(2)]
        pT = c.ps("pT", [P, SL, S])
        names = ("q_projected k_projected v_projected q qh ql k kh kl km kml v vh vl scored mx sub exp turned ph pl "
                 "weighed rec out x_done ctx_in ctx_h ctx_l tables_in ones").split()
        s = {n: c.sem(n + "_done") for n in names}
        fr = Front(c, X, ident, power, pT[:, :, :].rearrange("p (a b) t -> p a (b t)", a=2), (s["q_projected"], 1))
        cf = c.sb("ctx", [P, DC, GT])
        ch, cl = (c.sb(n, [P, DC, GT], f16) for n in ("ch", "cl"))
        bq, bk, bv = c.sb("bq", [P, DC]), c.sb("bk", [P, 1]), c.sb("bv", [P, HD])
        slot = c.sb("slot", [P, SL])
        q = c.sb("q", [P, DC, GT])
        qs = [c.sb(f"qs{t}", [P, DC, GT], f16) for t in range(2)]
        k = c.sb("k", [P, GT])
        ks = [c.sb(f"ks{t}", [P, GT], f16) for t in range(2)]
        km = [c.sb(f"km{t}", [P, SL, GT], f16) for t in range(2)]
        v = c.sb("v", [P, GB, HD + 1])
        vs = [c.sb(f"vs{t}", [P, GB, HD + 1], f16) for t in range(2)]
        mx = c.sb("mx", [P, 2, SL])
        sub = c.sb("sub", [P, 2, SL, S])
        ex = [c.sb(f"ex{i}", [P, SL, S]) for i in range(2)]
        pr = [[c.sb(f"p{t}{i}", [P, S, 2 * SL], f16) for i in range(2)] for t in range(2)]

        def half(part, b, dc):
            return pr[part][b % 2][:, :, dc * SL:(dc + 1) * SL].rearrange("k t c -> k c t")
        rec = c.sb("rec", [P, 2, NH])
        out = c.sb("out", [P, 2, NH, HD])

        def loop(eng, main):
            main(0, True, 1)
            with eng.Fori(1, NG - 1) as g:
                main(g, False, g + 1)
            main(NG - 1, False, None)

        with nc.Block() as block:
            @block.sync
            def _(sp):
                sp.dma_start(cf[:, :, :], A["ctxT"][:, :, 0:GT]).then_inc(s["ctx_in"], 16)
                for t, n in ((bq, "L1_xattn_bq"), (bk, "L1_xattn_bk"), (slot, "slot")):
                    sp.dma_start(t[:, :], A[n]).then_inc(s["tables_in"], 16)
                sp.dma_start(bv[:, :], A["L1_xattn_bv"].partition_broadcast(P)).then_inc(s["tables_in"], 16)
                with sp.Fori(1, NG) as g:
                    sp.wait_ge(s["ctx_l"], g)
                    sp.dma_start(cf[:, :, :], A["ctxT"][:, :, bass.ds(g * GT, GT)]).then_inc(s["ctx_in"], 16)

            @block.tensor
            def _(pe):
                def score(g, b, dc, first):
                    i = (g * GB + b) * 2 + dc
                    if b > 0 or not first:
                        pe.wait_ge(s["sub"], i - 1)
                    t = slice(b * S, (b + 1) * S)
                    for a in range(2):
                        for n, (x, y) in enumerate(TERMS):
                            last = pe.matmul(pS[dc][:, 4 * a:4 * a + 4, :], qs[x][:, dc, t], km[y][:, 4 * a:4 * a + 4, t],
                                             start=(n == 0), stop=(n == 2))
                    last.then_inc(s["scored"], 1)

                def turn(g, b, dc, first):
                    i = (g * GB + b) * 2 + dc
                    pe.wait_ge(s["exp"], i + 1)
                    if b > 0 or dc > 0:
                        pe.wait_ge(s["pl"], i)
                    else:
                        pe.wait_ge(s["k"], g + 1)
                        pe.wait_ge(s["v"], g + 1)
                    for j in range(SL):
                        last = pe.transpose(pT[:, j, :], ex[dc][:, j, :], ident[:, :])
                    last.then_inc(s["turned"], 1)

                def weigh(g, b):
                    pe.wait_ge(s["pl"], (g * GB + b) * 2 + 2)
                    if b < 2:
                        pe.wait_ge(s["q"], 2 * g + 2)
                    else:
                        pe.wait_ge(s["out"], g * GB + b - 1)
                    for h in range(NH):
                        for n, (x, y) in enumerate(TERMS):
                            still = pr[x][b % 2][:, 8 * h:8 * h + 8, :].rearrange("k t c -> k (t c)")
                            last = pe.matmul(pA[:, b % 2, h * (HD + 1):(h + 1) * (HD + 1)], still, vs[y][:, b, :],
                                             start=(n == 0), stop=(n == 2))
                    last.then_inc(s["weighed"], 1)

                def main(g, first, nxt):
                    pe.wait_ge(fr.xl_done, g + 1)
                    pe.wait_ge(s["ctx_l"], g + 1)
                    if not first:
                        pe.wait_ge(s["out"], g * GB)
                        pe.wait_ge(s["pl"], g * GB * 2)
                    for a in range(DC):
                        last = project_features(pe, pA[:, a, :], Wq, slice(a * P, (a + 1) * P), (fr.xh, fr.xl))
                    last.then_inc(s["q_projected"], 1)
                    project_features(pe, pT[:, 0:4, :], Wk, slice(0, P), (ch, cl)).then_inc(s["k_projected"], 1)
                    for b in range(GB):
                        last = project_tokens(pe, pT[:, 4, b * HD:(b + 1) * HD], Wv, slice(0, HD), (ch, cl),
                                              slice(b * S, (b + 1) * S))
                    last.then_inc(s["v_projected"], 1)
                    pe.wait_ge(s["ql"], g + 1)
                    pe.wait_ge(s["km"], (g + 1) * 2 * SL)
                    score(g, 0, 0, first)
                    score(g, 0, 1, first)
                    for b in range(GB):
                        turn(g, b, 0, first)
                        if b + 1 < GB:
                            score(g, b + 1, 0, first)
                        turn(g, b, 1, first)
                        if b == 0:
                            pe.wait_ge(s["vl"], g + 1)
                        if b + 1 < GB:
                            score(g, b + 1, 1, first)
                        if b == 2 and nxt is not None:
                            pe.wait_ge(s["pl"], (g * GB + b) * 2 + 2)
                            fr.transpose(pe, nxt)
                            pe.wait_ge(fr.xl_done, nxt + 1)
                        weigh(g, b)

                fr.transpose(pe, 0)
                loop(pe, main)

            @block.vector
            def _(dve):
                def context_low(g):
                    dve.wait_ge(s["ctx_h"], g + 1)
                    dve.tensor_tensor(cl[:, :, :], cf[:, :, :], ch[:, :, :], ALU.subtract).then_inc(s["ctx_l"], 1)

                def minus_max(g, i, first):
                    n = g * GB * 2 + i
                    u = i % 2
                    dve.wait_ge(s["scored"], n + 1)
                    if i >= 2 or not first:
                        dve.wait_ge(s["sub"], n - 1)
                    dve.tensor_reduce(mx[:, u, :], pS[u][:, :, :], AX, ALU.max).then_inc(s["mx"], 1)
                    dve.wait_ge(s["mx"], n + 1)
                    if i >= 2 or not first:
                        dve.wait_ge(s["exp"], n - 1)
                    dve.tensor_tensor(sub[:, u, :, :], pS[u][:, :, :], spread(mx[:, u, :], S), ALU.subtract)\
                       .then_inc(s["sub"], 1)

                def low(g, i):
                    n = g * GB * 2 + i
                    b, dc = i // 2, i % 2
                    dve.wait_ge(s["ph"], n + 1)
                    dve.tensor_tensor(half(1, b, dc), pT[:, :, :], half(0, b, dc), ALU.subtract).then_inc(s["pl"], 1)

                def finish(g, b, first):
                    n = g * GB + b
                    u = b % 2
                    o = pA[:, u, 0:NH * (HD + 1)].rearrange("p (h e) -> p h e", e=HD + 1)
                    dve.wait_ge(s["weighed"], n + 1)
                    if b >= 2 or not first:
                        dve.wait_ge(s["out"], n - 1)
                    dve.reciprocal(rec[:, u, :], o[:, :, HD]).then_inc(s["rec"], 1)
                    dve.wait_ge(s["rec"], n + 1)
                    if b >= 2 or not first:
                        dve.wait_ge(s["x_done"], n - 1)
                    dve.tensor_tensor(out[:, u, :, :], o[:, :, 0:HD], spread(rec[:, u, :], HD), ALU.mult)\
                       .then_inc(s["out"], 1)

                def main(g, first, nxt):
                    dve.wait_ge(s["q_projected"], g + 1)
                    for a in range(DC):
                        dve.tensor_scalar(q[:, a, :], pA[:, a, :], 1.0 / SCALE, bq[:, a:a + 1], ALU.mult, ALU.add)\
                           .then_inc(s["q"], 1)
                    dve.wait_ge(s["k_projected"], g + 1)
                    dve.tensor_scalar(k[:, :].rearrange("p (a b) -> p a b", a=4), pT[:, 0:4, :], 1.0 / SCALE, bk[:, 0:1],
                                      ALU.mult, ALU.add).then_inc(s["k"], 1)
                    dve.wait_ge(s["v_projected"], g + 1)
                    dve.scalar_tensor_tensor(v[:, :, 0:HD], pT[:, 4, 0:GB * HD].rearrange("p (b e) -> p b e", e=HD),
                                             1.0 / SCALE, repeat(bv[:, :], GB), ALU.mult, ALU.add).then_inc(s["v"], 1)
                    dve.wait_ge(s["kh"], g + 1)
                    dve.tensor_tensor(ks[1][:, :], k[:, :], ks[0][:, :], ALU.subtract).then_inc(s["kl"], 1)
                    dve.wait_ge(s["kl"], g + 1)
                    if not first:
                        dve.wait_ge(s["scored"], g * GB * 2)
                    for t in range(2):
                        for j in range(SL):
                            dve.tensor_scalar(km[t][:, j, :], ks[t][:, :], slot[:, j:j + 1], None, ALU.mult)\
                               .then_inc(s["km"], 1)
                    dve.wait_ge(s["qh"], g + 1)
                    dve.tensor_tensor(qs[1][:, :, :], q[:, :, :], qs[0][:, :, :], ALU.subtract).then_inc(s["ql"], 1)
                    dve.wait_ge(s["vh"], g + 1)
                    dve.tensor_tensor(vs[1][:, :, :], v[:, :, :], vs[0][:, :, :], ALU.subtract).then_inc(s["vl"], 1)
                    minus_max(g, 0, first)
                    for i in range(1, 2 * GB + 1):
                        if i < 2 * GB:
                            minus_max(g, i, first)
                        low(g, i - 1)
                        if i >= 4 and i % 2 == 0:
                            finish(g, i // 2 - 2, first)
                        if nxt is not None and i == 2:
                            fr.stats(dve, nxt)
                            context_low(nxt)
                        if nxt is not None and i == 4:
                            fr.norm(dve, nxt)
                        if nxt is not None and i == 6:
                            fr.low(dve, nxt)
                    finish(g, GB - 1, first)

                dve.memset(v[:, :, HD:HD + 1], 1.0).then_inc(s["ones"], 1)
                dve.wait_ge(s["ones"], 1)
                dve.wait_ge(s["tables_in"], 16 * 4)
                fr.stats(dve, 0)
                fr.norm(dve, 0, first=True)
                context_low(0)
                fr.low(dve, 0)
                loop(dve, main)

            @block.scalar
            def _(act):
                def context_high(g):
                    act.wait_ge(s["ctx_in"], g * 16 + 16)
                    if not starts(g, 0):
                        act.wait_ge(s["v_projected"], g)
                    act.activation(ch[:, :, :], cf[:, :, :], ACT.Copy).then_inc(s["ctx_h"], 1)

                def exp(g, i, first):
                    n = g * GB * 2 + i
                    act.wait_ge(s["sub"], n + 1)
                    if i >= 2 or not first:
                        act.wait_ge(s["turned"], n - 1)
                    act.activation(ex[i % 2][:, :, :], sub[:, i % 2, :, :], ACT.Exp, scale=1.0 / float(D) ** 0.5)\
                       .then_inc(s["exp"], 1)

                def high(g, i, first):
                    n = g * GB * 2 + i
                    b, dc = i // 2, i % 2
                    act.wait_ge(s["turned"], n + 1)
                    if b >= 2 or not first:
                        act.wait_ge(s["weighed"], g * GB + b - 1)
                    act.activation(half(0, b, dc), pT[:, :, :], ACT.Copy).then_inc(s["ph"], 1)

                def main(g, first, nxt):
                    act.wait_ge(s["k"], g + 1)
                    if not first:
                        act.wait_ge(s["km"], g * 2 * SL)
                    act.activation(ks[0][:, :], k[:, :], ACT.Copy).then_inc(s["kh"], 1)
                    act.wait_ge(s["q"], 2 * g + 2)
                    if not first:
                        act.wait_ge(s["scored"], g * GB * 2)
                    act.activation(qs[0][:, :, :], q[:, :, :], ACT.Copy).then_inc(s["qh"], 1)
                    act.wait_ge(s["v"], g + 1)
                    if not first:
                        act.wait_ge(s["weighed"], g * GB)
                    act.activation(vs[0][:, :, :], v[:, :, :], ACT.Copy).then_inc(s["vh"], 1)
                    exp(g, 0, first)
                    for i in range(1, 2 * GB + 1):
                        if i < 2 * GB:
                            exp(g, i, first)
                        high(g, i - 1, first)
                        if i == 1 and nxt is not None:
                            context_high(nxt)
                        if i == 6 and nxt is not None:
                            fr.high(act, nxt)

                nc.scalar.preload_act_table(ACT.Exp)
                context_high(0)
                fr.high(act, 0, first=True)
                loop(act, main)

            @block.gpsimd
            def _(pool):
                def main(g, first, nxt):
                    if nxt is not None:
                        fr.power_of_var(pool, nxt)
                    for b in range(GB):
                        n = g * GB + b
                        pool.wait_ge(s["out"], n + 1)
                        rows = X[:, g * GB + b, :]
                        pool.tensor_tensor(rows, rows, out[:, b % 2, :, :].rearrange("p h e -> p (h e)"), ALU.add)\
                            .then_inc(s["x_done"], 1)

                fr.power_of_var(pool, 0)
                loop(pool, main)


def moe_silu(nc, sems, X, ident, power, A):
    SCALE = 256.0
    N = E + 1
    RING = 3
    with ExitStack() as scope:
        c = Core(nc, scope, sems, "s_")
        XH, XL = c.sb("XH", [P, DC, B * S], f16), c.sb("XL", [P, DC, B * S], f16)
        cfT = c.sb("cfT", [P, B * S], f16)
        ident16 = c.sb("ident16", [P, P], f16)
        lower = c.sb("lower", [P, E * E])
        select = c.sb("select", [P, E, P], f16)
        constants(nc, sems, ident, ident16, lower, select, cfT, "const2_")
        W1 = [c.sb(f"w1{t}", [P, N, DC, P], f16) for t in range(2)]
        W2 = [c.sb(f"w2{t}", [P, N, D], f16) for t in range(2)]
        Wg = [c.sb(f"wg{t}", [P, DC, E], f16) for t in range(2)]
        b2 = [c.sb(f"b2{t}", [P, D], f16) for t in range(2)]
        b1 = c.sb("b1", [P, N])
        eb = c.sb("eb", [P, E])
        bias_in = c.sem("bias_in")

        def flat(t):
            return t.rearrange("p a b c -> p (a b c)") if len(t.shape) == 4 else t.rearrange("p a b -> p (a b)")

        split_weights(nc, sems, [(flat(A["L1_ffn_Wg"]), flat(Wg[0][:]), flat(Wg[1][:]), SCALE),
                                 (flat(A["L1_ffn_W1"]), flat(W1[0][:]), flat(W1[1][:]), SCALE),
                                 (flat(A["L1_ffn_W2"]), flat(W2[0][:]), flat(W2[1][:]), SCALE),
                                 (A["L1_ffn_b2"], b2[0][:, :], b2[1][:, :], SCALE)], "sw_")
        with ExitStack() as inner:
            r = Core(nc, inner, sems, "sr_")
            route = Router(r, X, ident, power, XH, XL, Wg)
            shares = Shares(r, cfT, ident16)
            lg, ab, ex, u, um, ln, lnt, quo, l1p, pos, sp, act_ = (
                r.sb(n, [P, B, E]) for n in ("lg", "ab", "ex", "u", "um", "ln", "lnt", "quo", "l1p", "pos", "sp", "act"))
            share = r.sb("share", [P, B, E])
            s, a_done = r.sem("routing"), r.sem("scalar_step")
            with nc.Block() as block:
                route.engines(block)

                @block.sync
                def _(sp_):
                    sp_.dma_start(eb[:, :], A["L1_ffn_expert_bias"].partition_broadcast(P)).then_inc(bias_in, 16)
                    sp_.dma_start(b1[:, :], A["L1_ffn_b1"]).then_inc(bias_in, 16)
            with nc.Block() as block:
                @block.vector
                def _(dve):
                    wait = own_steps(dve, s)
                    TINY = 1e-30
                    dve.wait_ge(bias_in, 32)
                    dve.scalar_tensor_tensor(lg[:, :, :], route.logits[:, :, :], 1.0 / SCALE, repeat(eb[:, :], B),
                                             ALU.mult, ALU.add).then_inc(s, 1)
                    wait(1)
                    dve.scalar_tensor_tensor(ab[:, :, :], lg[:, :, :], -1.0, lg[:, :, :], ALU.mult, ALU.max)\
                       .then_inc(s, 1)
                    wait(1)
                    dve.wait_ge(a_done, 1)
                    dve.tensor_scalar(u[:, :, :], ex[:, :, :], 1.0, None, ALU.add).then_inc(s, 1)
                    wait(1)
                    dve.tensor_scalar(um[:, :, :], u[:, :, :], -1.0, TINY, ALU.add, ALU.add).then_inc(s, 1)
                    dve.wait_ge(a_done, 2)
                    dve.tensor_scalar(lnt[:, :, :], ln[:, :, :], TINY, None, ALU.add).then_inc(s, 1)
                    wait(2)
                    dve.reciprocal(quo[:, :, :], um[:, :, :]).then_inc(s, 1)
                    wait(1)
                    dve.tensor_tensor(l1p[:, :, :], lnt[:, :, :], quo[:, :, :], ALU.mult).then_inc(s, 1)
                    wait(1)
                    dve.tensor_tensor(l1p[:, :, :], l1p[:, :, :], ex[:, :, :], ALU.mult).then_inc(s, 1)
                    dve.tensor_scalar(pos[:, :, :], lg[:, :, :], 0.0, None, ALU.max).then_inc(s, 1)
                    wait(2)
                    dve.tensor_tensor(sp[:, :, :], l1p[:, :, :], pos[:, :, :], ALU.add).then_inc(s, 1)
                    wait(1)
                    dve.wait_ge(a_done, 3)
                    chosen = choose_two(r, dve, act_, lower, s, wait)
                    dve.tensor_tensor(share[:, :, :], act_[:, :, :], chosen[:, :, :], ALU.mult).then_inc(s, 1)
                    wait(1)
                    shares.cut(dve, share, s, wait)
                    shares.keep(dve)

                @block.scalar
                def _(act):
                    act.wait_ge(s, 2)
                    act.activation(ex[:, :, :], ab[:, :, :], ACT.Exp, scale=-1.0).then_inc(a_done, 1)
                    act.wait_ge(s, 3)
                    act.activation(ln[:, :, :], u[:, :, :], ACT.Ln).then_inc(a_done, 1)
                    act.wait_ge(s, 10)
                    act.activation(act_[:, :, :], sp[:, :, :], ACT.Sqrt).then_inc(a_done, 1)

                @block.tensor
                def _(pe):
                    shares.turn(pe)
        pU = [c.ps(f"pU{i}", [P, GT]) for i in range(RING)]
        pC = [c.ps(f"pC{i}", [P, GT]) for i in range(RING)]
        pY = c.ps("pY", [P, GB, D])
        h, hc = ([c.sb(f"{n}{i}", [P, GT]) for i in range(RING)] for n in ("h", "hc"))
        hh, hl = ([c.sb(f"{n}{i}", [P, GT], f16) for i in range(RING)] for n in ("hh", "hl"))
        u_done, spread_done, h_done, hc_done, hh_done, hl_done, down_done, y_added = (
            c.sem(n) for n in "u_done spread_done h_done hc_done hh_done hl_done down_done y_added".split())

        def run(eng, group, tail):
            group(0, True)
            with eng.Fori(1, NG) as g:
                group(g, False)
            tail()

        with nc.Block() as block:
            @block.tensor
            def _(pe):
                def down(g, j):
                    pe.wait_ge(hl_done, g * N + j + 1)
                    if j == 0:
                        if not starts(g, 0):
                            pe.wait_ge(y_added, g)
                    for b in range(GB):
                        if j == 0:
                            for n in range(2):
                                pe.matmul(pY[:, b, :], cfT[:, bass.ds((g * GB + b) * S, S)], b2[n][:, :],
                                          start=(n == 0 and b % 2 == 0), stop=False, skip_group_check=True)
                        for x, y in TERMS:
                            last = pe.matmul(pY[:, b, :], (hh, hl)[x][j % RING][:, b * S:(b + 1) * S], W2[y][:, j, :],
                                             start=False, stop=False, skip_group_check=True)
                    last.then_inc(down_done, 1)

                def group(g, first):
                    for j in range(N):
                        if j >= RING or not first:
                            pe.wait_ge(h_done, g * N + j - RING + 1)
                            pe.wait_ge(hc_done, g * N + j - RING + 1)
                        steps = [(dc, x, y) for dc in range(DC) for x, y in TERMS]
                        for n, (dc, x, y) in enumerate(steps):
                            last = pe.matmul(pU[j % RING][:, :], W1[x][:, j, dc, :], (XH, XL)[y][:, dc, bass.ds(g * GT, GT)],
                                             start=(n == 0), stop=(n == len(steps) - 1))
                        last.then_inc(u_done, 1)
                        if j > 0:
                            pe.matmul(pC[j % RING][:, :], select[:, j - 1, :], cfT[:, bass.ds(g * GT, GT)], start=True,
                                      stop=True).then_inc(spread_done, 1)
                        if j >= 2:
                            down(g, j - 2)
                        elif not first:
                            down(g - 1, N + j - 2)

                def tail():
                    down(NG - 1, N - 2)
                    down(NG - 1, N - 1)
                run(pe, group, tail)

            @block.scalar
            def _(act):
                def high(g, j):
                    k = g * N + j
                    act.wait_ge(hc_done, k + 1)
                    if not (starts(g, 0) and j < RING):
                        act.wait_ge(down_done, k - RING + 1)
                    act.activation(hh[j % RING][:, :], hc[j % RING][:, :], ACT.Copy).then_inc(hh_done, 1)

                def group(g, first):
                    for j in range(N):
                        act.wait_ge(u_done, g * N + j + 1)
                        if j >= RING or not first:
                            act.wait_ge(hc_done, g * N + j - RING + 1)
                        act.activation(h[j % RING][:, :], pU[j % RING][:, :], ACT.Silu, bias=b1[:, j:j + 1],
                                       scale=1.0 / SCALE).then_inc(h_done, 1)
                        if j > 0:
                            high(g, j - 1)
                        elif not first:
                            high(g - 1, N - 1)
                nc.scalar.preload_act_table(ACT.Silu)
                run(act, group, lambda: high(NG - 1, N - 1))

            @block.vector
            def _(dve):
                def low(g, j):
                    k = g * N + j
                    dve.wait_ge(hh_done, k + 1)
                    dve.tensor_tensor(hl[j % RING][:, :], hc[j % RING][:, :], hh[j % RING][:, :], ALU.subtract)\
                       .then_inc(hl_done, 1)

                def take(g):
                    dve.wait_ge(down_done, g * N + N)
                    dve.scalar_tensor_tensor(X[:, bass.ds(g * GB, GB), :], pY[:, :, :], 1.0 / SCALE,
                                             X[:, bass.ds(g * GB, GB), :], ALU.mult, ALU.add).then_inc(y_added, 1)

                def group(g, first):
                    for j in range(N):
                        dve.wait_ge(h_done, g * N + j + 1)
                        if j >= RING or not first:
                            dve.wait_ge(hl_done, g * N + j - RING + 1)
                        if j == 0:
                            dve.tensor_copy(hc[0][:, :], h[0][:, :]).then_inc(hc_done, 1)
                        else:
                            dve.wait_ge(spread_done, g * (N - 1) + j)
                            dve.tensor_tensor(hc[j % RING][:, :], h[j % RING][:, :], pC[j % RING][:, :], ALU.mult)\
                               .then_inc(hc_done, 1)
                        if j > 0:
                            low(g, j - 1)
                        elif not first:
                            low(g - 1, N - 1)
                        if j == 1 and not first:
                            take(g - 1)

                def tail():
                    low(NG - 1, N - 1)
                    take(NG - 1)
                run(dve, group, tail)


def load_input(nc, sems, X, ident, power, A):
    with ExitStack() as scope:
        c = Core(nc, scope, sems, "in_")
        x_in, zeroed, made = c.sem("x_in"), c.sem("zeroed"), c.sem("made")
        with nc.Block() as block:
            @block.sync
            def _(sp):
                for h in range(4):
                    sp.dma_start(X[:, h * 8:(h + 1) * 8, :], A["x"][h * 8:(h + 1) * 8].rearrange("b s d -> s b d"))\
                      .then_inc(x_in, 16)
                sp.wait_ge(x_in, 64)

            @block.gpsimd
            def _(pool):
                pool.memset(power[:, :], -0.5).then_inc(made, 1)
                pool.memset(ident[:, :], 0.0).then_inc(zeroed, 1)
                pool.wait_ge(zeroed, 1)
                pool.affine_select(out=ident[:, :], in_=ident[:, :], compare_op=ALU.not_equal, fill=1.0, base=0,
                                   pattern=[[-1, P]], channel_multiplier=1).then_inc(made, 1)


def store_output(nc, sems, X, out):
    with ExitStack() as scope:
        c = Core(nc, scope, sems, "out_")
        stored = c.sem("stored")
        with nc.Block() as block:
            @block.sync
            def _(sp):
                for h in range(4):
                    sp.dma_start(out[h * 8:(h + 1) * 8].rearrange("b s d -> s b d"), X[:, h * 8:(h + 1) * 8, :])\
                      .then_inc(stored, 16)
                sp.wait_ge(stored, 64)


STAGES = ["softmax_attention", "retention", "moe_swiglu", "lie", "mqa", "moe_silu"]


def decoder(nc, A, out, stages):
    with ExitStack() as whole:
        c = Core(nc, whole, [], "")
        X = c.sb("X", [P, B, D])
        ident = c.sb("ident", [P, P])
        power = c.sb("power", [P, 64])
        work = {"softmax_attention": softmax_attention, "retention": retention, "moe_swiglu": moe_swiglu,
                "lie": lie_rotation, "mqa": one_key_attention, "moe_silu": moe_silu}
        sems = []
        load_input(nc, sems, X, ident, power, A)
        for name in stages:
            work[name](nc, sems, X, ident, power, A)
            give_back(nc, sems)
            sems = []
        store_output(nc, sems, X, out)


def layout(inputs):
    import numpy as np

    def rows(w):
        return np.ascontiguousarray(w.reshape(w.shape[0] // P, P, -1).transpose(1, 0, 2))

    def columns(v):
        return np.ascontiguousarray(v.reshape(-1, P).T)

    a = {n: np.asarray(v) for n, v in inputs.items()}
    d = {"x": a["x"]}
    for n in "qkv":
        d[f"L0_attn_W{n}"] = rows(a[f"L0_attn_W{n}"].T)
        d[f"L0_attn_b{n}"] = a[f"L0_attn_b{n}"]
        if n != "q":
            d[f"L0_attn_b{n}"] = columns(a[f"L0_attn_b{n}"])
    d["L0_ffn_Wg"] = rows(a["L0_ffn_Wg"])
    for n in ("W1", "W2", "W3"):
        w = a[f"L0_ffn_{n}"]
        d[f"L0_ffn_{n}"] = np.ascontiguousarray(w.reshape(E, w.shape[1] // P, P, -1).transpose(2, 0, 1, 3))
    d["ctxT"] = rows(a["ctx_1024"].reshape(B * S, D).T)
    swap = np.arange(D) ^ 1
    for n in "QKV":
        w = a[f"L0_xattn_W_{n}"].transpose(1, 0, 2).reshape(D, D)
        d[f"L0_xattn_W{n}"] = rows(w)
        if n != "V":
            d[f"L0_xattn_W{n}s"] = rows(w[:, swap])
    d["L0_xattn_Wg"], d["L0_xattn_Wo"] = rows(a["L0_xattn_g_w"].T), rows(a["L0_xattn_out_w"].T)
    d["L0_xattn_g_b"], d["L0_xattn_out_b"] = a["L0_xattn_g_b"], a["L0_xattn_out_b"]
    d.update(shape_tables())
    at = np.zeros((LD, LD), np.int64)
    at[np.triu_indices(LD, k=1)] = np.arange(LD * (LD - 1) // 2)
    at = at + at.T
    pair = ~np.eye(LD, dtype=bool)
    w = np.zeros((D, LD, LD), np.float32)
    w[:, pair] = a["L1_attn_omega_proj_w"].T[:, at[pair]]
    d["L1_attn_Wp"] = np.ascontiguousarray(w.reshape(DC, P, LD, LD).transpose(1, 0, 2, 3))
    bias = np.zeros((LD, LD), np.float32)
    bias[pair] = a["L1_attn_omega_proj_b"][at[pair]]
    d["L1_attn_omega_b"] = bias
    d["sign"] = (np.triu(np.ones((LD, LD)), 1) - np.tril(np.ones((LD, LD)), -1)).astype(np.float32)
    d["behind"] = np.ascontiguousarray(np.broadcast_to(CODES - np.arange(CODES, dtype=np.float32), (B, CODES)))
    d["L1_attn_Wvi"] = rows(a["L1_attn_vq_proj_in_w"].T)
    d["L1_attn_Wvo"] = np.ascontiguousarray(a["L1_attn_vq_proj_out_w"].T)
    d["L1_attn_Woo"] = np.ascontiguousarray(a["L1_attn_omega_out_w"].T)
    for n in ("omega_out_b", "vq_proj_in_b", "vq_proj_out_b", "codebook", "norm_w"):
        d[f"L1_attn_{n}"] = a[f"L1_attn_{n}"]
    for n in ("omega_mix", "vq_mix"):
        d[f"L1_attn_{n}"] = a[f"L1_attn_{n}"].reshape(1)
    d["L1_xattn_Wq"], d["L1_xattn_bq"] = rows(a["L1_xattn_Wq"]), columns(a["L1_xattn_bq"])
    d["L1_xattn_Wk"] = rows(np.tile(a["L1_xattn_Wk"], (1, P // HD)))
    d["L1_xattn_bk"] = np.tile(a["L1_xattn_bk"], P // HD)[:, None]
    d["L1_xattn_Wv"], d["L1_xattn_bv"] = rows(a["L1_xattn_Wv"]), a["L1_xattn_bv"]
    d["slot"] = (np.arange(P)[:, None] // HD == np.arange(P // HD)[None, :]).astype(np.float32)
    d["L1_ffn_Wg"], d["L1_ffn_expert_bias"] = rows(a["L1_ffn_routing_W"].T), a["L1_ffn_expert_bias"]
    w = np.concatenate([a["L1_ffn_sW1"][None], a["L1_ffn_rW1"]])
    d["L1_ffn_W1"] = np.ascontiguousarray(w.reshape(E + 1, DC, P, P).transpose(2, 0, 1, 3))
    w = np.concatenate([a["L1_ffn_sW2"][None], a["L1_ffn_rW2"]])
    d["L1_ffn_W2"] = np.ascontiguousarray(w.transpose(1, 0, 2))
    d["L1_ffn_b1"] = np.ascontiguousarray(np.concatenate([a["L1_ffn_sb1"][None], a["L1_ffn_rb1"]]).T)
    w = np.zeros((P, D), np.float32)
    w[0:3 * E], w[ONES] = np.tile(a["L1_ffn_rb2"], (3, 1)), a["L1_ffn_sb2"]
    d["L1_ffn_b2"] = w
    return d


def kernel(**inputs):
    import concourse.bacc as bacc
    from concourse.bass_utils import run_bass_kernel_spmd
    arrays = layout(inputs)
    nc = bacc.Bacc("TRN2", target_bir_lowering=False, num_devices=1)
    A = {n: nc.dram_tensor(f"in_{n}", v.shape, mybir.dt.from_np(v.dtype), kind="ExternalInput").ap()
         for n, v in arrays.items()}
    out = nc.dram_tensor("out", (B, S, D), f32, kind="ExternalOutput").ap()
    decoder(nc, A, out, STAGES)
    r = run_bass_kernel_spmd(nc, [{f"in_{n}": v for n, v in arrays.items()}], core_ids=[0])
    return r.results[0]["out"]
```

```python
import concourse.bass as bass
from concourse import mybir
from contextlib import ExitStack

f32 = mybir.dt.float32
f16 = mybir.dt.float16
bf16 = mybir.dt.bfloat16
i32 = mybir.dt.int32
u32 = mybir.dt.uint32
ALU = mybir.AluOpType
ACT = mybir.ActivationFunctionType
AX = mybir.AxisListType.X

B, S, D = 32, 128, 256
P = 128
DC = D // P
GB = 4
GT = GB * S
NG = B // GB
LN_EPS = 1e-5
E = 8
ONES = 32
TERMS = ((0, 0), (0, 1), (1, 0))


class Core:

    def __init__(self, nc, scope, sems, prefix):
        self.nc, self.scope, self.sems, self.prefix = nc, scope, sems, prefix

    def sb(self, name, shape, dt=f32):
        return self.scope.enter_context(self.nc.sbuf_tensor(self.prefix + name, shape, dt))

    def ps(self, name, shape, dt=f32):
        return self.scope.enter_context(self.nc.psum_tensor(self.prefix + name, shape, dt))

    def sem(self, name):
        self.sems.append(self.nc.alloc_semaphore(name=self.prefix + name))
        return self.sems[-1]


def give_back(nc, sems):
    with nc.Block() as block:
        @block.gpsimd
        def _(pool):
            nc.clear_and_free_semaphores(sems)


def spread(ap, n):
    return ap.unsqueeze(2).broadcast_to((ap.shape[0], ap.shape[1], n))


def repeat(ap, n):
    return ap.unsqueeze(1).broadcast_to((ap.shape[0], n, ap.shape[1]))


class RowStats:

    def __init__(self, c):
        self.stat = c.sb("rs_stat", [P, GB, 6])
        self.apart, self.apart2, self.both, self.dev, self.devs, self.mean, self.ve = (
            c.sb("rs_" + n, [P, GB]) for n in "apart apart2 both dev devs mean ve".split())
        self.stat_done, self.summed, self.scaled, self.ve_done = (
            c.sem("rs_" + n) for n in "stat_done summed scaled ve_done".split())

    def run(self, dve, X, g):
        mean_e, dev_e, mean_o, dev_o = (self.stat[:, :, n] for n in (1, 2, 4, 5))
        for b in range(GB):
            dve.bn_stats(self.stat[:, b, :], X[:, g * GB + b, :]).then_inc(self.stat_done, 1)
        dve.wait_ge(self.stat_done, g * GB + GB)
        dve.tensor_tensor(self.apart[:, :], mean_e, mean_o, ALU.subtract).then_inc(self.summed, 1)
        dve.tensor_tensor(self.both[:, :], mean_e, mean_o, ALU.add).then_inc(self.summed, 1)
        dve.tensor_tensor(self.dev[:, :], dev_e, dev_o, ALU.add).then_inc(self.summed, 1)
        dve.wait_ge(self.summed, g * 3 + 3)
        dve.tensor_tensor(self.apart2[:, :], self.apart[:, :], self.apart[:, :], ALU.mult).then_inc(self.scaled, 1)
        dve.tensor_scalar(self.mean[:, :], self.both[:, :], 0.5, None, ALU.mult).then_inc(self.scaled, 1)
        dve.tensor_scalar(self.devs[:, :], self.dev[:, :], 1.0 / D, LN_EPS, ALU.mult, ALU.add).then_inc(self.scaled, 1)
        dve.wait_ge(self.scaled, g * 3 + 3)
        dve.scalar_tensor_tensor(self.ve[:, :], self.apart2[:, :], 0.25, self.devs[:, :], ALU.mult, ALU.add)\
           .then_inc(self.ve_done, 1)


class Front:

    def __init__(self, c, X, ident, power, turn, used, kept=None):
        self.X, self.ident, self.power, self.turn, self.used = X, ident, power, turn, used
        self.kept = kept
        self.rs = RowStats(c)
        self.rstd = c.sb("ln_rstd", [P, GB])
        if kept is None:
            self.xn = c.sb("ln_xn", [P, GB, D])
        self.xh = c.sb("xh", [P, DC, GT], f16)
        self.xl = c.sb("xl", [P, DC, GT], f16)
        self.rstd_done = c.sem("ln_rstd_done")
        self.xn_done = c.sem("ln_xn_done")
        self.turned = c.sem("ln_turned")
        self.xh_done = c.sem("xh_done")
        self.xl_done = c.sem("xl_done")

    def stats(self, dve, g):
        self.rs.run(dve, self.X, g)

    def power_of_var(self, pool, g):
        pool.wait_ge(self.rs.ve_done, g + 1)
        pool.tensor_tensor(self.rstd[:, :], self.rs.ve[:, :], self.power[:, 0:GB], ALU.pow).then_inc(self.rstd_done, 1)

    def row(self, g, b):
        return self.xn[:, b, :] if self.kept is None else self.kept[:, g * GB + b, :]

    def norm(self, dve, g, first=False):
        dve.wait_ge(self.rstd_done, g + 1)
        if not first:
            dve.wait_ge(self.turned, g)
        for b in range(GB):
            dve.tensor_scalar(self.row(g, b), self.X[:, g * GB + b, :], self.rs.mean[:, b:b + 1],
                              self.rstd[:, b:b + 1], ALU.subtract, ALU.mult).then_inc(self.xn_done, 1)

    def transpose(self, pe, g):
        pe.wait_ge(self.xn_done, g * GB + GB)
        for dc in range(DC):
            for b in range(GB):
                last = pe.transpose(self.turn[:, dc, b * S:(b + 1) * S], self.row(g, b)[:, dc * P:(dc + 1) * P],
                                    self.ident[:, :])
        last.then_inc(self.turned, 1)

    def high(self, act, g, first=False):
        act.wait_ge(self.turned, g + 1)
        if not first:
            sem, per = self.used
            act.wait_ge(sem, g * per)
        act.activation(self.xh[:, :, :], self.turn[:, :, :], ACT.Copy).then_inc(self.xh_done, 1)

    def low(self, dve, g):
        dve.wait_ge(self.xh_done, g + 1)
        dve.tensor_tensor(self.xl[:, :, :], self.turn[:, :, :], self.xh[:, :, :], ALU.subtract)\
           .then_inc(self.xl_done, 1)


AHEAD = {
    "softmax_attention": ["L0_attn_Wq", "L0_attn_Wk", "L0_attn_Wv"],
    "retention": [f"L0_xattn_W{n}" for n in ("Q", "Qs", "K", "Ks", "V", "g", "o")],
    "moe_swiglu": ["L0_ffn_Wg"],
    "mqa": ["L1_xattn_Wq", "L1_xattn_Wk", "L1_xattn_Wv"],
    "moe_silu": ["L1_ffn_Wg", "L1_ffn_W1", "L1_ffn_W2", "L1_ffn_b2"],
}


def flat(t):
    return t.rearrange({2: "p a -> p a", 3: "p a b -> p (a b)", 4: "p a b c -> p (a b c)"}[len(t.shape)])


class Ahead:

    def __init__(self, c, A, stages):
        self.sources = {n: [flat(A[w]) for w in AHEAD[n]] for n in AHEAD if n in stages}
        self.width = max(sum(flat(A[w]).shape[1] for w in AHEAD[n]) for n in AHEAD)
        self.area = c.sb("ahead", [P, self.width])
        self.loaded = {n: c.sem("ahead_" + n) for n in self.sources}

    def held(self, name):
        at, views = 0, []
        for src in self.sources[name]:
            views.append(self.area[:, at:at + src.shape[1]])
            at += src.shape[1]
        return views

    def load(self, queue, name):
        if name in self.sources:
            for src, view in zip(self.sources[name], self.held(name)):
                queue.dma_start(view, src).then_inc(self.loaded[name], 16)


class SplitHeld:

    def __init__(self, c, ahead, name, parts, factor):
        self.loaded, self.views, self.factor = ahead.loaded[name], ahead.held(name), factor
        self.parts = [(flat(hi[:]), flat(lo[:])) for hi, lo in parts]
        self.count = len(parts)
        self.high_done, self.low_done = c.sem("weights_high_done"), c.sem("weights_low_done")

    def high(self, act, which=None):
        act.wait_ge(self.loaded, 16 * self.count)
        for n in which or range(self.count):
            act.activation(self.parts[n][0], self.views[n], ACT.Copy, scale=self.factor).then_inc(self.high_done, 1)

    def low(self, dve, which=None):
        for n in which or range(self.count):
            dve.wait_ge(self.high_done, n + 1)
            dve.scalar_tensor_tensor(self.parts[n][1], self.views[n], self.factor, self.parts[n][0],
                                     ALU.mult, ALU.subtract).then_inc(self.low_done, 1)


class SplitLoaded:
    WIDE, RING = 2048, 2

    def __init__(self, c, area, jobs):
        self.pieces = []
        for src, hi, lo, factor in jobs:
            n = src.shape[1]
            for a in range(0, n, self.WIDE):
                z = min(n, a + self.WIDE)
                self.pieces.append((src[:, a:z], hi[:, a:z], lo[:, a:z], factor))
        self.area = area
        self.loaded = [c.sem(f"loaded{i}") for i in range(self.RING)]
        self.high_done, self.low_done = c.sem("high_done"), c.sem("low_done")

    def stage(self, n):
        at = n % self.RING * self.WIDE
        return self.area[:, at:at + self.pieces[n][0].shape[1]]

    def load(self, sp):
        for n, (src, hi, lo, factor) in enumerate(self.pieces):
            if n >= self.RING:
                sp.wait_ge(self.low_done, n - self.RING + 1)
            sp.dma_start(self.stage(n), src).then_inc(self.loaded[n % self.RING], 16)

    def high(self, act):
        for n, (src, hi, lo, factor) in enumerate(self.pieces):
            act.wait_ge(self.loaded[n % self.RING], 16 * (n // self.RING + 1))
            act.activation(hi, self.stage(n), ACT.Copy, scale=factor).then_inc(self.high_done, 1)

    def low(self, dve):
        for n, (src, hi, lo, factor) in enumerate(self.pieces):
            dve.wait_ge(self.high_done, n + 1)
            dve.scalar_tensor_tensor(lo, self.stage(n), factor, hi, ALU.mult, ALU.subtract).then_inc(self.low_done, 1)


def project_features(pe, out, weight, cols, moving, done=None):
    steps = [(dc, a, b) for dc in range(DC) for a, b in TERMS]
    for n, (dc, a, b) in enumerate(steps):
        last = pe.matmul(out, weight[a][:, dc, cols], moving[b][:, dc, :], start=(n == 0), stop=(n == len(steps) - 1))
    return last


def project_tokens(pe, out, weight, cols, still, tokens):
    steps = [(dc, a, b) for dc in range(DC) for a, b in TERMS]
    for n, (dc, a, b) in enumerate(steps):
        last = pe.matmul(out, still[a][:, dc, tokens], weight[b][:, dc, cols], start=(n == 0),
                         stop=(n == len(steps) - 1))
    return last


ZERO_DMAS = 3


def zero_slots(queue, A):
    part = TILES * TILE // ZERO_DMAS
    for h in range(ZERO_DMAS):
        queue.dma_start(A["slot_rows"][h * part:(h + 1) * part, :].rearrange("(p n) d -> p n d", p=P),
                        repeat(A["zeros"], part // P)).then_inc(A["rows_zeroed"], 16)


def softmax_attention(nc, sems, X, ident, power, A, ahead):
    SCALE = 16.0
    with ExitStack() as scope:
        c = Core(nc, scope, sems, "a_")
        W = {n: [c.sb(f"w{n}{t}", [P, DC, D], f16) for t in range(2)] for n in "qkv"}
        split = SplitHeld(c, ahead, "softmax_attention", [W[n] for n in "qkv"], SCALE)
        pA, pB, pC, pD = (c.ps(n, [P, 2, 512]) for n in ("pA", "pB", "pC", "pD"))
        projected = {n: c.sem(f"{n}_projected") for n in "qkv"}
        fr = Front(c, X, ident, power, pA, (projected["q"], 1))
        bq = c.sb("bq", [P, D])
        bkv = c.sb("bkv", [P, 2, DC])
        bias_in = c.sem("bias_in")
        bkvs = c.sb("bkvs", [P, 2, DC])
        bias_done = c.sem("bias_done")
        q = c.sb("q", [P, GB, D])
        nqmax = c.sb("nqmax", [P, GB])
        qe = c.sb("qe", [P, GB, D])
        qsum = c.sb("qsum", [P, GB])
        qs16 = c.sb("qs16", [P, GB])
        rq = c.sb("rq", [P, GB])
        mx = {n: c.sb(f"{n}max", [P, 2 * GB]) for n in "kv"}
        mb = {n: c.sb(f"{n}maxb", [P, 2 * GB]) for n in "kv"}
        dif = {n: c.sb(f"{n}dif", [P, DC, GT]) for n in "kv"}
        ex = {n: c.sb(f"{n}exp", [P, DC, GT]) for n in "kv"}
        sm = {n: c.sb(f"{n}sum", [P, 2 * GB]) for n in "kv"}
        rs = {n: c.sb(f"{n}rec", [P, 2 * GB]) for n in "kv"}
        vn = c.sb("vn", [P, DC, GT])
        qT = c.sb("qT", [P, DC, GT])
        vt = c.sb("vt", [P, GB, D])
        aT = c.sb("aT", [P, GB, S])
        names = ("q_biased nqmax_done qexp_done q16_done rq_done qe_turned qT_done vn_done vn_turned vt_done "
                 "attended aT_done weighed x_done").split()
        s = {n: c.sem(n) for n in names}
        kv = {(n, w): c.sem(f"{n}_{w}") for n in "kv" for w in ("max", "maxb", "dif", "exp", "sum", "rec")}
        pC8 = pC[:, :, :].rearrange("p a (b t) -> p (a b) t", t=S)
        pD8 = pD[:, :, :].rearrange("p a (b t) -> p (a b) t", t=S)
        pA8 = pA[:, :, :].rearrange("p a (b t) -> p (a b) t", t=S)
        pB4 = pB[:, :, :].rearrange("p a (b t) -> p (a b) t", t=D)
        pC4 = pC[:, :, :].rearrange("p a (b t) -> p (a b) t", t=D)

        def eight(t):
            return t[:, :, :].rearrange("p a (b t) -> p (a b) t", t=S)

        with nc.Block() as block:
            @block.sync
            def _(sp):
                sp.dma_start(bq[:, :], A["L0_attn_bq"].partition_broadcast(P)).then_inc(bias_in, 16)
                sp.dma_start(bkv[:, 0, :], A["L0_attn_bk"]).then_inc(bias_in, 16)
                sp.dma_start(bkv[:, 1, :], A["L0_attn_bv"]).then_inc(bias_in, 16)
                sp.wait_ge(split.low_done, split.count)
                ahead.load(sp, "retention")
                zero_slots(sp, A)

            @block.tensor
            def _(pe):
                def project_v(g, first):
                    pe.wait_ge(fr.xl_done, g + 1)
                    if not first:
                        pe.wait_ge(kv["v", "dif"], g * 2)
                    for m in range(DC):
                        last = project_features(pe, pD[:, m, :], W["v"], slice(m * P, (m + 1) * P), (fr.xh, fr.xl))
                    last.then_inc(projected["v"], 1)

                def project_k(g, first):
                    if not first:
                        pe.wait_ge(s["vt_done"], g)
                    for m in range(DC):
                        last = project_features(pe, pC[:, m, :], W["k"], slice(m * P, (m + 1) * P), (fr.xh, fr.xl))
                    last.then_inc(projected["k"], 1)

                def main(g, first, nxt):
                    if not first:
                        pe.wait_ge(s["x_done"], g * GB)
                    for b in range(GB):
                        last = project_tokens(pe, pB4[:, b, :], [w[:, :, :] for w in W["q"]], slice(0, D),
                                              (fr.xh, fr.xl), slice(b * S, (b + 1) * S))
                    last.then_inc(projected["q"], 1)
                    pe.wait_ge(kv["k", "dif"], g * 2 + 2)
                    pe.wait_ge(s["vn_done"], g + 1)
                    for b in range(GB):
                        for dc in range(DC):
                            last = pe.transpose(pC4[:, b, dc * P:(dc + 1) * P], vn[:, dc, b * S:(b + 1) * S], ident[:, :])
                    last.then_inc(s["vn_turned"], 1)
                    pe.wait_ge(s["qexp_done"], g * GB + GB)
                    for dc in range(DC):
                        for b in range(GB):
                            last = pe.transpose(pA[:, dc, b * S:(b + 1) * S], qe[:, b, dc * P:(dc + 1) * P], ident[:, :])
                    last.then_inc(s["qe_turned"], 1)
                    pe.wait_ge(s["qT_done"], g + 1)
                    if nxt is not None:
                        fr.transpose(pe, nxt)
                    pe.wait_ge(kv["k", "exp"], g + 1)
                    for b in range(GB):
                        t = slice(b * S, (b + 1) * S)
                        for dc in range(DC):
                            last = pe.matmul(pB[:, 0, t], ex["k"][:, dc, t], qT[:, dc, t], start=(dc == 0), stop=(dc == DC - 1))
                    last.then_inc(s["attended"], 1)
                    if nxt is not None:
                        project_v(nxt, False)
                    pe.wait_ge(s["aT_done"], g + 1)
                    pe.wait_ge(s["vt_done"], g + 1)
                    for b in range(GB):
                        last = pe.matmul(pB4[:, b, :], aT[:, b, :], vt[:, b, :], start=True, stop=True)
                    last.then_inc(s["weighed"], 1)
                    if nxt is not None:
                        project_k(nxt, False)

                fr.transpose(pe, 0)
                pe.wait_ge(split.low_done, split.count)
                project_v(0, True)
                project_k(0, True)
                main(0, True, 1)
                with pe.Fori(1, NG - 1) as g:
                    main(g, False, g + 1)
                main(NG - 1, False, None)

            @block.vector
            def _(dve):
                def difference(n, g, psum8):
                    at = 0 if n == "k" else 1
                    dve.wait_ge(projected[n], g + 1)
                    dve.tensor_reduce(mx[n][:, :], psum8, AX, ALU.max).then_inc(kv[n, "max"], 1)
                    dve.wait_ge(kv[n, "max"], g + 1)
                    dve.tensor_tensor(mb[n][:, :].rearrange("p (a b) -> p a b", a=DC),
                                      mx[n][:, :].rearrange("p (a b) -> p a b", a=DC),
                                      spread(bkvs[:, at, :], GB), ALU.add).then_inc(kv[n, "maxb"], 1)
                    dve.wait_ge(kv[n, "maxb"], g + 1)
                    for m in range(DC):
                        dve.scalar_tensor_tensor(eight(dif[n])[:, m * GB:(m + 1) * GB, :], psum8[:, m * GB:(m + 1) * GB, :],
                                                 bkvs[:, at, m:m + 1], spread(mb[n][:, m * GB:(m + 1) * GB], S),
                                                 ALU.add, ALU.subtract).then_inc(kv[n, "dif"], 1)

                def invert_sum(n, g):
                    dve.wait_ge(kv[n, "exp"], g + 1)
                    dve.tensor_reduce(sm[n][:, :], eight(ex[n]), AX, ALU.add).then_inc(kv[n, "sum"], 1)
                    dve.wait_ge(kv[n, "sum"], g + 1)
                    dve.reciprocal(rs[n][:, :], sm[n][:, :]).then_inc(kv[n, "rec"], 1)

                def main(g, first, nxt):
                    invert_sum("v", g)
                    dve.wait_ge(projected["q"], g + 1)
                    dve.scalar_tensor_tensor(q[:, :, :], pB4, 1.0 / SCALE, repeat(bq[:, :], GB), ALU.mult, ALU.add)\
                       .then_inc(s["q_biased"], 1)
                    dve.wait_ge(s["q_biased"], g + 1)
                    dve.tensor_reduce(nqmax[:, :], q[:, :, :], AX, ALU.max, negate=True).then_inc(s["nqmax_done"], 1)
                    if nxt is not None:
                        fr.stats(dve, nxt)
                    invert_sum("k", g)
                    if nxt is not None:
                        fr.norm(dve, nxt)
                    dve.wait_ge(kv["k", "rec"], g + 1)
                    dve.wait_ge(s["qe_turned"], g + 1)
                    dve.tensor_tensor(eight(qT), pA8, spread(rs["k"][:, :], S), ALU.mult).then_inc(s["qT_done"], 1)
                    dve.wait_ge(s["qexp_done"], g * GB + GB)
                    dve.tensor_scalar(qs16[:, :], qsum[:, :], float(D) ** 0.5, None, ALU.mult).then_inc(s["q16_done"], 1)
                    dve.wait_ge(s["q16_done"], g + 1)
                    dve.reciprocal(rq[:, :], qs16[:, :]).then_inc(s["rq_done"], 1)
                    if nxt is not None:
                        fr.low(dve, nxt)
                        difference("v", nxt, pD8)
                    dve.wait_ge(s["rq_done"], g + 1)
                    dve.wait_ge(s["weighed"], g + 1)
                    for b in range(GB):
                        dve.scalar_tensor_tensor(X[:, g * GB + b, :], pB4[:, b, :], rq[:, b:b + 1], X[:, g * GB + b, :],
                                                 ALU.mult, ALU.add).then_inc(s["x_done"], 1)
                    if nxt is not None:
                        difference("k", nxt, pC8)

                dve.wait_ge(bias_in, 48)
                dve.tensor_scalar(bkvs[:, :, :], bkv[:, :, :], SCALE, None, ALU.mult).then_inc(bias_done, 1)
                dve.wait_ge(bias_done, 1)
                fr.stats(dve, 0)
                fr.norm(dve, 0, first=True)
                split.low(dve)
                fr.low(dve, 0)
                difference("v", 0, pD8)
                difference("k", 0, pC8)
                main(0, True, 1)
                with dve.Fori(1, NG - 1) as g:
                    main(g, False, g + 1)
                main(NG - 1, False, None)

            @block.scalar
            def _(act):
                def exps(g):
                    for n in "vk":
                        act.wait_ge(kv[n, "dif"], g * 2 + 2)
                        act.activation(ex[n][:, :, :], dif[n][:, :, :], ACT.Exp, scale=1.0 / SCALE)\
                           .then_inc(kv[n, "exp"], 1)

                def main(g, first, nxt):
                    act.wait_ge(s["nqmax_done"], g + 1)
                    for b in range(GB):
                        act.activation(qe[:, b, :], q[:, b, :], ACT.Exp, bias=nqmax[:, b:b + 1],
                                       accum_out=qsum[:, b:b + 1]).then_inc(s["qexp_done"], 1)
                    act.wait_ge(s["vn_turned"], g + 1)
                    act.activation(vt[:, :, :], pC4, ACT.Copy).then_inc(s["vt_done"], 1)
                    if nxt is not None:
                        fr.high(act, nxt)
                    act.wait_ge(s["attended"], g + 1)
                    act.activation(aT[:, :, :].rearrange("p a b -> p (a b)"), pB[:, 0, :], ACT.Copy).then_inc(s["aT_done"], 1)
                    if nxt is not None:
                        exps(nxt)

                nc.scalar.preload_act_table(ACT.Exp)
                split.high(act)
                fr.high(act, 0, first=True)
                exps(0)
                main(0, True, 1)
                with act.Fori(1, NG - 1) as g:
                    main(g, False, g + 1)
                main(NG - 1, False, None)

            @block.gpsimd
            def _(pool):
                def main(g, first, nxt):
                    pool.wait_ge(kv["v", "rec"], g + 1)
                    pool.tensor_tensor(eight(vn), eight(ex["v"]), spread(rs["v"][:, :], S), ALU.mult)\
                        .then_inc(s["vn_done"], 1)
                    if nxt is not None:
                        fr.power_of_var(pool, nxt)

                fr.power_of_var(pool, 0)
                main(0, True, 1)
                with pool.Fori(1, NG - 1) as g:
                    main(g, False, g + 1)
                main(NG - 1, False, None)


class Router:

    def __init__(self, c, X, ident, power, XH, XL, Wg, split):
        self.split = split
        self.turn = [c.ps(f"turn{i}", [P, DC, GT]) for i in range(1)]
        self.logits = c.ps("logits", [P, B, E])
        self.fr = Front(c, X, ident, power, self.turn[0], None)
        self.XH, self.XL, self.Wg = XH, XL, Wg
        self.logits_done = c.sem("logits_done")

    def high(self, act, g):
        fr = self.fr
        act.wait_ge(fr.turned, g + 1)
        act.activation(self.XH[:, :, bass.ds(g * GT, GT)], fr.turn[:, :, :], ACT.Copy).then_inc(fr.xh_done, 1)

    def low(self, dve, g):
        fr = self.fr
        dve.wait_ge(fr.xh_done, g + 1)
        dve.tensor_tensor(self.XL[:, :, bass.ds(g * GT, GT)], fr.turn[:, :, :], self.XH[:, :, bass.ds(g * GT, GT)],
                          ALU.subtract).then_inc(fr.xl_done, 1)

    def engines(self, block):
        fr = self.fr

        @block.tensor
        def _(pe):
            fr.transpose(pe, 0)

            def rest(g):
                pe.wait_ge(fr.xl_done, g)
                fr.transpose(pe, g)
            with pe.Fori(1, NG) as g:
                rest(g)
            pe.wait_ge(fr.xl_done, NG)
            pe.wait_ge(self.split.low_done, 1)
            steps = [(dc, a, b) for dc in range(DC) for a, b in TERMS]
            for t in range(B):
                for n, (dc, a, b) in enumerate(steps):
                    last = pe.matmul(self.logits[:, t, :], (self.XH, self.XL)[a][:, dc, t * S:(t + 1) * S],
                                     self.Wg[b][:, dc, :], start=(n == 0), stop=(n == len(steps) - 1))
            last.then_inc(self.logits_done, 1)

        @block.scalar
        def _(act):
            self.split.high(act, [0])
            self.high(act, 0)
            with act.Fori(1, NG) as g:
                self.high(act, g)
            self.split.high(act, range(1, self.split.count))

        @block.gpsimd
        def _(pool):
            with pool.Fori(0, NG) as g:
                fr.power_of_var(pool, g)

        @block.vector
        def _(dve):
            fr.stats(dve, 0)
            fr.norm(dve, 0, first=True)
            self.split.low(dve, [0])
            with dve.Fori(0, NG - 1) as g:
                fr.stats(dve, g + 1)
                fr.norm(dve, g + 1)
                self.low(dve, g)
            self.low(dve, NG - 1)
            self.split.low(dve, range(1, self.split.count))


def choose_two(c, dve, score, lower, s, wait):
    gt = c.sb("gt", [P, B, E, E])
    eq = c.sb("eq", [P, B, E, E])
    rank = c.sb("rank", [P, B, E])
    chosen = c.sb("chosen", [P, B, E])
    mine = score[:, :, :].unsqueeze(3).broadcast_to((P, B, E, E))
    other = score[:, :, :].unsqueeze(2).broadcast_to((P, B, E, E))
    dve.tensor_tensor(gt[:, :, :, :], other, mine, ALU.is_gt).then_inc(s, 1)
    dve.tensor_tensor(eq[:, :, :, :], other, mine, ALU.is_equal).then_inc(s, 1)
    wait(2)
    dve.tensor_tensor(eq[:, :, :, :].rearrange("p b e f -> p b (e f)"), eq[:, :, :, :].rearrange("p b e f -> p b (e f)"),
                      repeat(lower[:, :], B), ALU.mult).then_inc(s, 1)
    wait(1)
    dve.tensor_tensor(gt[:, :, :, :], gt[:, :, :, :], eq[:, :, :, :], ALU.add).then_inc(s, 1)
    wait(1)
    dve.tensor_reduce(rank[:, :, :].rearrange("p b e -> p (b e)"), gt[:, :, :, :].rearrange("p b e f -> p (b e) f"),
                      AX, ALU.add).then_inc(s, 1)
    wait(1)
    dve.tensor_scalar(chosen[:, :, :], rank[:, :, :], 1.5, None, ALU.is_lt).then_inc(s, 1)
    wait(1)
    return chosen, rank


def starts(value, n):
    return isinstance(value, int) and value == n


def own_steps(dve, s):
    count = [0]

    def wait(n):
        count[0] += n
        dve.wait_ge(s, count[0])
    return wait


class Shares:

    def __init__(self, c, cfT, ident16):
        self.c, self.cfT, self.ident16 = c, cfT, ident16
        self.parts = c.sb("parts", [P, B, 3, E], f16)
        self.left1 = c.sb("left1", [P, B, E])
        self.left2 = c.sb("left2", [P, B, E])
        self.turned = c.ps("shares_turned", [P, B * S], f16)
        self.parts_done = c.sem("parts_done")
        self.shares_turned = c.sem("shares_turned_done")
        self.cfT_done = c.sem("cfT_done")

    def cut(self, dve, share, s, wait):
        dve.tensor_copy(self.parts[:, :, 0, :], share[:, :, :]).then_inc(s, 1)
        wait(1)
        dve.tensor_tensor(self.left1[:, :, :], share[:, :, :], self.parts[:, :, 0, :], ALU.subtract).then_inc(s, 1)
        wait(1)
        dve.tensor_copy(self.parts[:, :, 1, :], self.left1[:, :, :]).then_inc(s, 1)
        wait(1)
        dve.tensor_tensor(self.left2[:, :, :], self.left1[:, :, :], self.parts[:, :, 1, :], ALU.subtract).then_inc(s, 1)
        wait(1)
        dve.tensor_copy(self.parts[:, :, 2, :], self.left2[:, :, :]).then_inc(self.parts_done, 1)

    def turn(self, pe):
        pe.wait_ge(self.parts_done, 1)
        for b in range(B):
            last = pe.transpose(self.turned[0:3 * E, b * S:(b + 1) * S],
                                self.parts[:, b, :, :].rearrange("p a e -> p (a e)"), self.ident16[:, :])
        last.then_inc(self.shares_turned, 1)

    def keep(self, dve):
        dve.wait_ge(self.shares_turned, 1)
        dve.tensor_copy(self.cfT[0:3 * E, :], self.turned[0:3 * E, :]).then_inc(self.cfT_done, 1)


def constants(nc, sems, ident, ident16, lower, select, cfT, prefix):
    with ExitStack() as scope:
        c = Core(nc, scope, sems, prefix)
        zeroed, made, copied = c.sem("zeroed"), c.sem("made"), c.sem("copied")
        with nc.Block() as block:
            @block.gpsimd
            def _(pool):
                pool.memset(lower[:, :], 1.0).then_inc(zeroed, 1)
                pool.memset(select[:, :, :], 0.0).then_inc(zeroed, 1)
                pool.wait_ge(zeroed, 2)
                pool.affine_select(out=lower[:, :].rearrange("p (e f) -> p e f", e=E),
                                   in_=lower[:, :].rearrange("p (e f) -> p e f", e=E), compare_op=ALU.is_gt, fill=0.0,
                                   base=0, pattern=[[1, E], [-1, E]], channel_multiplier=0).then_inc(made, 1)
                for part in range(3):
                    pool.affine_select(out=select[:, :, :], in_=select[:, :, :], compare_op=ALU.not_equal, fill=1.0,
                                       base=-E * part, pattern=[[-1, E], [0, P]], channel_multiplier=1)\
                        .then_inc(made, 1)
                    pool.wait_ge(made, part + 2)

            @block.vector
            def _(dve):
                dve.tensor_copy(ident16[:, :], ident[:, :]).then_inc(copied, 1)
                dve.memset(cfT[:, :], 0.0).then_inc(copied, 1)
                dve.wait_ge(copied, 2)
                dve.memset(cfT[ONES:ONES + 1, :], 1.0).then_inc(copied, 1)


TILE = 2 * P
TILES = (2 * B * S + E * (TILE - 1)) // TILE
STEPS = B * S // TILE


def dispatch_constants(nc, sems, lower, before, ones, steps, tile_start, A):
    with ExitStack() as scope:
        c = Core(nc, scope, sems, "const1_")
        zeroed, made, loaded = c.sem("zeroed"), c.sem("made"), c.sem("loaded")
        with nc.Block() as block:
            @block.gpsimd
            def _(pool):
                pool.memset(lower[:, :], 1.0).then_inc(zeroed, 1)
                pool.memset(before[:, :], 1.0).then_inc(zeroed, 1)
                pool.memset(ones[:, :], 1.0).then_inc(zeroed, 1)
                pool.wait_ge(zeroed, 3)
                pool.affine_select(out=lower[:, :].rearrange("p (e f) -> p e f", e=E),
                                   in_=lower[:, :].rearrange("p (e f) -> p e f", e=E), compare_op=ALU.is_gt, fill=0.0,
                                   base=0, pattern=[[1, E], [-1, E]], channel_multiplier=0).then_inc(made, 1)
                pool.affine_select(out=before[:, :], in_=before[:, :], compare_op=ALU.is_gt, fill=0.0, base=0,
                                   pattern=[[1, P]], channel_multiplier=-1).then_inc(made, 1)

            @block.sync
            def _(sp):
                sp.dma_start(steps[:, :], A["tile_start"][0:STEPS].partition_broadcast(P)).then_inc(loaded, 16)
                sp.dma_start(tile_start[:, :], A["tile_start"].partition_broadcast(P)).then_inc(loaded, 16)
                sp.wait_ge(loaded, 32)


def moe_swiglu(nc, sems, X, ident, power, A, ahead):
    SCALE = 256.0
    HC = 4
    HID = HC * P
    rows, results, slot, part = (A[n] for n in ("slot_rows", "slot_results", "token_slots", "token_parts"))
    with ExitStack() as scope:
        c = Core(nc, scope, sems, "m_")
        owner = c.sb("owner", [P, TILES], i32)
        with ExitStack() as inner:
            w = Core(nc, inner, sems, "mw_")
            def jobs(pairs):
                return [(flat(A[f"L0_ffn_{n}"]), flat(w[0][:]), flat(w[1][:]), SCALE) for n, w in pairs]

            rowsN = w.sb("rows", [P, B, D])
            with ExitStack() as routing:
                r = Core(nc, routing, sems, "mr_")
                Wg = [r.sb(f"wg{t}", [P, DC, E], f16) for t in range(2)]
                split = SplitHeld(r, ahead, "moe_swiglu", [Wg], SCALE)
                route(nc, r, sems, X, ident, power, A, Wg, split, SCALE, rowsN, slot, part, owner)
            W1, W2 = ([w.sb(f"w{n}{t}", [P, E, DC, HID], f16) for t in range(2)] for n in (1, 2))
            W3 = [w.sb(f"w3{t}", [P, E, HC, D], f16) for t in range(2)]
            with ExitStack() as moving:
                m = Core(nc, moving, sems, "ms_")
                split = SplitLoaded(m, ahead.area, jobs([("W1", W1), ("W2", W2), ("W3", W3)]))
                scattered = m.sem("scattered")
                with nc.Block() as block:
                    block.sync(split.load)
                    block.scalar(split.high)
                    block.vector(split.low)

                    @block.gpsimd
                    def _(pool):
                        pool.wait_ge(A["rows_zeroed"], 16 * ZERO_DMAS)
                        for k in range(2):
                            for b in range(B):
                                pool.indirect_dma_start(rows[:, :],
                                                        bass.IndirectOffsetOnAxis(ap=slot[:, k, b:b + 1], axis=0),
                                                        rowsN[:, b, :], None).then_inc(scattered, 16)
                        pool.wait_ge(scattered, 16 * 2 * B)
            with ExitStack() as tiles:
                expert_tiles(nc, Core(nc, tiles, sems, "mt_"), ahead.area, ident, W1, W2, W3, SCALE, HC, owner, rows,
                             results)


def route(nc, r, sems, X, ident, power, A, Wg, split, SCALE, rowsN, slot, part, owner):
    lower = r.sb("lower", [P, E * E])
    before, ones = r.sb("before", [P, P], f16), r.sb("ones", [P, P], f16)
    steps, tile_start = r.sb("steps", [P, STEPS]), r.sb("tile_start", [P, TILES])
    dispatch_constants(nc, sems, lower, before, ones, steps, tile_start, A)
    turn = r.ps("turn", [P, DC, GT])
    logits = r.ps("logits", [P, B, E])
    counts = r.ps("counts", [P, B + 1, E])
    logits_done = r.sem("logits_done")
    fr = Front(r, X, ident, power, turn, (logits_done, 1), rowsN)
    with nc.Block() as block:
        @block.tensor
        def _(pe):
            def weigh(g):
                pe.wait_ge(fr.xl_done, g + 1)
                for b in range(GB):
                    last = project_tokens(pe, logits[:, bass.ds(g * GB + b, 1), :].rearrange("p b e -> p (b e)"),
                                          Wg, slice(0, E), (fr.xh, fr.xl), slice(b * S, (b + 1) * S))
                last.then_inc(logits_done, 1)
            fr.transpose(pe, 0)
            pe.wait_ge(split.low_done, 1)
            for g in range(1, NG):
                weigh(g - 1)
                fr.transpose(pe, g)
            weigh(NG - 1)

        @block.scalar
        def _(act):
            split.high(act)
            fr.high(act, 0, first=True)
            with act.Fori(1, NG) as g:
                fr.high(act, g)

        @block.gpsimd
        def _(pool):
            with pool.Fori(0, NG) as g:
                fr.power_of_var(pool, g)

        @block.vector
        def _(dve):
            fr.stats(dve, 0)
            fr.norm(dve, 0, first=True)
            split.low(dve)
            with dve.Fori(0, NG - 1) as g:
                fr.stats(dve, g + 1)
                fr.norm(dve, g + 1)
                fr.low(dve, g)
            fr.low(dve, NG - 1)

    big = "lg low ex kept share first second at picked".split()
    lg, low, ex, kept, share, first, second, at, picked = (r.sb(n, [P, B, E]) for n in big)
    top, tot, rec, slot_f = (r.sb(n, [P, B]) for n in "top tot rec slot_f".split())
    slot_g = r.sb("slot_g", [P, B])
    more, need, ahead, base = (r.sb("more", [P, E, STEPS]), r.sb("need", [P, E]), r.sb("ahead", [P, E, E]),
                               r.sb("base", [P, E]))
    total = r.sb("total", [P, E])
    passed, owner_f = r.sb("passed", [P, TILES, E - 1]), r.sb("owner_f", [P, TILES])
    chosen16 = r.sb("chosen16", [P, B, E], f16)
    s, exp_done, low_done, chosen_done, counted = (
        r.sem(n) for n in "routing exp_done low_done chosen_done counted".split())
    with nc.Block() as block:
        @block.vector
        def _(dve):
            wait = own_steps(dve, s)

            def step(instruction):
                instruction.then_inc(s, 1)
                wait(1)
            step(dve.tensor_scalar(lg[:, :, :], logits[:, :, :], 1.0 / SCALE, None, ALU.mult))
            step(dve.tensor_reduce(top[:, :], lg[:, :, :], AX, ALU.max))
            dve.tensor_tensor(low[:, :, :], lg[:, :, :], spread(top[:, :], E), ALU.subtract).then_inc(low_done, 1)
            chosen, rank = choose_two(r, dve, lg, lower, s, wait)
            dve.tensor_copy(chosen16[:, :, :], chosen[:, :, :]).then_inc(chosen_done, 1)
            step(dve.tensor_scalar(first[:, :, :], rank[:, :, :], 0.5, None, ALU.is_lt))
            step(dve.tensor_tensor(second[:, :, :], chosen[:, :, :], first[:, :, :], ALU.subtract))
            dve.wait_ge(counted, 1)
            step(dve.tensor_copy(total[:, :], counts[:, B, :]))
            step(dve.tensor_tensor(more[:, :, :], spread(total[:, :], STEPS), repeat(steps[:, :], E), ALU.is_gt))
            step(dve.tensor_reduce(need[:, :], more[:, :, :], AX, ALU.add))
            step(dve.tensor_tensor(ahead[:, :, :], lower[:, :].rearrange("p (e f) -> p e f", e=E),
                                   repeat(need[:, :], E), ALU.mult))
            step(dve.tensor_reduce(need[:, :], ahead[:, :, :], AX, ALU.add))
            step(dve.tensor_scalar(base[:, :], need[:, :], float(TILE), None, ALU.mult))
            step(dve.tensor_tensor(at[:, :, :], counts[:, 0:B, :], repeat(base[:, :], B), ALU.add))
            for k, (one, at_f) in enumerate(((first, slot_f), (second, slot_g))):
                step(dve.tensor_tensor(picked[:, :, :], at[:, :, :], one[:, :, :], ALU.mult))
                step(dve.tensor_reduce(at_f[:, :], picked[:, :, :], AX, ALU.add))
                step(dve.tensor_copy(slot[:, k, :], at_f[:, :]))
            step(dve.tensor_tensor(passed[:, :, :], spread(tile_start[:, :], E - 1), repeat(base[:, 1:E], TILES),
                                   ALU.is_ge))
            step(dve.tensor_reduce(owner_f[:, :], passed[:, :, :], AX, ALU.add))
            step(dve.tensor_copy(owner[:, :], owner_f[:, :]))
            dve.wait_ge(exp_done, 1)
            step(dve.tensor_tensor(kept[:, :, :], ex[:, :, :], chosen[:, :, :], ALU.mult))
            step(dve.tensor_reduce(tot[:, :], kept[:, :, :], AX, ALU.add))
            step(dve.reciprocal(rec[:, :], tot[:, :]))
            step(dve.tensor_tensor(share[:, :, :], kept[:, :, :], spread(rec[:, :], E), ALU.mult))
            for k, one in enumerate((first, second)):
                step(dve.tensor_tensor(picked[:, :, :], share[:, :, :], one[:, :, :], ALU.mult))
                step(dve.tensor_reduce(part[:, k, :], picked[:, :, :], AX, ALU.add))

        @block.scalar
        def _(act):
            act.wait_ge(low_done, 1)
            act.activation(ex[:, :, :], low[:, :, :], ACT.Exp).then_inc(exp_done, 1)

        @block.tensor
        def _(pe):
            pe.wait_ge(chosen_done, 1)
            pe.matmul(counts[:, 0:B, :], before[:, :], chosen16[:, :, :], start=True, stop=False,
                      skip_group_check=True)
            for b in range(B):
                last = pe.matmul(counts[:, b + 1:B + 1, :], ones[:, :], repeat(chosen16[:, b, :], B - b), start=False,
                                 stop=False, skip_group_check=True)
            last.then_inc(counted, 1)


def expert_tiles(nc, c, area, ident, W1, W2, W3, SCALE, HC, owner, rows, results):
    HALF = HC // 2
    BLK = TILE // P
    turn = c.ps("turn", [P, DC, TILE])
    pU, pV = ([c.ps(f"{n}{i}", [P, HALF, TILE]) for i in range(2)] for n in ("pU", "pV"))
    pY = c.ps("pY", [P, BLK, D])
    xin, yout = ([c.sb(f"{n}{i}", [P, BLK, D]) for i in range(2)] for n in ("xin", "yout"))
    xh, xl = ([c.sb(f"{n}{i}", [P, DC, TILE], f16) for i in range(2)] for n in ("xh", "xl"))
    sg, t_, h = ([area[:, (2 * n + i) * HALF * TILE:(2 * n + i + 1) * HALF * TILE].rearrange(
        "p (a t) -> p a t", a=HALF) for i in range(2)] for n in range(3))
    hh, hl = ([c.sb(f"{n}{i}", [P, HALF, TILE], f16) for i in range(2)] for n in ("hh", "hl"))
    loaded, stored = ([c.sem(f"{n}{i}") for i in range(2)] for n in ("loaded", "stored"))
    (turned, xh_done, xl_done, u_done, v_done, sg_done, t_done, h_done, hh_done, hl_done, down_done, y_copied) = (
        c.sem(n) for n in "turned xh_done xl_done u_done v_done sg_done t_done h_done hh_done hl_done down_done "
                          "y_copied".split())

    with nc.Block() as block:
        @block.sync
        def _(sp):
            def load(n, k, p, age):
                if age == 2:
                    sp.wait_ge(turned, n - 1)
                sp.dma_start(xin[p][:, :, :], rows[bass.ds(n * TILE, TILE), :].rearrange("(a p) d -> p a d", p=P))\
                  .then_inc(loaded[p], 16)

            def step(n, k, p, age):
                if age > 0:
                    store(n - 1, 1 - p)
                load(n, k, p, age)

            def store(n, p):
                sp.wait_ge(y_copied, n + 1)
                sp.dma_start(results[bass.ds(n * TILE, TILE), :].rearrange("(a p) d -> p a d", p=P), yout[p][:, :, :])\
                  .then_inc(stored[p], 16)
            load(0, 0, 0, 0)
            load(1, 0, 1, 1)
            load(2, 1, 0, 2)
            store(0, 0)
            with sp.Fori(1, (TILES - 1) // 2) as i:
                load(2 * i + 1, i, 1, 2)
                store(2 * i - 1, 1)
                load(2 * i + 2, i + 1, 0, 2)
                store(2 * i, 0)
            store(TILES - 2, 1)
            store(TILES - 1, 0)
            sp.wait_ge(stored[0], 16 * ((TILES + 1) // 2))
            sp.wait_ge(stored[1], 16 * (TILES // 2))

        @block.tensor
        def _(pe):
            def transpose(n, k, p, first=False):
                pe.wait_ge(loaded[p], 16 * k + 16)
                if not first:
                    pe.wait_ge(xl_done, n)
                for dc in range(DC):
                    for a in range(BLK):
                        last = pe.transpose(turn[:, dc, a * P:(a + 1) * P], xin[p][:, a, dc * P:(dc + 1) * P],
                                            ident[:, :])
                last.then_inc(turned, 1)

            def up(n, p, half, e, first):
                pe.wait_ge(xl_done, n + 1)
                if not first:
                    pe.wait_ge(h_done, 2 * n - 1 + half)
                for ps, W, sem in ((pU, W1, u_done), (pV, W2, v_done)):
                    steps = [(dc, x, y) for dc in range(DC) for x, y in TERMS]
                    for j in range(HALF):
                        cols = slice((half * HALF + j) * P, (half * HALF + j + 1) * P)
                        for m, (dc, x, y) in enumerate(steps):
                            last = pe.matmul(ps[half][:, j, :], W[x][:, e, dc, cols], (xh, xl)[y][p][:, dc, :],
                                             start=(m == 0), stop=(m == len(steps) - 1))
                    last.then_inc(sem, 1)

            def down(n, half, e, first):
                pe.wait_ge(hl_done, 2 * n + half + 1)
                if half == 0 and not first:
                    pe.wait_ge(y_copied, n)
                for j in range(HALF):
                    for a in range(BLK):
                        for m, (x, y) in enumerate(TERMS):
                            last = pe.matmul(pY[:, a, :], (hh, hl)[x][half][:, j, a * P:(a + 1) * P],
                                             W3[y][:, e, half * HALF + j, :],
                                             start=half == 0 and j == 0 and a == 0 and m == 0, stop=False,
                                             skip_group_check=True)
                last.then_inc(down_done, 1)

            def step(n, k, p, age):
                e = pe.value_load(owner[0:1, bass.ds(n, 1)], min_val=0, max_val=E - 1)
                up(n, p, 0, e, age == 0)
                if age > 0:
                    before = pe.value_load(owner[0:1, bass.ds(n - 1, 1)], min_val=0, max_val=E - 1)
                    down(n - 1, 1, before, False)
                if not starts(n, TILES - 1):
                    transpose(n + 1, k + p, 1 - p)
                up(n, p, 1, e, age == 0)
                down(n, 0, e, age == 0)
            transpose(0, 0, 0, first=True)
            for n in range(3):
                step(n, n // 2, n % 2, min(n, 2))
            with pe.Fori(1, (TILES - 3) // 2) as i:
                step(2 * i + 1, i, 1, 2)
                step(2 * i + 2, i + 1, 0, 2)
            step(TILES - 2, (TILES - 2) // 2, 1, 2)
            step(TILES - 1, (TILES - 1) // 2, 0, 2)
            last = pe.value_load(owner[0:1, TILES - 1:TILES], min_val=0, max_val=E - 1)
            down(TILES - 1, 1, last, False)

        @block.scalar
        def _(act):
            def high(n, p, old):
                act.wait_ge(turned, n + 1)
                if old:
                    act.wait_ge(v_done, 2 * n - 2)
                act.activation(xh[p][:, :, :], turn[:, :, :], ACT.Copy).then_inc(xh_done, 1)

            def sigmoid(n, half, first):
                act.wait_ge(u_done, 2 * n + half + 1)
                if not first:
                    act.wait_ge(t_done, 2 * n - 1 + half)
                act.activation(sg[half][:, :, :], pU[half][:, :, :], ACT.Sigmoid, scale=1.0 / SCALE).then_inc(sg_done, 1)

            def hidden_high(n, half, first):
                act.wait_ge(h_done, 2 * n + half + 1)
                if not first:
                    act.wait_ge(down_done, 2 * n - 1 + half)
                act.activation(hh[half][:, :, :], h[half][:, :, :], ACT.Copy).then_inc(hh_done, 1)

            def result(n, k, p, old):
                act.wait_ge(down_done, 2 * n + 2)
                if old:
                    act.wait_ge(stored[p], 16 * k)
                act.activation(yout[p][:, :, :], pY[:, :, :], ACT.Copy, scale=1.0 / SCALE).then_inc(y_copied, 1)

            def step(n, k, p, age):
                sigmoid(n, 0, age == 0)
                hidden_high(n, 0, age == 0)
                if age > 0:
                    result(n - 1, k - 1 + p, 1 - p, not starts(n, 1) and not starts(n, 2))
                if not starts(n, TILES - 1):
                    high(n + 1, 1 - p, age > 0)
                sigmoid(n, 1, age == 0)
                hidden_high(n, 1, age == 0)
            nc.scalar.preload_act_table(ACT.Sigmoid)
            high(0, 0, False)
            for n in range(3):
                step(n, n // 2, n % 2, min(n, 2))
            with act.Fori(1, (TILES - 3) // 2) as i:
                step(2 * i + 1, i, 1, 2)
                step(2 * i + 2, i + 1, 0, 2)
            step(TILES - 2, (TILES - 2) // 2, 1, 2)
            step(TILES - 1, (TILES - 1) // 2, 0, 2)
            result(TILES - 1, (TILES - 1) // 2, 0, True)

        @block.vector
        def _(dve):
            def low(n, p):
                dve.wait_ge(xh_done, n + 1)
                dve.tensor_tensor(xl[p][:, :, :], turn[:, :, :], xh[p][:, :, :], ALU.subtract).then_inc(xl_done, 1)

            def gate(n, half, first):
                dve.wait_ge(sg_done, 2 * n + half + 1)
                if not first:
                    dve.wait_ge(hl_done, 2 * n - 1 + half)
                dve.tensor_tensor(t_[half][:, :, :], pU[half][:, :, :], sg[half][:, :, :], ALU.mult).then_inc(t_done, 1)
                dve.wait_ge(t_done, 2 * n + half + 1)
                dve.wait_ge(v_done, 2 * n + half + 1)
                dve.scalar_tensor_tensor(h[half][:, :, :], t_[half][:, :, :], 1.0 / SCALE / SCALE, pV[half][:, :, :],
                                         ALU.mult, ALU.mult).then_inc(h_done, 1)

            def hidden_low(n, half):
                dve.wait_ge(hh_done, 2 * n + half + 1)
                dve.tensor_tensor(hl[half][:, :, :], h[half][:, :, :], hh[half][:, :, :], ALU.subtract)\
                   .then_inc(hl_done, 1)

            def step(n, k, p, age):
                gate(n, 0, age == 0)
                hidden_low(n, 0)
                if not starts(n, TILES - 1):
                    low(n + 1, 1 - p)
                gate(n, 1, age == 0)
                hidden_low(n, 1)
            low(0, 0)
            for n in range(3):
                step(n, n // 2, n % 2, min(n, 2))
            with dve.Fori(1, (TILES - 3) // 2) as i:
                step(2 * i + 1, i, 1, 2)
                step(2 * i + 2, i + 1, 0, 2)
            step(TILES - 2, (TILES - 2) // 2, 1, 2)
            step(TILES - 1, (TILES - 1) // 2, 0, 2)


NH, HD = 16, 16


def retention(nc, sems, X, ident, power, A, ahead):
    SCALE = 256.0
    QK = 16.0
    RET = QK * QK * SCALE
    HB = NH // DC
    with ExitStack() as scope:
        c = Core(nc, scope, sems, "r_")
        W = {n: [c.sb(f"w{n}{t}", [P, DC, D], f16) for t in range(2)] for n in ("Q", "Qs", "K", "Ks", "V", "g", "o")}
        split = SplitHeld(c, ahead, "retention", [W[n] for n in W], SCALE)
        pA, pB = (c.ps(n, [P, 2, 512]) for n in ("pA", "pB"))
        pS = [c.ps(f"pS{i}", [P, HB, S]) for i in range(DC)]
        names = ("q_projected qs_projected k_projected ks_projected v_projected gate_projected q1 q2 qr qh ql qm k1 k2 "
                 "kT kh kl qm_act qm_pool vh vl gz gate scored masked simh siml0 siml1 retained kept mu_sum mu centred squared var_sum var sd "
                 "rstd normed gated gated_turned gh gl out_projected bias_added x_done ctx_in ctx_h ctx_l "
                 "tables_in").split()
        s = {n: c.sem(n + "_done") for n in names}
        fr = Front(c, X, ident, power, pB, (s["gate_projected"], 1))
        cf = c.sb("ctx", [P, DC, GT])
        ch, cl = (c.sb(n, [P, DC, GT], f16) for n in ("ch", "cl"))
        tab = {n: c.sb(n, [P, S]) for n in ("cos_q", "sin_q", "cos_k", "sin_k")}
        slot = c.sb("slot", [P, HB])
        decay = c.sb("decay", [P, DC, HB, S])
        gb, ob = c.sb("gb", [P, D]), c.sb("ob", [P, D])
        a1, a2, qr, kT = (c.sb(n, [P, DC, GT]) for n in ("a1", "a2", "qr", "kT"))
        qs, ks = ([c.sb(f"{n}s{t}", [P, DC, GT], f16) for t in range(2)] for n in "qk")
        qm = [c.sb(f"qm{t}", [P, HB, DC, GT], f16) for t in range(2)]
        vh, vl = (c.sb(n, [P, GB, D], f16) for n in ("vh", "vl"))
        gz, gate = (c.sb(n, [P, GB, D]) for n in ("gz", "gate"))
        sim = [c.sb(f"sim{i}", [P, HB, S]) for i in range(DC)]
        simh, siml = ([c.sb(f"{n}{i}", [P, HB, S], f16) for i in range(DC)] for n in ("simh", "siml"))
        kept = c.sb("kept", [P, GB * NH, HD])
        sq = c.sb("sq", [P, GB * NH, HD])
        musum, mu, varsum, var, sd, rstd = (c.sb(n, [P, GB * NH]) for n in ("musum", "mu", "varsum", "var", "sd", "rstd"))
        gh, gl = (c.sb(n, [P, DC, GT], f16) for n in ("gh", "gl"))
        pA4 = pA[:, :, :].rearrange("p a (b t) -> p (a b) t", t=D)
        pB4 = pB[:, :, :].rearrange("p a (b t) -> p (a b) t", t=D)
        pA8 = pA[:, :, :].rearrange("p a (b t) -> p (a b) t", t=S)
        pB8 = pB[:, :, :].rearrange("p a (b t) -> p (a b) t", t=S)

        masks = {"act": [(0, h) for h in range(4, HB)], "pool": [(0, 0), (0, 1), (1, 0)],
                 "dve": [(0, 2), (0, 3)] + [(1, h) for h in range(1, HB)]}

        def eight(t):
            return t[:, :, :].rearrange("p a (b t) -> p (a b) t", t=S)

        def loop(eng, main):
            main(0, True, 1)
            with eng.Fori(1, NG - 1) as g:
                main(g, False, g + 1)
            main(NG - 1, False, None)

        def half(g, i):
            return g * GB * DC + i

        with nc.Block() as block:
            @block.sync
            def _(sp):
                sp.dma_start(cf[:, :, :], A["ctxT"][:, :, 0:GT]).then_inc(s["ctx_in"], 16)
                for t, n in [(tab[n][:, :], n) for n in tab] + [(slot[:, :], "slot"),
                                                                (decay[:, :, :, :].rearrange("p c h t -> p (c h t)"), "decay")]:
                    sp.dma_start(t, A[n]).then_inc(s["tables_in"], 16)
                for t, n in ((gb, "L0_xattn_g_b"), (ob, "L0_xattn_out_b")):
                    sp.dma_start(t[:, :], A[n].partition_broadcast(P)).then_inc(s["tables_in"], 16)
                sp.wait_ge(split.low_done, split.count)
                ahead.load(sp, "moe_swiglu")
                with sp.Fori(1, NG) as g:
                    sp.wait_ge(s["ctx_l"], g)
                    sp.dma_start(cf[:, :, :], A["ctxT"][:, :, bass.ds(g * GT, GT)]).then_inc(s["ctx_in"], 16)

            @block.tensor
            def _(pe):
                def score(g, i, first):
                    b, dc = i // 2, i % 2
                    if i >= 2 or not first:
                        pe.wait_ge(s["masked"], half(g, i) - 1)
                    t = slice(b * S, (b + 1) * S)
                    for a in range(2):
                        heads = slice(a * HB // 2, (a + 1) * HB // 2)
                        for n, (x, y) in enumerate(TERMS):
                            last = pe.matmul(pS[dc][:, heads, :], ks[x][:, dc, t], qm[y][:, heads, dc, t],
                                             start=(n == 0), stop=(n == 2))
                    last.then_inc(s["scored"], 1)

                def retain(g, i):
                    b, dc = i // 2, i % 2
                    pe.wait_ge(s[f"siml{i % 2}"], g * GB + i // 2 + 1)
                    for h in range(HB):
                        e = slice((dc * HB + h) * HD, (dc * HB + h + 1) * HD)
                        for n, (x, y) in enumerate(TERMS):
                            last = pe.matmul(pA4[:, b, e], (simh, siml)[x][dc][:, h, :], (vh, vl)[y][:, b, e],
                                             start=(n == 0), stop=(n == 2))
                    last.then_inc(s["retained"], 1)

                def turn_gated(g):
                    pe.wait_ge(s["gated"], g + 1)
                    for dc in range(DC):
                        for b in range(GB):
                            last = pe.transpose(pB[:, dc, b * S:(b + 1) * S], gate[:, b, dc * P:(dc + 1) * P], ident[:, :])
                    last.then_inc(s["gated_turned"], 1)

                def project_out(g):
                    pe.wait_ge(s["gl"], g + 1)
                    for b in range(GB):
                        last = project_tokens(pe, pB4[:, b, :], W["o"], slice(0, D), (gh, gl), slice(b * S, (b + 1) * S))
                    last.then_inc(s["out_projected"], 1)

                def main(g, first, nxt):
                    pe.wait_ge(fr.xl_done, g + 1)
                    pe.wait_ge(s["ctx_l"], g + 1)
                    x, ctx = (fr.xh, fr.xl), (ch, cl)
                    for n, ps, m, done, free in (("Q", pA, x, "q_projected", ("kept", 0)),
                                                 ("Qs", pB, x, "qs_projected", ("x_done", -1)),
                                                 ("K", pA, ctx, "k_projected", ("q1", 1)),
                                                 ("Ks", pB, ctx, "ks_projected", ("q2", 1))):
                        if free[1] == 1:
                            pe.wait_ge(s[free[0]], g + 1)
                        elif free[1] == 0 and not first:
                            pe.wait_ge(s[free[0]], g)
                        elif free[1] == -1 and not first and not starts(g, 1):
                            pe.wait_ge(s[free[0]], g - 1)
                        for a in range(DC):
                            last = project_features(pe, ps[:, a, :], W[n], slice(a * P, (a + 1) * P), m)
                        last.then_inc(s[done], 1)
                    pe.wait_ge(s["k1"], g + 1)
                    for b in range(GB):
                        last = project_tokens(pe, pA4[:, b, :], W["V"], slice(0, D), ctx, slice(b * S, (b + 1) * S))
                    last.then_inc(s["v_projected"], 1)
                    pe.wait_ge(s["k2"], g + 1)
                    for b in range(GB):
                        last = project_tokens(pe, pB4[:, b, :], W["g"], slice(0, D), x, slice(b * S, (b + 1) * S))
                    last.then_inc(s["gate_projected"], 1)
                    pe.wait_ge(s["kl"], g + 1)
                    pe.wait_ge(s["qm"], (g + 1) * len(masks["dve"]))
                    pe.wait_ge(s["qm_act"], (g + 1) * len(masks["act"]))
                    pe.wait_ge(s["qm_pool"], (g + 1) * len(masks["pool"]))
                    score(g, 0, first)
                    score(g, 1, first)
                    pe.wait_ge(s["vl"], g + 1)
                    for i in range(2, 2 * GB):
                        score(g, i, first)
                        retain(g, i - 2)
                        if i == 3 and not first:
                            pe.wait_ge(s["gz"], g + 1)
                            turn_gated(g - 1)
                        if i == 5 and nxt is not None:
                            if first:
                                pe.wait_ge(s["gz"], g + 1)
                            else:
                                pe.wait_ge(s["gl"], g)
                            fr.transpose(pe, nxt)
                        if i == 7 and not first:
                            if nxt is not None:
                                pe.wait_ge(fr.xl_done, nxt + 1)
                            project_out(g - 1)
                    retain(g, 2 * GB - 2)
                    retain(g, 2 * GB - 1)

                fr.transpose(pe, 0)
                pe.wait_ge(split.low_done, split.count)
                loop(pe, main)
                pe.wait_ge(s["x_done"], NG - 1)
                turn_gated(NG - 1)
                project_out(NG - 1)

            @block.vector
            def _(dve):
                def mask(g, i, first):
                    dc = i % 2
                    dve.wait_ge(s["scored"], half(g, i) + 1)
                    if i >= 2 or not first:
                        dve.wait_ge(s[f"siml{dc}"], g * GB + i // 2)
                    dve.tensor_tensor(sim[dc][:, :, :], pS[dc][:, :, :], decay[:, dc, :, :], ALU.mult)\
                       .then_inc(s["masked"], 1)

                def sim_low(g, i):
                    dve.wait_ge(s["simh"], half(g, i) + 1)
                    dve.tensor_tensor(siml[1][:, :, :], sim[1][:, :, :], simh[1][:, :, :], ALU.subtract)\
                       .then_inc(s["siml1"], 1)

                def centre(g):
                    dve.wait_ge(s["kept"], g + 1)
                    dve.tensor_reduce(musum[:, :], kept[:, :, :], AX, ALU.add).then_inc(s["mu_sum"], 1)
                    dve.wait_ge(s["mu_sum"], g + 1)
                    dve.tensor_scalar(mu[:, :], musum[:, :], 1.0 / HD, None, ALU.mult).then_inc(s["mu"], 1)
                    dve.wait_ge(s["mu"], g + 1)
                    dve.tensor_tensor(kept[:, :, :], kept[:, :, :], spread(mu[:, :], HD), ALU.subtract)\
                       .then_inc(s["centred"], 1)

                def vary(g):
                    dve.wait_ge(s["squared"], g + 1)
                    dve.tensor_reduce(varsum[:, :], sq[:, :, :], AX, ALU.add).then_inc(s["var_sum"], 1)
                    dve.wait_ge(s["var_sum"], g + 1)
                    dve.tensor_scalar(var[:, :], varsum[:, :], 1.0 / HD, LN_EPS * RET * RET, ALU.mult, ALU.add)\
                       .then_inc(s["var"], 1)

                def invert(g):
                    dve.wait_ge(s["sd"], g + 1)
                    dve.reciprocal(rstd[:, :], sd[:, :]).then_inc(s["rstd"], 1)

                def low_gated(g):
                    dve.wait_ge(s["gh"], g + 1)
                    dve.tensor_tensor(gl[:, :, :], pB[:, :, :], gh[:, :, :], ALU.subtract).then_inc(s["gl"], 1)

                def add_out(g):
                    dve.wait_ge(s["out_projected"], g + 1)
                    dve.wait_ge(s["bias_added"], g + 1)
                    rows = X[:, bass.ds(g * GB, GB), :]
                    dve.scalar_tensor_tensor(rows, pB4, 1.0 / SCALE, rows, ALU.mult, ALU.add).then_inc(s["x_done"], 1)

                def main(g, first, nxt):
                    dve.wait_ge(s["q_projected"], g + 1)
                    if not first:
                        dve.wait_ge(s["kT"], g)
                    dve.tensor_tensor(eight(a1), pA8, repeat(tab["cos_q"][:, :], 8), ALU.mult).then_inc(s["q1"], 1)
                    dve.wait_ge(s["qs_projected"], g + 1)
                    dve.tensor_tensor(eight(a2), pB8, repeat(tab["sin_q"][:, :], 8), ALU.mult).then_inc(s["q2"], 1)
                    dve.wait_ge(s["q1"], g + 1)
                    dve.wait_ge(s["q2"], g + 1)
                    dve.tensor_tensor(qr[:, :, :], a1[:, :, :], a2[:, :, :], ALU.add).then_inc(s["qr"], 1)
                    dve.wait_ge(s["qr"], g + 1)
                    dve.wait_ge(s["k_projected"], g + 1)
                    dve.tensor_tensor(eight(a1), pA8, repeat(tab["cos_k"][:, :], 8), ALU.mult).then_inc(s["k1"], 1)
                    dve.wait_ge(s["ks_projected"], g + 1)
                    dve.tensor_tensor(eight(a2), pB8, repeat(tab["sin_k"][:, :], 8), ALU.mult).then_inc(s["k2"], 1)
                    dve.wait_ge(s["k1"], g + 1)
                    dve.wait_ge(s["k2"], g + 1)
                    dve.tensor_tensor(kT[:, :, :], a1[:, :, :], a2[:, :, :], ALU.add).then_inc(s["kT"], 1)
                    dve.wait_ge(s["qh"], g + 1)
                    dve.tensor_tensor(qs[1][:, :, :], qr[:, :, :], qs[0][:, :, :], ALU.subtract).then_inc(s["ql"], 1)
                    dve.wait_ge(s["ql"], g + 1)
                    for t, h in masks["dve"]:
                        dve.tensor_scalar(qm[t][:, h, :, :], qs[t][:, :, :], slot[:, h:h + 1], None, ALU.mult)\
                           .then_inc(s["qm"], 1)
                    dve.wait_ge(s["vh"], g + 1)
                    dve.tensor_tensor(vl[:, :, :], pA4, vh[:, :, :], ALU.subtract).then_inc(s["vl"], 1)
                    dve.wait_ge(s["gate_projected"], g + 1)
                    if not first:
                        dve.wait_ge(s["gate"], g)
                    dve.scalar_tensor_tensor(gz[:, :, :], pB4, 1.0 / SCALE, repeat(gb[:, :], GB), ALU.mult, ALU.add)\
                       .then_inc(s["gz"], 1)
                    mask(g, 0, first)
                    mask(g, 1, first)
                    sim_low(g, 1)
                    mask(g, 2, first)
                    mask(g, 3, first)
                    if nxt is not None:
                        fr.stats(dve, nxt)
                    sim_low(g, 3)
                    if not first:
                        low_gated(g - 1)
                    mask(g, 4, first)
                    mask(g, 5, first)
                    if nxt is not None:
                        fr.norm(dve, nxt)
                    sim_low(g, 5)
                    mask(g, 6, first)
                    if nxt is not None:
                        fr.low(dve, nxt)
                    mask(g, 7, first)
                    sim_low(g, 7)
                    if not first:
                        add_out(g - 1)
                    centre(g)
                    vary(g)
                    invert(g)

                fr.stats(dve, 0)
                fr.norm(dve, 0, first=True)
                split.low(dve)
                dve.wait_ge(s["tables_in"], 16 * 8)
                fr.low(dve, 0)
                loop(dve, main)
                low_gated(NG - 1)
                add_out(NG - 1)

            @block.scalar
            def _(act):
                def context_high(g):
                    act.wait_ge(s["ctx_in"], g * 16 + 16)
                    if not starts(g, 0):
                        act.wait_ge(s["v_projected"], g)
                    act.activation(ch[:, :, :], cf[:, :, :], ACT.Copy).then_inc(s["ctx_h"], 1)

                def sim_high(g, i, first):
                    dc = i % 2
                    act.wait_ge(s["masked"], half(g, i) + 1)
                    if i >= 2 or not first:
                        act.wait_ge(s["retained"], half(g, i) - 1)
                    act.activation(simh[dc][:, :, :], sim[dc][:, :, :], ACT.Copy).then_inc(s["simh"], 1)

                def high_gated(g):
                    act.wait_ge(s["gated_turned"], g + 1)
                    act.activation(gh[:, :, :], pB[:, :, :], ACT.Copy).then_inc(s["gh"], 1)

                def main(g, first, nxt):
                    act.wait_ge(s["qr"], g + 1)
                    if not first:
                        act.wait_ge(s["qm"], g * len(masks["dve"]))
                    act.activation(qs[0][:, :, :], qr[:, :, :], ACT.Copy).then_inc(s["qh"], 1)
                    act.wait_ge(s["qh"], g + 1)
                    for t, h in masks["act"]:
                        act.activation(qm[t][:, h, :, :], qs[t][:, :, :], ACT.Copy, scale=slot[:, h:h + 1])\
                           .then_inc(s["qm_act"], 1)
                    act.wait_ge(s["kT"], g + 1)
                    if not first:
                        act.wait_ge(s["scored"], half(g, 0))
                    act.activation(ks[0][:, :, :], kT[:, :, :], ACT.Copy).then_inc(s["kh"], 1)
                    act.wait_ge(s["v_projected"], g + 1)
                    act.activation(vh[:, :, :], pA4, ACT.Copy).then_inc(s["vh"], 1)
                    for i in range(4):
                        sim_high(g, i, first)
                    if not first:
                        high_gated(g - 1)
                    if nxt is not None:
                        context_high(nxt)
                    act.wait_ge(s["gz"], g + 1)
                    act.activation(gate[:, :, :], gz[:, :, :], ACT.Silu).then_inc(s["gate"], 1)
                    sim_high(g, 4, first)
                    sim_high(g, 5, first)
                    if nxt is not None:
                        fr.high(act, nxt)
                    sim_high(g, 6, first)
                    sim_high(g, 7, first)
                    act.wait_ge(s["retained"], half(g, 2 * GB))
                    if not first:
                        act.wait_ge(s["normed"], g)
                    act.activation(kept[:, :, :].rearrange("p a e -> p (a e)"), pA[:, :, :].rearrange("p a t -> p (a t)"),
                                   ACT.Copy).then_inc(s["kept"], 1)
                    act.wait_ge(s["centred"], g + 1)
                    act.activation(sq[:, :, :], kept[:, :, :], ACT.Square).then_inc(s["squared"], 1)
                    act.wait_ge(s["var"], g + 1)
                    act.activation(sd[:, :], var[:, :], ACT.Sqrt).then_inc(s["sd"], 1)

                split.high(act)
                act.wait_ge(s["tables_in"], 16 * 8)
                context_high(0)
                fr.high(act, 0, first=True)
                loop(act, main)
                high_gated(NG - 1)

            @block.gpsimd
            def _(pool):
                def context_low(g):
                    pool.wait_ge(s["ctx_h"], g + 1)
                    pool.tensor_tensor(cl[:, :, :], cf[:, :, :], ch[:, :, :], ALU.subtract).then_inc(s["ctx_l"], 1)

                def mask(t, h):
                    pool.tensor_tensor(qm[t][:, h, :, :], qs[t][:, :, :],
                                       slot[:, h:h + 1].unsqueeze(2).broadcast_to((P, DC, GT)), ALU.mult)\
                        .then_inc(s["qm_pool"], 1)

                def main(g, first, nxt):
                    pool.wait_ge(s["qh"], g + 1)
                    for t, h in masks["pool"][:2]:
                        mask(t, h)
                    pool.wait_ge(s["kh"], g + 1)
                    pool.tensor_tensor(ks[1][:, :, :], kT[:, :, :], ks[0][:, :, :], ALU.subtract).then_inc(s["kl"], 1)
                    pool.wait_ge(s["ql"], g + 1)
                    for t, h in masks["pool"][2:]:
                        mask(t, h)
                    for i in range(0, 2 * GB, 2):
                        pool.wait_ge(s["simh"], half(g, i) + 1)
                        pool.tensor_tensor(siml[0][:, :, :], sim[0][:, :, :], simh[0][:, :, :], ALU.subtract)\
                            .then_inc(s["siml0"], 1)
                        if i == 0:
                            rows = X[:, bass.ds(g * GB, GB), :]
                            pool.wait_ge(fr.xn_done, g * GB + GB)
                            pool.tensor_tensor(rows, rows, repeat(ob[:, :], GB), ALU.add).then_inc(s["bias_added"], 1)
                        if i == 2 and nxt is not None:
                            fr.power_of_var(pool, nxt)
                            context_low(nxt)
                    pool.wait_ge(s["rstd"], g + 1)
                    pool.tensor_tensor(sq[:, :, :], kept[:, :, :], spread(rstd[:, :], HD), ALU.mult).then_inc(s["normed"], 1)
                    pool.wait_ge(s["normed"], g + 1)
                    pool.wait_ge(s["gate"], g + 1)
                    pool.tensor_tensor(gate[:, :, :].rearrange("p b d -> p (b d)"), sq[:, :, :].rearrange("p a e -> p (a e)"),
                                       gate[:, :, :].rearrange("p b d -> p (b d)"), ALU.mult).then_inc(s["gated"], 1)

                pool.wait_ge(s["tables_in"], 16 * 8)
                fr.power_of_var(pool, 0)
                context_low(0)
                loop(pool, main)


def shape_tables():
    import numpy as np
    f = np.float32
    half = HD // 2
    base = (np.arange(0, HD, 2, dtype=f) + f(0.4 * HD)) / f(1.4 * HD)
    powers = (np.arange(-(S // 2), S - S // 2, dtype=f) / f(512.0))[:, None]
    scale = base[None, :] ** powers
    inv = (1.0 / 10000.0 ** (np.arange(half, dtype=f) / half)).astype(f)
    ang = np.arange(S, dtype=f)[:, None] * inv[None, :]
    sin, cos = np.sin(ang), np.cos(ang)
    sign = np.where(np.arange(HD) % 2 == 0, -1.0, 1.0).astype(f)[:, None]

    def feature_rows(t, factor):
        return np.tile(np.repeat(t, 2, axis=1).T * f(factor), (8, 1)).astype(f)

    down = 16.0 / 256.0
    d = {"cos_q": feature_rows(cos * scale, down), "sin_q": feature_rows(sin * scale, down) * np.tile(sign, (8, 1)),
         "cos_k": feature_rows(cos / scale, down), "sin_k": feature_rows(sin / scale, down) * np.tile(sign, (8, 1))}
    gammas = 1.0 - np.exp(np.linspace(np.log(1.0 / 32.0), np.log(1.0 / 512.0), NH)).astype(f)
    dist = np.arange(S)[None, :] - np.arange(S)[:, None]
    m = np.where(dist[None] >= 0, gammas[:, None, None].astype(f) ** np.maximum(dist, 0)[None].astype(f), 0.0).astype(f)
    d["decay"] = np.ascontiguousarray(m.transpose(1, 0, 2)).reshape(P, -1)
    d["slot"] = (np.arange(P)[:, None] // HD == np.arange(P // HD)[None, :]).astype(f)
    return {n: np.ascontiguousarray(v) for n, v in d.items()}


LD, CODES = 64, 64


def lie_rotation(nc, sems, X, ident, power, A, ahead):
    SCALE = 16.0
    with ExitStack() as scope:
        c = Core(nc, scope, sems, "l_")
        XN = c.sb("XN", [P, B, D])
        hT = [c.sb(f"hT{t}", [P, B * S], f16) for t in range(2)]
        pb = [c.sb(f"pb{t}", [P, B, D], f16) for t in range(2)]
        nw = c.sb("nw", [P, D])
        hm = c.sb("hm", [P, DC, B])
        mix = c.sb("mix", [P, 2])
        ones = c.sb("ones", [P, 1])
        Wp = c.sb("Wp", [P, DC, LD, LD])
        bp, sign = c.sb("bp", [LD, LD]), c.sb("sign", [LD, LD])
        Wvi, Wvo, Woo = c.sb("Wvi", [P, DC, LD]), c.sb("Wvo", [LD, D]), c.sb("Woo", [LD, D])
        bvi, bvo, boo = c.sb("bvi", [B, LD]), c.sb("bvo", [B, D]), c.sb("boo", [B, D])
        code, behind = c.sb("code", [CODES, LD]), c.sb("behind", [B, CODES])
        consts_in, w_in = c.sem("consts_in"), c.sem("w_in")

        with ExitStack() as inner:
            r = Core(nc, inner, sems, "lf_")
            rs, rstd = RowStats(r), r.sb("rstd", [P, GB])
            xn = r.sb("xn", [P, 2, GB, D])
            pT = r.ps("pT", [P, 2, GB * S])
            pM = r.ps("pM", [P, DC, B])
            second = ahead.area[:, -2 * GB * D:].rearrange("p (u b d) -> p u b d", u=2, b=GB)
            gathered = [r.sem(f"gathered{u}") for u in range(2)]
            names = "rstd xn xn_kept meant turned high low ones first_added second_added".split()
            s = {n: r.sem(n + "_done") for n in names}
            with nc.Block() as block:
                @block.sync
                def _(sp):
                    sp.dma_start(nw[:, :], A["L1_attn_norm_w"].partition_broadcast(P)).then_inc(consts_in, 16)
                    sp.dma_start(mix[:, 0:1], A["L1_attn_omega_mix"].partition_broadcast(P)).then_inc(consts_in, 16)
                    sp.dma_start(mix[:, 1:2], A["L1_attn_vq_mix"].partition_broadcast(P)).then_inc(consts_in, 16)
                    sp.dma_start(Wp[:, :, :, :], A["L1_attn_Wp"]).then_inc(w_in, 16)
                    for t, n in ((bp, "L1_attn_omega_b"), (sign, "sign"), (Wvi, "L1_attn_Wvi"), (Wvo, "L1_attn_Wvo"),
                                 (Woo, "L1_attn_Woo"), (code, "L1_attn_codebook"), (behind, "behind")):
                        sp.dma_start(t[:], A[n]).then_inc(w_in, 16)
                    for t, n in ((bvi, "L1_attn_vq_proj_in_b"), (bvo, "L1_attn_vq_proj_out_b"),
                                 (boo, "L1_attn_omega_out_b")):
                        sp.dma_start(t[:, :], A[n].partition_broadcast(B)).then_inc(w_in, 16)
                    sp.wait_ge(consts_in, 48)
                    ahead.load(sp, "mqa")

                @block.vector
                def _(dve):
                    dve.memset(ones[:, :], 1.0 / S).then_inc(s["ones"], 1)
                    dve.memset(hT[0][LD:LD + 1, :], 1.0).then_inc(s["ones"], 1)
                    dve.memset(hT[1][LD:LD + 1, :], 0.0).then_inc(s["ones"], 1)

                    def norm(g, early):
                        u = g % 2
                        dve.wait_ge(gathered[u], 16 * 2 * GB * (g // 2 + 1))
                        for one, results, added in ((0, XN[:, bass.ds(g * GB, GB), :], "first_added"),
                                                    (1, second[:, u, :, :], "second_added")):
                            if one:
                                dve.wait_ge(s["first_added"], g * GB + GB)
                            for b in range(GB):
                                rows = X[:, g * GB + b, :]
                                dve.scalar_tensor_tensor(rows, results[:, b, :], A["token_parts"][:, one, bass.ds(g * GB + b, 1)],
                                                         rows, ALU.mult, ALU.add).then_inc(s[added], 1)
                        dve.wait_ge(s["second_added"], g * GB + GB)
                        rs.run(dve, X, g)
                        dve.wait_ge(s["rstd"], g + 1)
                        if not early:
                            dve.wait_ge(s["turned"], g - 1)
                            dve.wait_ge(s["xn_kept"], g - 1)
                        for b in range(GB):
                            dve.tensor_scalar(xn[:, u, b, :], X[:, g * GB + b, :], rs.mean[:, b:b + 1], rstd[:, b:b + 1],
                                              ALU.subtract, ALU.mult).then_inc(s["xn"], 1)

                    def low(g):
                        rows = slice(g * GT, (g + 1) * GT)
                        dve.wait_ge(s["high"], g + 1)
                        dve.tensor_tensor(hT[1][0:LD, rows], pT[0:LD, g % 2, :], hT[0][0:LD, rows], ALU.subtract)\
                           .then_inc(s["low"], 1)
                    norm(0, True)
                    for g in range(1, NG):
                        norm(g, g < 2)
                        low(g - 1)
                    low(NG - 1)

                @block.gpsimd
                def _(pool):
                    def gather(g):
                        if g >= 2:
                            pool.wait_ge(s["second_added"], (g - 1) * GB)
                        for b in range(GB):
                            for one, to in ((0, XN[:, g * GB + b, :]), (1, second[:, g % 2, b, :])):
                                pool.indirect_dma_start(
                                    to, None, A["slot_results"][:, :],
                                    bass.IndirectOffsetOnAxis(ap=A["token_slots"][:, one, g * GB + b:g * GB + b + 1], axis=0))\
                                    .then_inc(gathered[g % 2], 16)

                    gather(0)
                    for g in range(NG):
                        if g + 1 < NG:
                            gather(g + 1)
                        pool.wait_ge(rs.ve_done, g + 1)
                        pool.tensor_tensor(rstd[:, :], rs.ve[:, :], power[:, 0:GB], ALU.pow).then_inc(s["rstd"], 1)

                @block.tensor
                def _(pe):
                    pe.wait_ge(s["ones"], 3)

                    def group(g, u, early):
                        pe.wait_ge(s["xn"], g * GB + GB)
                        if not early:
                            pe.wait_ge(s["low"], g - 1)
                        for b in range(GB):
                            for dc in range(DC):
                                pe.matmul(pM[:, dc, bass.ds(g * GB + b, 1)], xn[:, u, b, dc * P:(dc + 1) * P],
                                          ones[:, :], start=True, stop=True)
                        for b in range(GB):
                            last = pe.transpose(pT[0:LD, u, b * S:(b + 1) * S], xn[:, u, b, 0:LD], ident[:, :])
                        last.then_inc(s["turned"], 1)
                    group(0, 0, True)
                    group(1, 1, True)
                    with pe.Fori(2, NG - 1, 2) as g:
                        group(g, 0, False)
                        group(g + 1, 1, False)

                @block.scalar
                def _(act):
                    def group(g, u):
                        act.wait_ge(s["turned"], g + 1)
                        act.activation(hT[0][0:LD, bass.ds(g * GT, GT)], pT[0:LD, u, :], ACT.Copy).then_inc(s["high"], 1)
                        act.activation(XN[:, bass.ds(g * GB, GB), :], xn[:, u, :, :], ACT.Copy).then_inc(s["xn_kept"], 1)
                    with act.Fori(0, NG - 1, 2) as g:
                        group(g, 0)
                        group(g + 1, 1)
                    act.wait_ge(s["turned"], NG)
                    act.activation(hm[:, :, :], pM[:, :, :], ACT.Copy).then_inc(s["meant"], 1)

        with ExitStack() as inner:
            r = Core(nc, inner, sems, "lo_")
            om0, om, m2, GT_ = (flat(Wp[:])[0:LD, n * B * LD:(n + 1) * B * LD].rearrange("p (b j) -> p b j", j=LD)
                                for n in range(4))
            g1, g2 = om0, m2
            shift = r.sb("shift", [B, D])
            shift_part = [r.sb(f"shift{t}", [B, D], f16) for t in range(2)]
            mix_scaled = r.sb("mix_scaled", [LD, 1])
            p1, p2 = r.ps("p1", [P, 2048]), r.ps("p2", [P, 2048])
            shift_in, split_high = r.sem("shift_in"), r.sem("split_high")
            d_, t_, a_ = r.sem("vector_step"), r.sem("tensor_step"), r.sem("pool_step")
            half = r.sb("half", [P, 1])
            sm = {n: r.sb(n, sh) for n, sh in (("vq", [B, LD]), ("vsq", [B, LD]), ("vss", [B, 1]), ("vn0", [B, 1]),
                                              ("vn1", [B, 1]), ("vn2", [B, 1]), ("vnorm", [B, LD]),
                                              ("csq", [CODES, LD]), ("css", [CODES, 1]), ("cn0", [CODES, 1]),
                                              ("cn1", [CODES, 1]), ("cn2", [CODES, 1]), ("cnorm", [CODES, LD]),
                                              ("vT", [LD, B]), ("cT", [LD, CODES]), ("sc", [B, CODES]), ("top", [B, 1]),
                                              ("eq", [B, CODES]), ("val", [B, CODES]), ("best", [B, 1]),
                                              ("hot", [B, CODES]), ("hotT", [CODES, B]), ("dif", [B, LD]),
                                              ("vqo", [B, LD]), ("vqoT", [LD, B]), ("sh1", [B, D]), ("sh2", [B, D]),
                                              ("bo2", [B, D]))}
            with nc.Block() as block:
                @block.sync
                def _(sp):
                    sp.wait_ge(d_, 29)
                    for t in range(2):
                        sp.dma_start(pb[t][LD:LD + 1, :, :], shift_part[t][:, :]).then_inc(shift_in, 16)
                    sp.wait_ge(shift_in, 32)

                @block.tensor
                def _(pe):
                    pe.wait_ge(w_in, 16 * 11)
                    for dc in range(DC):
                        last = pe.matmul(p2[0:B, 0:LD], hm[:, dc, :], Wvi[:, dc, :], start=(dc == 0), stop=(dc == 1))
                    last.then_inc(t_, 1)
                    for j in range(LD):
                        for dc in range(DC):
                            last = pe.matmul(p1[0:LD, j * B:(j + 1) * B], Wp[:, dc, :, j], hm[:, dc, :],
                                             start=(dc == 0), stop=(dc == 1))
                    last.then_inc(t_, 1)
                    pe.wait_ge(d_, 11)
                    pe.transpose(p2[0:LD, 512:512 + B], sm["vnorm"][:, :], ident[0:B, 0:B]).then_inc(t_, 1)
                    pe.transpose(p2[0:LD, 1024:1024 + CODES], sm["cnorm"][:, :], ident[0:CODES, 0:CODES]).then_inc(t_, 1)
                    pe.wait_ge(d_, 13)
                    pe.matmul(p2[0:B, 1536:1536 + CODES], sm["vT"][:, :], sm["cT"][:, :], start=True, stop=True)\
                      .then_inc(t_, 1)
                    pe.wait_ge(d_, 19)
                    pe.transpose(p2[0:CODES, 512:512 + B], sm["hot"][:, :], ident[0:B, 0:B]).then_inc(t_, 1)
                    pe.wait_ge(d_, 20)
                    pe.matmul(p2[0:B, 1024:1024 + LD], sm["hotT"][:, :], code[:, :], start=True, stop=True).then_inc(t_, 1)
                    pe.wait_ge(d_, 22)
                    pe.transpose(p2[0:LD, 512:512 + B], sm["vqo"][:, :], ident[0:B, 0:B]).then_inc(t_, 1)
                    pe.wait_ge(d_, 23)
                    pe.matmul(p2[0:B, 0:D], sm["vqoT"][:, :], Wvo[:, :], start=True, stop=True).then_inc(t_, 1)
                    pe.wait_ge(d_, 31)
                    for b in range(B):
                        last = pe.matmul(p1[0:LD, b * LD:(b + 1) * LD], om[:, b, :], om[:, b, :], start=True, stop=True)
                    last.then_inc(t_, 1)
                    pe.wait_ge(d_, 32)
                    for b in range(B):
                        last = pe.matmul(p2[0:LD, b * LD:(b + 1) * LD], m2[:, b, :], om[:, b, :], start=True, stop=True)
                    last.then_inc(t_, 1)
                    pe.wait_ge(d_, 35)
                    for q in range(B // 8):
                        ps = (p1, p2)[q % 2]
                        if q >= 2:
                            pe.wait_ge(d_, 35 + q - 1)
                        for b in range(8):
                            last = pe.matmul(ps[0:LD, b * D:(b + 1) * D], GT_[:, q * 8 + b, :], Woo[:, :], start=True,
                                             stop=True)
                        last.then_inc(t_, 1)

                @block.gpsimd
                def _(pool):
                    pool.memset(half[:, :], 0.5).then_inc(a_, 1)
                    pool.wait_ge(a_, 1)
                    pool.wait_ge(d_, 5)
                    pool.tensor_tensor(sm["vn0"][:, :], sm["vss"][:, :], half[0:B, :], ALU.pow).then_inc(a_, 1)
                    pool.tensor_tensor(sm["cn0"][:, :], sm["css"][:, :], half[0:CODES, :], ALU.pow).then_inc(a_, 1)

                @block.vector
                def _(dve):
                    n = [0]

                    def step(ins, settle=True):
                        ins.then_inc(d_, 1)
                        n[0] += 1
                        if settle:
                            dve.wait_ge(d_, n[0])

                    def bc(t, m):
                        return t.broadcast_to((t.shape[0], m))
                    v = sm
                    dve.wait_ge(w_in, 16 * 11)
                    dve.wait_ge(t_, 1)
                    step(dve.tensor_tensor(v["vq"][:, :], p2[0:B, 0:LD], bvi[:, :], ALU.add))
                    step(dve.tensor_tensor(v["vsq"][:, :], v["vq"][:, :], v["vq"][:, :], ALU.mult))
                    step(dve.tensor_reduce(v["vss"][:, :], v["vsq"][:, :], AX, ALU.add))
                    step(dve.tensor_tensor(v["csq"][:, :], code[:, :], code[:, :], ALU.mult))
                    step(dve.tensor_reduce(v["css"][:, :], v["csq"][:, :], AX, ALU.add))
                    dve.wait_ge(a_, 3)
                    step(dve.tensor_scalar(v["vn1"][:, :], v["vn0"][:, :], 1e-12, None, ALU.max))
                    step(dve.reciprocal(v["vn2"][:, :], v["vn1"][:, :]))
                    step(dve.tensor_scalar(v["cn1"][:, :], v["cn0"][:, :], 1e-12, None, ALU.max))
                    step(dve.reciprocal(v["cn2"][:, :], v["cn1"][:, :]))
                    step(dve.tensor_scalar(v["vnorm"][:, :], v["vq"][:, :], v["vn2"][:, 0:1], None, ALU.mult))
                    step(dve.tensor_scalar(v["cnorm"][:, :], code[:, :], v["cn2"][:, 0:1], None, ALU.mult))
                    dve.wait_ge(t_, 4)
                    step(dve.tensor_copy(v["vT"][:, :], p2[0:LD, 512:512 + B]))
                    step(dve.tensor_copy(v["cT"][:, :], p2[0:LD, 1024:1024 + CODES]))
                    dve.wait_ge(t_, 5)
                    step(dve.tensor_copy(v["sc"][:, :], p2[0:B, 1536:1536 + CODES]))
                    step(dve.tensor_reduce(v["top"][:, :], v["sc"][:, :], AX, ALU.max))
                    step(dve.tensor_tensor(v["eq"][:, :], v["sc"][:, :], bc(v["top"][:, :], CODES), ALU.is_equal))
                    step(dve.tensor_tensor(v["val"][:, :], v["eq"][:, :], behind[:, :], ALU.mult))
                    step(dve.tensor_reduce(v["best"][:, :], v["val"][:, :], AX, ALU.max))
                    step(dve.tensor_tensor(v["hot"][:, :], v["val"][:, :], bc(v["best"][:, :], CODES), ALU.is_equal))
                    dve.wait_ge(t_, 6)
                    step(dve.tensor_copy(v["hotT"][:, :], p2[0:CODES, 512:512 + B]))
                    dve.wait_ge(t_, 7)
                    step(dve.tensor_tensor(v["dif"][:, :], p2[0:B, 1024:1024 + LD], v["vq"][:, :], ALU.subtract))
                    step(dve.tensor_tensor(v["vqo"][:, :], v["vq"][:, :], v["dif"][:, :], ALU.add))
                    dve.wait_ge(t_, 8)
                    step(dve.tensor_copy(v["vqoT"][:, :], p2[0:LD, 512:512 + B]))
                    dve.wait_ge(t_, 9)
                    step(dve.tensor_tensor(v["sh1"][:, :], p2[0:B, 0:D], bvo[:, :], ALU.add))
                    step(dve.tensor_scalar(v["bo2"][:, :], boo[:, :], mix[0:B, 0:1], None, ALU.mult))
                    step(dve.scalar_tensor_tensor(shift[:, :], v["sh1"][:, :], mix[0:B, 1:2], v["bo2"][:, :],
                                                  ALU.mult, ALU.add))
                    step(dve.tensor_scalar(mix_scaled[:, :], mix[0:LD, 0:1], SCALE, None, ALU.mult))
                    step(dve.tensor_scalar(shift_part[0][:, :], shift[:, :], SCALE, None, ALU.mult))
                    step(dve.scalar_tensor_tensor(shift_part[1][:, :], shift[:, :], SCALE, shift_part[0][:, :],
                                                  ALU.mult, ALU.subtract))
                    step(dve.tensor_tensor(om0[:, :, :].rearrange("p b j -> p j b"),
                                           p1[0:LD, :].rearrange("p (j b) -> p j b", b=B), spread(bp[:, :], B), ALU.add))
                    step(dve.tensor_tensor(om[:, :, :], om0[:, :, :], repeat(sign[:, :], B), ALU.mult))
                    dve.wait_ge(t_, 10)
                    step(dve.tensor_copy(m2[:, :, :].rearrange("p b j -> p (b j)"), p1[0:LD, :]))
                    step(dve.scalar_tensor_tensor(g1[:, :, :], m2[:, :, :], -0.5, om[:, :, :], ALU.mult, ALU.subtract))
                    dve.wait_ge(t_, 11)
                    step(dve.scalar_tensor_tensor(g2[:, :, :].rearrange("p b j -> p (b j)"), p2[0:LD, :], 1.0 / 6.0,
                                                  g1[:, :, :].rearrange("p b j -> p (b j)"), ALU.mult, ALU.add))
                    step(dve.tensor_tensor(GT_[:, :, :], g2[:, :, :], repeat(ident[0:LD, 0:LD], B), ALU.add))
                    for q in range(B // 8):
                        dve.wait_ge(split_high, q + 1)
                        step(dve.scalar_tensor_tensor(pb[1][0:LD, q * 8:(q + 1) * 8, :].rearrange("p b d -> p (b d)"),
                                                      (p1, p2)[q % 2][0:LD, :], mix_scaled[:, 0:1],
                                                      pb[0][0:LD, q * 8:(q + 1) * 8, :].rearrange("p b d -> p (b d)"),
                                                      ALU.mult, ALU.subtract), settle=False)

                @block.scalar
                def _(act):
                    act.wait_ge(d_, 27)
                    for q in range(B // 8):
                        act.wait_ge(t_, 12 + q)
                        act.activation(pb[0][0:LD, q * 8:(q + 1) * 8, :].rearrange("p b d -> p (b d)"),
                                       (p1, p2)[q % 2][0:LD, :], ACT.Copy, scale=mix_scaled[:, 0:1]).then_inc(split_high, 1)

        with ExitStack() as inner:
            r = Core(nc, inner, sems, "ly_")
            pY = [r.ps(f"pY{i}", [P, GB, D]) for i in range(2)]
            y, sq, z = (r.sb(n, [P, 2, GB, D]) for n in ("y", "sq", "z"))
            ss, me, rr = (r.sb(n, [P, 2, GB]) for n in ("ss", "me", "rr"))
            eps, nw16 = r.sb("eps", [P, GB]), r.sb("nw16", [P, D])
            eps_made, nw_made = r.sem("eps_made"), r.sem("nw_made")
            names = "rotated y squared ss me rr z x".split()
            s = {n: r.sem(n + "_done") for n in names}
            with nc.Block() as block:
                def twos(eng, group):
                    group(0, 0, True)
                    group(1, 1, True)
                    with eng.Fori(2, NG - 1, 2) as g:
                        group(g, 0, False)
                        group(g + 1, 1, False)

                @block.tensor
                def _(pe):
                    def group(g, u, early):
                        if not early:
                            pe.wait_ge(s["y"], g - 1)
                        for b in range(GB):
                            for n, (x, w) in enumerate(TERMS):
                                last = pe.matmul(pY[u][:, b, :], hT[x][0:LD + 1, bass.ds((g * GB + b) * S, S)],
                                                 pb[w][0:LD + 1, g * GB + b, :], start=(n == 0), stop=(n == 2))
                        last.then_inc(s["rotated"], 1)
                    twos(pe, group)

                @block.vector
                def _(dve):
                    def take(g, u, early):
                        dve.wait_ge(s["rotated"], g + 1)
                        if not early:
                            dve.wait_ge(s["z"], (g - 1) * GB)
                            dve.wait_ge(s["squared"], (g - 1) * GB)
                        dve.scalar_tensor_tensor(y[:, u, :, :], pY[u][:, :, :], 1.0 / SCALE, XN[:, bass.ds(g * GB, GB), :],
                                                 ALU.mult, ALU.add).then_inc(s["y"], 1)

                    def finish(g, u, early):
                        dve.wait_ge(s["rr"], g + 1)
                        if not early:
                            dve.wait_ge(s["x"], g - 1)
                        for b in range(GB):
                            dve.scalar_tensor_tensor(z[:, u, b, :], y[:, u, b, :], rr[:, u, b:b + 1], nw16[:, :], ALU.mult,
                                                     ALU.mult).then_inc(s["z"], 1)

                    dve.tensor_scalar(nw16[:, :], nw[:, :], float(D) ** 0.5, None, ALU.mult).then_inc(nw_made, 1)
                    dve.wait_ge(nw_made, 1)
                    take(0, 0, True)
                    take(1, 1, True)
                    finish(0, 0, True)
                    take(2, 0, False)
                    finish(1, 1, True)
                    with dve.Fori(2, NG - 2, 2) as g:
                        take(g + 1, 1, False)
                        finish(g, 0, False)
                        take(g + 2, 0, False)
                        finish(g + 1, 1, False)
                    take(NG - 1, 1, False)
                    finish(NG - 2, 0, False)
                    finish(NG - 1, 1, False)

                @block.scalar
                def _(act):
                    def group(g, u, early):
                        act.wait_ge(s["y"], g + 1)
                        if not early:
                            act.wait_ge(s["me"], g - 1)
                        for b in range(GB):
                            act.activation(sq[:, u, b, :], y[:, u, b, :], ACT.Square, accum_out=ss[:, u, b:b + 1])\
                               .then_inc(s["squared"], 1)
                    twos(act, group)

                @block.gpsimd
                def _(pool):
                    pool.memset(eps[:, :], D * 1e-6).then_inc(eps_made, 1)
                    pool.wait_ge(eps_made, 1)

                    def invert(g, u, early):
                        pool.wait_ge(s["squared"], g * GB + GB)
                        pool.tensor_tensor(me[:, u, :], ss[:, u, :], eps[:, :], ALU.add).then_inc(s["me"], 1)
                        pool.wait_ge(s["me"], g + 1)
                        if not early:
                            pool.wait_ge(s["z"], (g - 1) * GB)
                        pool.tensor_tensor(rr[:, u, :], me[:, u, :], power[:, 0:GB], ALU.pow).then_inc(s["rr"], 1)

                    def add(g, u):
                        pool.wait_ge(s["z"], g * GB + GB)
                        rows = X[:, bass.ds(g * GB, GB), :]
                        pool.tensor_tensor(rows, rows, z[:, u, :, :], ALU.add).then_inc(s["x"], 1)
                    invert(0, 0, True)
                    invert(1, 1, True)
                    add(0, 0)
                    with pool.Fori(0, (NG - 2) // 2) as i:
                        invert(2 * i + 2, 0, False)
                        add(2 * i + 1, 1)
                        invert(2 * i + 3, 1, False)
                        add(2 * i + 2, 0)
                    add(NG - 1, 1)


def one_key_attention(nc, sems, X, ident, power, A, ahead):
    SCALE = 256.0
    SL = P // HD
    ATT = 1.0 / float(D) ** 0.5
    UNIT = 4
    UNITS = GB * NH // UNIT
    with ExitStack() as scope:
        c = Core(nc, scope, sems, "q_")
        Wq = [c.sb(f"wq{t}", [P, DC, D], f16) for t in range(2)]
        Wk = [c.sb(f"wk{t}", [P, DC, P], f16) for t in range(2)]
        Wv = [c.sb(f"wv{t}", [P, DC, HD], f16) for t in range(2)]
        split = SplitHeld(c, ahead, "mqa", [Wq, Wk, Wv], SCALE)
        pP = c.ps("pP", [P, 2, 512])
        pO = [c.ps(f"pO{i}", [P, 512]) for i in range(2)]
        pS = [c.ps(f"pS{i}", [P, UNIT, S]) for i in range(2)]
        pT = [c.ps(f"pT{i}", [P, UNIT, S]) for i in range(2)]
        names = ("q_projected k_projected v_projected q qh ql k kh kl km km_pool v vh vl scored mx sub negated exp turned ph pl "
                 "weighed rec out x_done ctx_in ctx_h ctx_l tables_in ones").split()
        s = {n: c.sem(n + "_done") for n in names}
        fr = Front(c, X, ident, power, pP, (s["q_projected"], 1))
        cf = c.sb("ctx", [P, DC, GT])
        ch, cl = (c.sb(n, [P, DC, GT], f16) for n in ("ch", "cl"))
        bq, bk, bv = c.sb("bq", [P, DC]), c.sb("bk", [P, 1]), c.sb("bv", [P, HD])
        slot = c.sb("slot", [P, SL])
        q = c.sb("q", [P, DC, GT])
        k = c.sb("k", [P, GT])
        ks = [c.sb(f"ks{t}", [P, GT], f16) for t in range(2)]
        v = c.sb("v", [P, GB, HD + 1])
        qs = [[c.sb(f"qs{t}{p}", [P, DC, GT], f16) for p in range(2)] for t in range(2)]
        km = [[c.sb(f"km{t}{p}", [P, SL, GT], f16) for p in range(2)] for t in range(2)]
        vs = [[c.sb(f"vs{t}{p}", [P, GB, HD + 1], f16) for p in range(2)] for t in range(2)]
        BY_POOL = 4
        mx = c.sb("mx", [P, 2, UNIT])
        negated = c.sb("negated", [P, UNIT])
        sub = c.sb("sub", [P, UNIT, S])
        ex = [c.sb(f"ex{i}", [P, UNIT, S]) for i in range(2)]
        pr = [[c.sb(f"p{t}{i}", [P, S, NH], f16) for i in range(2)] for t in range(2)]
        rec = c.sb("rec", [P, 2, NH])
        out = c.sb("out", [P, 2, NH, HD])

        def part_of(part, u):
            b, at = u // 4 % 2, UNIT * (u % 4)
            return pr[part][b][:, :, at:at + UNIT].rearrange("k t c -> k c t")

        def exps(g, u):
            return g * (UNITS // 2) * (1 + UNIT) + u // 2 * (1 + UNIT) + (1 + u % 2 * UNIT)

        def loop(eng, main):
            main(0, 0, True, True)
            with eng.Fori(0, (NG - 2) // 2) as i:
                main(2 * i + 1, 1, False, True)
                main(2 * i + 2, 0, False, True)
            main(NG - 1, 1, False, False)

        def lagging(g, u, lag, first):
            if u >= lag:
                return g, u - lag
            return None if first else (g - 1, u - lag + UNITS)

        with nc.Block() as block:
            @block.sync
            def _(sp):
                sp.dma_start(cf[:, :, :], A["ctxT"][:, :, 0:GT]).then_inc(s["ctx_in"], 16)
                for t, n in ((bq, "L1_xattn_bq"), (bk, "L1_xattn_bk"), (slot, "slot")):
                    sp.dma_start(t[:, :], A[n]).then_inc(s["tables_in"], 16)
                sp.dma_start(bv[:, :], A["L1_xattn_bv"].partition_broadcast(P)).then_inc(s["tables_in"], 16)
                sp.wait_ge(split.low_done, split.count)
                ahead.load(sp, "moe_silu")
                with sp.Fori(1, NG) as g:
                    sp.wait_ge(s["ctx_l"], g)
                    sp.dma_start(cf[:, :, :], A["ctxT"][:, :, bass.ds(g * GT, GT)]).then_inc(s["ctx_in"], 16)

            @block.tensor
            def _(pe):
                def score(g, p, u, first):
                    n = g * UNITS + u
                    if u >= 2 or not first:
                        if u % 2 == 0:
                            pe.wait_ge(s["sub"], g * (UNITS // 2) + u // 2)
                        else:
                            pe.wait_ge(s["exp"], exps(g, u - 2))
                    if u == 0:
                        pe.wait_ge(s["ql"], g + 1)
                        pe.wait_ge(s["km"], (g + 1) * (2 * SL - BY_POOL))
                        pe.wait_ge(s["km_pool"], (g + 1) * BY_POOL)
                    b, dc, a = u // 4, u % 4 // 2, u % 2
                    t = slice(b * S, (b + 1) * S)
                    for m, (x, y) in enumerate(TERMS):
                        last = pe.matmul(pS[u % 2][:, :, :], qs[x][p][:, dc, t], km[y][p][:, UNIT * a:UNIT * (a + 1), t],
                                         start=(m == 0), stop=(m == 2))
                    last.then_inc(s["scored"], 1)

                def turn(g, u, early):
                    n = g * UNITS + u
                    pe.wait_ge(s["exp"], exps(g, u))
                    if not early:
                        pe.wait_ge(s["pl"], n - 1)
                    for j in range(UNIT):
                        last = pe.transpose(pT[u % 2][:, j, :], ex[u % 2][:, j, :], ident[:, :])
                    last.then_inc(s["turned"], 1)

                def weigh(g, p, b, early):
                    pe.wait_ge(s["pl"], g * UNITS + 4 * b + 4)
                    if b == 0:
                        pe.wait_ge(s["vl"], g + 1)
                    if not early:
                        pe.wait_ge(s["out"], g * GB + b - 1)
                    for h in range(NH):
                        for m, (x, y) in enumerate(TERMS):
                            still = pr[x][b % 2][:, 8 * h:8 * h + 8, :].rearrange("k t c -> k (t c)")
                            last = pe.matmul(pO[b % 2][:, h * (HD + 1):(h + 1) * (HD + 1)], still, vs[y][p][:, b, :],
                                             start=(m == 0), stop=(m == 2))
                    last.then_inc(s["weighed"], 1)

                def project_q(g):
                    pe.wait_ge(fr.xl_done, g + 1)
                    for a in range(DC):
                        last = project_features(pe, pP[:, a, :], Wq, slice(a * P, (a + 1) * P), (fr.xh, fr.xl))
                    last.then_inc(s["q_projected"], 1)

                def project_kv(g):
                    pe.wait_ge(s["ctx_l"], g + 1)
                    pe.wait_ge(s["q"], 2 * g + 2)
                    project_features(pe, pP[:, 0, :], Wk, slice(0, P), (ch, cl)).then_inc(s["k_projected"], 1)
                    for b in range(GB):
                        last = project_tokens(pe, pP[:, 1, b * HD:(b + 1) * HD], Wv, slice(0, HD), (ch, cl),
                                              slice(b * S, (b + 1) * S))
                    last.then_inc(s["v_projected"], 1)

                def turn_rows(g):
                    pe.wait_ge(s["k"], g)
                    pe.wait_ge(s["v"], g)
                    fr.transpose(pe, g)

                def main(g, p, first, more):
                    for u in range(UNITS):
                        score(g, p, u, first)
                        back = lagging(g, u, 2, first)
                        if back is not None:
                            turn(*back, first and u < 4)
                        if u % 4 == 3 and (u > 3 or not first):
                            b = (u // 4 - 1) % 4
                            weigh(g if u > 3 else g - 1, p if u > 3 else 1 - p, b, first and b < 2)
                        if more and u == 5:
                            turn_rows(g + 1)
                        if more and u == 8:
                            project_q(g + 1)
                        if more and u == 10:
                            project_kv(g + 1)

                fr.transpose(pe, 0)
                pe.wait_ge(split.low_done, split.count)
                project_q(0)
                project_kv(0)
                loop(pe, main)
                turn(NG - 1, UNITS - 2, False)
                turn(NG - 1, UNITS - 1, False)
                weigh(NG - 1, 1, GB - 1, False)

            @block.vector
            def _(dve):
                def maximum(g, u, first):
                    n = g * UNITS + u
                    dve.wait_ge(s["scored"], n + 1)
                    if u >= 2 or not first:
                        dve.wait_ge(s["exp"], exps(g, u - 2))
                    dve.tensor_reduce(mx[:, u % 2, :], pS[u % 2][:, :, :], AX, ALU.max).then_inc(s["mx"], 1)

                def low(g, u):
                    dve.wait_ge(s["ph"], g * UNITS + u + 1)
                    dve.tensor_tensor(part_of(1, u), pT[u % 2][:, :, :], part_of(0, u), ALU.subtract).then_inc(s["pl"], 1)

                def finish(g, b, early):
                    n = g * GB + b
                    o = pO[b % 2][:, 0:NH * (HD + 1)].rearrange("p (h e) -> p h e", e=HD + 1)
                    dve.wait_ge(s["weighed"], n + 1)
                    if not early:
                        dve.wait_ge(s["out"], n - 1)
                    dve.reciprocal(rec[:, b % 2, :], o[:, :, HD]).then_inc(s["rec"], 1)
                    dve.wait_ge(s["rec"], n + 1)
                    if not early:
                        dve.wait_ge(s["x_done"], n - 1)
                    dve.tensor_tensor(out[:, b % 2, :, :], o[:, :, 0:HD], spread(rec[:, b % 2, :], HD), ALU.mult)\
                       .then_inc(s["out"], 1)

                def take_v(g):
                    dve.wait_ge(s["v_projected"], g + 1)
                    if not starts(g, 0):
                        dve.wait_ge(s["vl"], g)
                    dve.scalar_tensor_tensor(v[:, :, 0:HD], pP[:, 1, 0:GB * HD].rearrange("p (b e) -> p b e", e=HD),
                                             1.0 / SCALE, repeat(bv[:, :], GB), ALU.mult, ALU.add).then_inc(s["v"], 1)

                def v_low(g, p):
                    dve.wait_ge(s["vh"], g + 1)
                    dve.tensor_tensor(vs[1][p][:, :, :], v[:, :, :], vs[0][p][:, :, :], ALU.subtract).then_inc(s["vl"], 1)

                def mask_keys(g, p, t, slices):
                    dve.wait_ge(s["kh" if t == 0 else "kl"], g + 1)
                    if t == 0 and not starts(g, 0) and not starts(g, 1):
                        dve.wait_ge(s["scored"], (g - 1) * UNITS)
                    for j in slices:
                        dve.tensor_scalar(km[t][p][:, j, :], ks[t][:, :], slot[:, j:j + 1], None, ALU.mult)\
                           .then_inc(s["km"], 1)

                def main(g, p, first, more):
                    for u in range(UNITS):
                        maximum(g, u, first)
                        back = lagging(g, u, 3, first)
                        if back is not None:
                            low(*back)
                        dve.wait_ge(s["mx"], g * UNITS + u + 1)
                        if u % 2 == 0:
                            dve.tensor_tensor(sub[:, :, :], pS[0][:, :, :], spread(mx[:, 0, :], S), ALU.subtract)\
                               .then_inc(s["sub"], 1)
                        else:
                            dve.tensor_scalar(negated[:, :], mx[:, 1, :], -ATT, None, ALU.mult).then_inc(s["negated"], 1)
                        if u % 4 == 0 and (u > 4 or not first):
                            b = (u // 4 - 2) % 4
                            finish(g if u > 4 else g - 1, b, first and b < 2)
                        if more and u == 1:
                            fr.stats(dve, g + 1)
                        if more and u == 3:
                            fr.norm(dve, g + 1)
                        if more and u == 7:
                            fr.low(dve, g + 1)
                        if more and u == 11:
                            take_v(g + 1)
                        if more and u == 13:
                            mask_keys(g + 1, 1 - p, 0, range(BY_POOL, SL))
                            v_low(g + 1, 1 - p)
                        if more and u == 14:
                            mask_keys(g + 1, 1 - p, 1, range(0, SL // 2))
                        if more and u == 15:
                            mask_keys(g + 1, 1 - p, 1, range(SL // 2, SL))

                dve.memset(v[:, :, HD:HD + 1], 1.0).then_inc(s["ones"], 1)
                dve.wait_ge(s["ones"], 1)
                dve.wait_ge(s["tables_in"], 16 * 4)
                fr.stats(dve, 0)
                fr.norm(dve, 0, first=True)
                split.low(dve)
                fr.low(dve, 0)
                take_v(0)
                mask_keys(0, 0, 0, range(BY_POOL, SL))
                mask_keys(0, 0, 1, range(SL))
                v_low(0, 0)
                loop(dve, main)
                for u in range(UNITS - 3, UNITS):
                    low(NG - 1, u)
                finish(NG - 1, GB - 2, False)
                finish(NG - 1, GB - 1, False)

            @block.scalar
            def _(act):
                def context_high(g):
                    act.wait_ge(s["ctx_in"], g * 16 + 16)
                    if not starts(g, 0):
                        act.wait_ge(s["v_projected"], g)
                    act.activation(ch[:, :, :], cf[:, :, :], ACT.Copy).then_inc(s["ctx_h"], 1)

                def exp(g, u, first):
                    n = g * UNITS + u
                    if u >= 2 or not first:
                        act.wait_ge(s["turned"], n - 1)
                    if u % 2 == 0:
                        act.wait_ge(s["sub"], g * (UNITS // 2) + u // 2 + 1)
                        act.activation(ex[0][:, :, :], sub[:, :, :], ACT.Exp, scale=ATT).then_inc(s["exp"], 1)
                    else:
                        act.wait_ge(s["negated"], g * (UNITS // 2) + u // 2 + 1)
                        for j in range(UNIT):
                            act.activation(ex[1][:, j, :], pS[1][:, j, :], ACT.Exp, scale=ATT, bias=negated[:, j:j + 1])\
                               .then_inc(s["exp"], 1)

                def high(g, u, early):
                    act.wait_ge(s["turned"], g * UNITS + u + 1)
                    if not early:
                        act.wait_ge(s["weighed"], g * GB + u // 4 - 1)
                    act.activation(part_of(0, u), pT[u % 2][:, :, :], ACT.Copy).then_inc(s["ph"], 1)

                def take_q(g, p):
                    act.wait_ge(s["q_projected"], g + 1)
                    if not starts(g, 0):
                        act.wait_ge(s["ql"], g)
                    for a in range(DC):
                        act.activation(q[:, a, :], pP[:, a, :], ACT.Identity, scale=1.0 / SCALE, bias=bq[:, a:a + 1])\
                           .then_inc(s["q"], 1)
                    if not starts(g, 0) and not starts(g, 1):
                        act.wait_ge(s["scored"], (g - 1) * UNITS)
                    act.wait_ge(s["q"], 2 * g + 2)
                    act.activation(qs[0][p][:, :, :], q[:, :, :], ACT.Copy).then_inc(s["qh"], 1)

                def take_k(g):
                    act.wait_ge(s["k_projected"], g + 1)
                    if not starts(g, 0):
                        act.wait_ge(s["km"], g * (2 * SL - BY_POOL))
                        act.wait_ge(s["km_pool"], g * BY_POOL)
                    act.activation(k[:, :], pP[:, 0, :], ACT.Identity, scale=1.0 / SCALE, bias=bk[:, 0:1])\
                       .then_inc(s["k"], 1)
                    act.wait_ge(s["k"], g + 1)
                    act.activation(ks[0][:, :], k[:, :], ACT.Copy).then_inc(s["kh"], 1)

                def v_high(g, p):
                    act.wait_ge(s["v"], g + 1)
                    if not starts(g, 0) and not starts(g, 1):
                        act.wait_ge(s["weighed"], (g - 1) * GB)
                    act.activation(vs[0][p][:, :, :], v[:, :, :], ACT.Copy).then_inc(s["vh"], 1)

                def main(g, p, first, more):
                    for u in range(UNITS):
                        back = lagging(g, u, 2, first)
                        if back is not None:
                            high(*back, first and u < 10)
                        exp(g, u, first)
                        if more and u == 1:
                            context_high(g + 1)
                        if more and u == 6:
                            fr.high(act, g + 1)
                        if more and u == 9:
                            take_q(g + 1, 1 - p)
                        if more and u == 11:
                            take_k(g + 1)
                        if more and u == 12:
                            v_high(g + 1, 1 - p)

                nc.scalar.preload_act_table(ACT.Exp)
                split.high(act)
                act.wait_ge(s["tables_in"], 16 * 4)
                context_high(0)
                fr.high(act, 0, first=True)
                take_q(0, 0)
                take_k(0)
                v_high(0, 0)
                loop(act, main)
                high(NG - 1, UNITS - 2, False)
                high(NG - 1, UNITS - 1, False)

            @block.gpsimd
            def _(pool):
                def low_part(done, high, g, out, value, high_part):
                    pool.wait_ge(s[high], g + 1)
                    pool.tensor_tensor(out, value, high_part, ALU.subtract).then_inc(s[done], 1)

                def context_low(g):
                    low_part("ctx_l", "ctx_h", g, cl[:, :, :], cf[:, :, :], ch[:, :, :])

                def q_low(g, p):
                    low_part("ql", "qh", g, qs[1][p][:, :, :], q[:, :, :], qs[0][p][:, :, :])

                def k_low(g):
                    low_part("kl", "kh", g, ks[1][:, :], k[:, :], ks[0][:, :])

                def mask_keys(g, p):
                    if not starts(g, 0) and not starts(g, 1):
                        pool.wait_ge(s["scored"], (g - 1) * UNITS)
                    for j in range(BY_POOL):
                        pool.tensor_tensor(km[0][p][:, j, :], ks[0][:, :], slot[:, j:j + 1].broadcast_to((P, GT)), ALU.mult)\
                            .then_inc(s["km_pool"], 1)

                def add(g, b):
                    pool.wait_ge(s["out"], g * GB + b + 1)
                    rows = X[:, g * GB + b, :]
                    pool.tensor_tensor(rows, rows, out[:, b % 2, :, :].rearrange("p h e -> p (h e)"), ALU.add)\
                        .then_inc(s["x_done"], 1)

                def main(g, p, first, more):
                    for u in range(UNITS):
                        if u % 4 == 1 and (u > 5 or not first):
                            add(g if u > 5 else g - 1, (u // 4 - 2) % 4)
                        if more and u == 1:
                            fr.power_of_var(pool, g + 1)
                        if more and u == 3:
                            context_low(g + 1)
                        if more and u == 10:
                            q_low(g + 1, 1 - p)
                        if more and u == 12:
                            k_low(g + 1)
                            mask_keys(g + 1, 1 - p)

                fr.power_of_var(pool, 0)
                context_low(0)
                q_low(0, 0)
                k_low(0)
                mask_keys(0, 0)
                loop(pool, main)
                add(NG - 1, GB - 2)
                add(NG - 1, GB - 1)


def moe_silu(nc, sems, X, ident, power, A, ahead):
    SCALE = 256.0
    N = E + 1
    RING = 3
    with ExitStack() as scope:
        c = Core(nc, scope, sems, "s_")
        XH, XL = c.sb("XH", [P, DC, B * S], f16), c.sb("XL", [P, DC, B * S], f16)
        cfT = c.sb("cfT", [P, B * S], f16)
        ident16 = c.sb("ident16", [P, P], f16)
        lower = c.sb("lower", [P, E * E])
        select = c.sb("select", [P, E, P], f16)
        constants(nc, sems, ident, ident16, lower, select, cfT, "const2_")
        W1 = [c.sb(f"w1{t}", [P, N, DC, P], f16) for t in range(2)]
        W2 = [c.sb(f"w2{t}", [P, N, D], f16) for t in range(2)]
        Wg = [c.sb(f"wg{t}", [P, DC, E], f16) for t in range(2)]
        b2 = [c.sb(f"b2{t}", [P, D], f16) for t in range(2)]
        b1 = c.sb("b1", [P, N])
        eb = c.sb("eb", [P, E])
        bias_in = c.sem("bias_in")

        split = SplitHeld(c, ahead, "moe_silu", [Wg, W1, W2, b2], SCALE)
        with ExitStack() as inner:
            r = Core(nc, inner, sems, "sr_")
            route = Router(r, X, ident, power, XH, XL, Wg, split)
            shares = Shares(r, cfT, ident16)
            lg, ab, ex, u, um, ln, lnt, quo, l1p, pos, sp, act_ = (
                r.sb(n, [P, B, E]) for n in ("lg", "ab", "ex", "u", "um", "ln", "lnt", "quo", "l1p", "pos", "sp", "act"))
            share = r.sb("share", [P, B, E])
            s, a_done = r.sem("routing"), r.sem("scalar_step")
            with nc.Block() as block:
                route.engines(block)

                @block.sync
                def _(sp_):
                    sp_.dma_start(eb[:, :], A["L1_ffn_expert_bias"].partition_broadcast(P)).then_inc(bias_in, 16)
                    sp_.dma_start(b1[:, :], A["L1_ffn_b1"]).then_inc(bias_in, 16)
            with nc.Block() as block:
                @block.vector
                def _(dve):
                    wait = own_steps(dve, s)
                    TINY = 1e-30
                    dve.wait_ge(bias_in, 32)
                    dve.scalar_tensor_tensor(lg[:, :, :], route.logits[:, :, :], 1.0 / SCALE, repeat(eb[:, :], B),
                                             ALU.mult, ALU.add).then_inc(s, 1)
                    wait(1)
                    dve.scalar_tensor_tensor(ab[:, :, :], lg[:, :, :], -1.0, lg[:, :, :], ALU.mult, ALU.max)\
                       .then_inc(s, 1)
                    wait(1)
                    dve.wait_ge(a_done, 1)
                    dve.tensor_scalar(u[:, :, :], ex[:, :, :], 1.0, None, ALU.add).then_inc(s, 1)
                    wait(1)
                    dve.tensor_scalar(um[:, :, :], u[:, :, :], -1.0, TINY, ALU.add, ALU.add).then_inc(s, 1)
                    dve.wait_ge(a_done, 2)
                    dve.tensor_scalar(lnt[:, :, :], ln[:, :, :], TINY, None, ALU.add).then_inc(s, 1)
                    wait(2)
                    dve.reciprocal(quo[:, :, :], um[:, :, :]).then_inc(s, 1)
                    wait(1)
                    dve.tensor_tensor(l1p[:, :, :], lnt[:, :, :], quo[:, :, :], ALU.mult).then_inc(s, 1)
                    wait(1)
                    dve.tensor_tensor(l1p[:, :, :], l1p[:, :, :], ex[:, :, :], ALU.mult).then_inc(s, 1)
                    dve.tensor_scalar(pos[:, :, :], lg[:, :, :], 0.0, None, ALU.max).then_inc(s, 1)
                    wait(2)
                    dve.tensor_tensor(sp[:, :, :], l1p[:, :, :], pos[:, :, :], ALU.add).then_inc(s, 1)
                    wait(1)
                    dve.wait_ge(a_done, 3)
                    chosen, _ = choose_two(r, dve, act_, lower, s, wait)
                    dve.tensor_tensor(share[:, :, :], act_[:, :, :], chosen[:, :, :], ALU.mult).then_inc(s, 1)
                    wait(1)
                    shares.cut(dve, share, s, wait)
                    shares.keep(dve)

                @block.scalar
                def _(act):
                    act.wait_ge(s, 2)
                    act.activation(ex[:, :, :], ab[:, :, :], ACT.Exp, scale=-1.0).then_inc(a_done, 1)
                    act.wait_ge(s, 3)
                    act.activation(ln[:, :, :], u[:, :, :], ACT.Ln).then_inc(a_done, 1)
                    act.wait_ge(s, 10)
                    act.activation(act_[:, :, :], sp[:, :, :], ACT.Sqrt).then_inc(a_done, 1)

                @block.tensor
                def _(pe):
                    shares.turn(pe)
        pU = [c.ps(f"pU{i}", [P, GT]) for i in range(RING)]
        pC = [c.ps(f"pC{i}", [P, GT]) for i in range(RING)]
        pY = c.ps("pY", [P, GB, D])
        h, hc = ([c.sb(f"{n}{i}", [P, GT]) for i in range(RING)] for n in ("h", "hc"))
        hh, hl = ([c.sb(f"{n}{i}", [P, GT], f16) for i in range(RING)] for n in ("hh", "hl"))
        u_done, spread_done, h_done, hc_done, hh_done, hl_done, down_done, y_added = (
            c.sem(n) for n in "u_done spread_done h_done hc_done hh_done hl_done down_done y_added".split())

        def run(eng, group, tail):
            group(0, True)
            with eng.Fori(1, NG) as g:
                group(g, False)
            tail()

        with nc.Block() as block:
            @block.tensor
            def _(pe):
                def down(g, j):
                    pe.wait_ge(hl_done, g * N + j + 1)
                    if j == 0:
                        if not starts(g, 0):
                            pe.wait_ge(y_added, g)
                    for b in range(GB):
                        if j == 0:
                            for n in range(2):
                                pe.matmul(pY[:, b, :], cfT[:, bass.ds((g * GB + b) * S, S)], b2[n][:, :],
                                          start=(n == 0 and b % 2 == 0), stop=False, skip_group_check=True)
                        for x, y in TERMS:
                            last = pe.matmul(pY[:, b, :], (hh, hl)[x][j % RING][:, b * S:(b + 1) * S], W2[y][:, j, :],
                                             start=False, stop=False, skip_group_check=True)
                    last.then_inc(down_done, 1)

                def group(g, first):
                    for j in range(N):
                        if j >= RING or not first:
                            pe.wait_ge(h_done, g * N + j - RING + 1)
                            pe.wait_ge(hc_done, g * N + j - RING + 1)
                        steps = [(dc, x, y) for dc in range(DC) for x, y in TERMS]
                        for n, (dc, x, y) in enumerate(steps):
                            last = pe.matmul(pU[j % RING][:, :], W1[x][:, j, dc, :], (XH, XL)[y][:, dc, bass.ds(g * GT, GT)],
                                             start=(n == 0), stop=(n == len(steps) - 1))
                        last.then_inc(u_done, 1)
                        if j > 0:
                            pe.matmul(pC[j % RING][:, :], select[:, j - 1, :], cfT[:, bass.ds(g * GT, GT)], start=True,
                                      stop=True).then_inc(spread_done, 1)
                        if j >= 2:
                            down(g, j - 2)
                        elif not first:
                            down(g - 1, N + j - 2)

                def tail():
                    down(NG - 1, N - 2)
                    down(NG - 1, N - 1)
                run(pe, group, tail)

            @block.scalar
            def _(act):
                def high(g, j):
                    k = g * N + j
                    act.wait_ge(hc_done, k + 1)
                    if not (starts(g, 0) and j < RING):
                        act.wait_ge(down_done, k - RING + 1)
                    act.activation(hh[j % RING][:, :], hc[j % RING][:, :], ACT.Copy).then_inc(hh_done, 1)

                def group(g, first):
                    for j in range(N):
                        act.wait_ge(u_done, g * N + j + 1)
                        if j >= RING or not first:
                            act.wait_ge(hc_done, g * N + j - RING + 1)
                        act.activation(h[j % RING][:, :], pU[j % RING][:, :], ACT.Silu, bias=b1[:, j:j + 1],
                                       scale=1.0 / SCALE).then_inc(h_done, 1)
                        if j > 0:
                            high(g, j - 1)
                        elif not first:
                            high(g - 1, N - 1)
                nc.scalar.preload_act_table(ACT.Silu)
                run(act, group, lambda: high(NG - 1, N - 1))

            @block.vector
            def _(dve):
                def low(g, j):
                    k = g * N + j
                    dve.wait_ge(hh_done, k + 1)
                    dve.tensor_tensor(hl[j % RING][:, :], hc[j % RING][:, :], hh[j % RING][:, :], ALU.subtract)\
                       .then_inc(hl_done, 1)

                def take(g):
                    dve.wait_ge(down_done, g * N + N)
                    dve.scalar_tensor_tensor(X[:, bass.ds(g * GB, GB), :], pY[:, :, :], 1.0 / SCALE,
                                             X[:, bass.ds(g * GB, GB), :], ALU.mult, ALU.add).then_inc(y_added, 1)

                def group(g, first):
                    for j in range(N):
                        dve.wait_ge(h_done, g * N + j + 1)
                        if j >= RING or not first:
                            dve.wait_ge(hl_done, g * N + j - RING + 1)
                        if j == 0:
                            dve.tensor_copy(hc[0][:, :], h[0][:, :]).then_inc(hc_done, 1)
                        else:
                            dve.wait_ge(spread_done, g * (N - 1) + j)
                            dve.tensor_tensor(hc[j % RING][:, :], h[j % RING][:, :], pC[j % RING][:, :], ALU.mult)\
                               .then_inc(hc_done, 1)
                        if j > 0:
                            low(g, j - 1)
                        elif not first:
                            low(g - 1, N - 1)
                        if j == 1 and not first:
                            take(g - 1)

                def tail():
                    low(NG - 1, N - 1)
                    take(NG - 1)
                run(dve, group, tail)


def load_input(nc, sems, X, ident, power, zeros, A, ahead, first):
    with ExitStack() as scope:
        c = Core(nc, scope, sems, "in_")
        x_in, zeroed, made = c.sem("x_in"), c.sem("zeroed"), c.sem("made")
        with nc.Block() as block:
            @block.sync
            def _(sp):
                for h in range(4):
                    sp.dma_start(X[:, h * 8:(h + 1) * 8, :], A["x"][h * 8:(h + 1) * 8].rearrange("b s d -> s b d"))\
                      .then_inc(x_in, 16)
                ahead.load(sp, first)
                sp.wait_ge(x_in, 64)

            @block.gpsimd
            def _(pool):
                pool.memset(zeros[:, :], 0.0).then_inc(made, 1)
                pool.memset(power[:, :], -0.5).then_inc(made, 1)
                pool.memset(ident[:, :], 0.0).then_inc(zeroed, 1)
                pool.wait_ge(zeroed, 1)
                pool.affine_select(out=ident[:, :], in_=ident[:, :], compare_op=ALU.not_equal, fill=1.0, base=0,
                                   pattern=[[-1, P]], channel_multiplier=1).then_inc(made, 1)


def store_output(nc, sems, X, out):
    with ExitStack() as scope:
        c = Core(nc, scope, sems, "out_")
        stored = c.sem("stored")
        with nc.Block() as block:
            @block.sync
            def _(sp):
                for h in range(4):
                    sp.dma_start(out[h * 8:(h + 1) * 8].rearrange("b s d -> s b d"), X[:, h * 8:(h + 1) * 8, :])\
                      .then_inc(stored, 16)
                sp.wait_ge(stored, 64)


STAGES = ["softmax_attention", "retention", "moe_swiglu", "lie", "mqa", "moe_silu"]


def decoder(nc, A, out, stages):
    with ExitStack() as whole:
        c = Core(nc, whole, [], "")
        X = c.sb("X", [P, B, D])
        ident = c.sb("ident", [P, P])
        power = c.sb("power", [P, 64])
        work = {"softmax_attention": softmax_attention, "retention": retention, "moe_swiglu": moe_swiglu,
                "lie": lie_rotation, "mqa": one_key_attention, "moe_silu": moe_silu}
        sems = []
        zeros = c.sb("zeros", [P, D])
        slot = c.sb("slot", [P, 2, B], u32)
        part = c.sb("part", [P, 2, B])
        A = dict(A, token_slots=slot, token_parts=part, zeros=zeros[:, :], rows_zeroed=c.sem("rows_zeroed"))
        for n in ("slot_rows", "slot_results"):
            A[n] = nc.dram_tensor(n, (TILES * TILE, D), f32, kind="Internal").ap()
        ahead = Ahead(c, A, stages)
        load_input(nc, sems, X, ident, power, zeros, A, ahead, stages[0])
        for name in stages:
            work[name](nc, sems, X, ident, power, A, ahead)
            give_back(nc, sems)
            sems = []
        store_output(nc, sems, X, out)


def layout(inputs):
    import numpy as np

    def rows(w):
        return np.ascontiguousarray(w.reshape(w.shape[0] // P, P, -1).transpose(1, 0, 2))

    def columns(v):
        return np.ascontiguousarray(v.reshape(-1, P).T)

    a = {n: np.asarray(v) for n, v in inputs.items()}
    d = {"x": a["x"]}
    for n in "qkv":
        d[f"L0_attn_W{n}"] = rows(a[f"L0_attn_W{n}"].T)
        d[f"L0_attn_b{n}"] = a[f"L0_attn_b{n}"]
        if n != "q":
            d[f"L0_attn_b{n}"] = columns(a[f"L0_attn_b{n}"])
    d["L0_ffn_Wg"] = rows(a["L0_ffn_Wg"])
    for n in ("W1", "W2", "W3"):
        w = a[f"L0_ffn_{n}"]
        d[f"L0_ffn_{n}"] = np.ascontiguousarray(w.reshape(E, w.shape[1] // P, P, -1).transpose(2, 0, 1, 3))
    d["tile_start"] = (np.arange(TILES) * TILE).astype(np.float32)
    d["ctxT"] = rows(a["ctx_1024"].reshape(B * S, D).T)
    swap = np.arange(D) ^ 1
    for n in "QKV":
        w = a[f"L0_xattn_W_{n}"].transpose(1, 0, 2).reshape(D, D)
        d[f"L0_xattn_W{n}"] = rows(w)
        if n != "V":
            d[f"L0_xattn_W{n}s"] = rows(w[:, swap])
    d["L0_xattn_Wg"], d["L0_xattn_Wo"] = rows(a["L0_xattn_g_w"].T), rows(a["L0_xattn_out_w"].T)
    d["L0_xattn_g_b"], d["L0_xattn_out_b"] = a["L0_xattn_g_b"], a["L0_xattn_out_b"]
    d.update(shape_tables())
    at = np.zeros((LD, LD), np.int64)
    at[np.triu_indices(LD, k=1)] = np.arange(LD * (LD - 1) // 2)
    at = at + at.T
    pair = ~np.eye(LD, dtype=bool)
    w = np.zeros((D, LD, LD), np.float32)
    w[:, pair] = a["L1_attn_omega_proj_w"].T[:, at[pair]]
    d["L1_attn_Wp"] = np.ascontiguousarray(w.reshape(DC, P, LD, LD).transpose(1, 0, 2, 3))
    bias = np.zeros((LD, LD), np.float32)
    bias[pair] = a["L1_attn_omega_proj_b"][at[pair]]
    d["L1_attn_omega_b"] = bias
    d["sign"] = (np.triu(np.ones((LD, LD)), 1) - np.tril(np.ones((LD, LD)), -1)).astype(np.float32)
    d["behind"] = np.ascontiguousarray(np.broadcast_to(CODES - np.arange(CODES, dtype=np.float32), (B, CODES)))
    d["L1_attn_Wvi"] = rows(a["L1_attn_vq_proj_in_w"].T)
    d["L1_attn_Wvo"] = np.ascontiguousarray(a["L1_attn_vq_proj_out_w"].T)
    d["L1_attn_Woo"] = np.ascontiguousarray(a["L1_attn_omega_out_w"].T)
    for n in ("omega_out_b", "vq_proj_in_b", "vq_proj_out_b", "codebook", "norm_w"):
        d[f"L1_attn_{n}"] = a[f"L1_attn_{n}"]
    for n in ("omega_mix", "vq_mix"):
        d[f"L1_attn_{n}"] = a[f"L1_attn_{n}"].reshape(1)
    d["L1_xattn_Wq"], d["L1_xattn_bq"] = rows(a["L1_xattn_Wq"]), columns(a["L1_xattn_bq"])
    d["L1_xattn_Wk"] = rows(np.tile(a["L1_xattn_Wk"], (1, P // HD)))
    d["L1_xattn_bk"] = np.tile(a["L1_xattn_bk"], P // HD)[:, None]
    d["L1_xattn_Wv"], d["L1_xattn_bv"] = rows(a["L1_xattn_Wv"]), a["L1_xattn_bv"]
    d["L1_ffn_Wg"], d["L1_ffn_expert_bias"] = rows(a["L1_ffn_routing_W"].T), a["L1_ffn_expert_bias"]
    w = np.concatenate([a["L1_ffn_sW1"][None], a["L1_ffn_rW1"]])
    d["L1_ffn_W1"] = np.ascontiguousarray(w.reshape(E + 1, DC, P, P).transpose(2, 0, 1, 3))
    w = np.concatenate([a["L1_ffn_sW2"][None], a["L1_ffn_rW2"]])
    d["L1_ffn_W2"] = np.ascontiguousarray(w.transpose(1, 0, 2))
    d["L1_ffn_b1"] = np.ascontiguousarray(np.concatenate([a["L1_ffn_sb1"][None], a["L1_ffn_rb1"]]).T)
    w = np.zeros((P, D), np.float32)
    w[0:3 * E], w[ONES] = np.tile(a["L1_ffn_rb2"], (3, 1)), a["L1_ffn_sb2"]
    d["L1_ffn_b2"] = w
    return d


def kernel(**inputs):
    import concourse.bacc as bacc
    from concourse.bass_utils import run_bass_kernel_spmd
    arrays = layout(inputs)
    nc = bacc.Bacc("TRN2", target_bir_lowering=False, num_devices=1)
    A = {n: nc.dram_tensor(f"in_{n}", v.shape, mybir.dt.from_np(v.dtype), kind="ExternalInput").ap()
         for n, v in arrays.items()}
    out = nc.dram_tensor("out", (B, S, D), f32, kind="ExternalOutput").ap()
    decoder(nc, A, out, STAGES)
    r = run_bass_kernel_spmd(nc, [{f"in_{n}": v for n, v in arrays.items()}], core_ids=[0])
    return r.results[0]["out"]
```
